# Optimizing a Trainium2 kernel written in Bass

```python
import numpy as np
import jax
import jax.numpy as jnp

def _softmax(x, axis=-1):
    return jax.nn.softmax(x, axis=axis)

def _gelu(x):
    return jax.nn.gelu(x, approximate=True)

def _silu(x):
    return jax.nn.silu(x)

def _sigmoid(x):
    return jax.nn.sigmoid(x)

def _layernorm(x, axis=-1, eps=1e-05):
    m = jnp.mean(x, axis=axis, keepdims=True)
    v = jnp.var(x, axis=axis, keepdims=True)
    return (x - m) / jnp.sqrt(v + eps)

def _scatter_add(tgt, idx, src, axis=0):
    return tgt.at[idx].add(src)

def _segment_sum(src, seg, n):
    return jax.ops.segment_sum(src, seg, n)
kernel_name = 'mk_perceiver_d2_seqx_r4_91a6d5'

def setup_inputs(seed: int=0):
    np.random.seed(seed)
    _w = jnp.asarray

    def _rec_inputs():
        import jax
        import jax.numpy as jnp
        _rk = jax.random.key(seed)
        x = -0.0003929 + 0.9999 * jax.random.normal(jax.random.fold_in(_rk, 1), (32, 64, 256), jnp.float32)
        _lenS = 64 - jax.random.randint(jax.random.fold_in(_rk, 7), (32,), 0, max(1, 64 // 4) + 1, jnp.int32)
        _lenS2 = 1601 - jax.random.randint(jax.random.fold_in(_rk, 8), (32,), 0, max(1, 1601 // 4) + 1, jnp.int32)
        _ctx_1024P = jax.random.normal(jax.random.fold_in(_rk, 11), (32, 16, 256), jnp.float32)
        _ctx_1024c = jax.random.dirichlet(jax.random.fold_in(_rk, 511), 0.3 * jnp.ones((16,), jnp.float32), (32, 1601))
        _ctx_1024t = jnp.einsum('bsk,bkd->bsd', _ctx_1024c, _ctx_1024P)
        _ctx_1024t = _ctx_1024t * jax.lax.rsqrt(jnp.mean(jnp.square(_ctx_1024t)) + 1e-12) * 0.953939
        ctx_1024 = 2.81802e-05 + 1.00001 * (_ctx_1024t + 0.3 * jax.random.normal(jax.random.fold_in(_rk, 611), (32, 1601, 256), jnp.float32))
        return (x, ctx_1024)
    x, ctx_1024 = _rec_inputs()

    def _L0_xattn_setup():
        import jax, jax.numpy as jnp
        import numpy as np
        D1, D2, D3 = (256, 256, 256)
        key = jax.random.key(seed)
        k1, k2, kw, kb = jax.random.split(key, 4)
        x1 = jax.random.normal(k1, (8, 512, D1), dtype=jnp.float32)
        x2 = jax.random.normal(k2, (8, 512, D2), dtype=jnp.float32)
        bound = 1.0 / np.sqrt(D1 + D2)
        W = jax.random.uniform(kw, (D3, D1 + D2), minval=-bound, maxval=bound, dtype=jnp.float32)
        b = jax.random.uniform(kb, (D3,), minval=-bound, maxval=bound, dtype=jnp.float32)
        return {'x1': x1, 'x2': x2, 'W': W, 'b': b}
    _L0_xattn_all = _L0_xattn_setup()
    _L0_xattn_in = {k: v for k, v in _L0_xattn_all.items() if k in ('W', 'b')}
    del _L0_xattn_all

    def _L0_attn_setup():
        import jax, jax.numpy as jnp
        import numpy as np
        import math
        B, S, HID, H = (2, 512, 256, 16)
        D = HID // H

        def _get_slopes(n):
            start = 2 ** (-2 ** (-(math.log2(n) - 3)))
            return np.array([start * 2 ** (-i) for i in range(n)], dtype=np.float32)
        key = jax.random.key(seed)
        ks = jax.random.split(key, 9)
        sc = 1.0 / math.sqrt(HID)
        return {'x': jax.random.normal(ks[0], (B, S, HID), dtype=jnp.float32), 'Wq': jax.random.normal(ks[1], (HID, HID), dtype=jnp.float32) * sc, 'bq': jnp.zeros((HID,), dtype=jnp.float32), 'Wk': jax.random.normal(ks[2], (HID, HID), dtype=jnp.float32) * sc, 'bk': jnp.zeros((HID,), dtype=jnp.float32), 'Wv': jax.random.normal(ks[3], (HID, HID), dtype=jnp.float32) * sc, 'bv': jnp.zeros((HID,), dtype=jnp.float32), 'Wo': jax.random.normal(ks[4], (HID, HID), dtype=jnp.float32) * sc, 'bo': jnp.zeros((HID,), dtype=jnp.float32), 'slopes': jnp.asarray(_get_slopes(H))}
    _L0_attn_all = _L0_attn_setup()
    _L0_attn_in = {k: v for k, v in _L0_attn_all.items() if k in ('Wq', 'bq', 'Wk', 'bk', 'Wv', 'bv', 'Wo', 'bo', 'slopes')}
    del _L0_attn_all

    def _L0_ffn_setup():
        import jax, jax.numpy as jnp
        import numpy as np
        E = 8
        G = 4
        LG = 2
        TOPK = 2
        ROUTE_SCALE = 1.0

        def _grouped_mm(x, w, counts):
            counts = counts.astype(jnp.int32)
            if hasattr(jax.lax, 'ragged_dot'):
                return jax.lax.ragged_dot(x, w, counts)
            offs = jnp.cumsum(counts)
            eid = jnp.searchsorted(offs, jnp.arange(x.shape[0]), side='right')
            oh = jax.nn.one_hot(eid, w.shape[0], dtype=x.dtype)
            return jnp.einsum('nd,ne,edh->nh', x, oh, w)
        key = jax.random.key(seed)
        ks = jax.random.split(key, 8)
        bs, slen, dim, hid, shid = (2, 512, 256, 128, 256)
        std = 0.02
        return {'x': jax.random.normal(ks[0], (bs, slen, dim), jnp.float32), 'w_gate': jax.random.normal(ks[1], (E, dim), jnp.float32) * std, 'w1': jax.random.normal(ks[2], (E, dim, hid), jnp.float32) * std, 'w2': jax.random.normal(ks[3], (E, hid, dim), jnp.float32) * std, 'w3': jax.random.normal(ks[4], (E, dim, hid), jnp.float32) * std, 'sw1': jax.random.normal(ks[5], (shid, dim), jnp.float32) * std, 'sw2': jax.random.normal(ks[6], (dim, shid), jnp.float32) * std, 'sw3': jax.random.normal(ks[7], (shid, dim), jnp.float32) * std, 'expert_bias': jnp.zeros((E,), jnp.float32)}
    _L0_ffn_all = _L0_ffn_setup()
    _L0_ffn_in = {k: v for k, v in _L0_ffn_all.items() if k in ('w_gate', 'w1', 'w2', 'w3', 'sw1', 'sw2', 'sw3', 'expert_bias')}
    del _L0_ffn_all

    def _L1_xattn_setup():
        import jax, jax.numpy as jnp
        import numpy as np
        MODEL_DIM = 256
        HEADS = 16
        HEAD_DIM = MODEL_DIM // HEADS
        OUT_DIM = 256
        B, S = (2, 512)

        def _split_heads(x):
            b, s, _ = x.shape
            return x.reshape(b, s, HEADS, HEAD_DIM).transpose(0, 2, 1, 3)
        key = jax.random.key(seed)
        ks = jax.random.split(key, 10)
        scale = 1.0 / np.sqrt(MODEL_DIM)
        return {'query': jax.random.normal(ks[0], (B, S, MODEL_DIM), dtype=jnp.float32), 'bank': jax.random.normal(ks[1], (B, S, MODEL_DIM), dtype=jnp.float32), 'Wq': jax.random.normal(ks[2], (MODEL_DIM, MODEL_DIM), dtype=jnp.float32) * scale, 'bq': jnp.zeros((MODEL_DIM,), dtype=jnp.float32), 'Wk': jax.random.normal(ks[3], (MODEL_DIM, MODEL_DIM), dtype=jnp.float32) * scale, 'bk': jnp.zeros((MODEL_DIM,), dtype=jnp.float32), 'Wv': jax.random.normal(ks[4], (MODEL_DIM, MODEL_DIM), dtype=jnp.float32) * scale, 'bv': jnp.zeros((MODEL_DIM,), dtype=jnp.float32), 'Wo': jax.random.normal(ks[5], (OUT_DIM, MODEL_DIM), dtype=jnp.float32) * scale, 'bo': jnp.zeros((OUT_DIM,), dtype=jnp.float32)}
    _L1_xattn_all = _L1_xattn_setup()
    _L1_xattn_in = {k: v for k, v in _L1_xattn_all.items() if k in ('Wq', 'bq', 'Wk', 'bk', 'Wv', 'bv', 'Wo', 'bo')}
    del _L1_xattn_all

    def _L1_attn_setup():
        import jax, jax.numpy as jnp
        import numpy as np
        import math
        D = 256
        H = 4
        HD = D // H
        DI = int(HD * 1.5)
        FF_INNER = int(D * 4 * 2 / 3)
        K = 4
        RES_SCALE = 1.0

        def _rmsnorm(x, gamma):
            n = jnp.sqrt(jnp.sum(x * x, axis=-1, keepdims=True))
            return x / jnp.maximum(n, 1e-12) * math.sqrt(x.shape[-1]) * (gamma + 1.0)

        def _log_g(x):
            return jnp.where(x >= 0, jnp.log(jax.nn.relu(x) + 0.5), -jax.nn.softplus(-x))

        def _causal_conv(x, dw_w, dw_b, pw_w, pw_b):
            xt = jnp.transpose(x, (0, 2, 1))
            xt = jnp.pad(xt, ((0, 0), (0, 0), (K - 1, 0)))
            y = jax.lax.conv_general_dilated(xt, dw_w, (1,), 'VALID', dimension_numbers=('NCH', 'OIH', 'NCH'), feature_group_count=D) + dw_b[None, :, None]
            y = jnp.einsum('bdl,ed->bel', y, pw_w) + pw_b[None, :, None]
            return jnp.transpose(y, (0, 2, 1))

        def _reference_tuple_inner(x, dw_w, dw_b, pw_w, pw_b, conv_gamma, gru_gamma, ff_gamma, w_hg, w_out, w_gate, w_value, w_ff_out):
            B, L, _ = x.shape
            x = _causal_conv(_rmsnorm(x, conv_gamma), dw_w, dw_b, pw_w, pw_b) * RES_SCALE + x
            normed = _rmsnorm(x, gru_gamma).reshape(B, L, H, HD)
            hg = jnp.einsum('blhd,hde->blhe', normed, w_hg)
            hidden, gate = (hg[..., :DI], hg[..., DI:])
            log_coeffs = -jax.nn.softplus(gate)
            log_values = -jax.nn.softplus(-gate) + _log_g(hidden)
            a_star = jnp.cumsum(log_coeffs, axis=1)
            log_h = a_star + jax.lax.cumlogsumexp(log_values - a_star, axis=1)
            h = jnp.exp(log_h)
            next_hidden = h[:, -1:].reshape(B, 1, H * DI)
            gru_out = jnp.einsum('blhe,heo->blho', h, w_out).reshape(B, L, D)
            x = gru_out * RES_SCALE + x
            n = _rmsnorm(x, ff_gamma)
            ff = jax.nn.silu(n @ w_gate) * (n @ w_value) @ w_ff_out
            x = ff * RES_SCALE + x
            return (x, next_hidden)
        key = jax.random.key(seed)
        ks = jax.random.split(key, 12)
        s = lambda k, shape, sc: jax.random.normal(k, shape, jnp.float32) * sc
        return {'x': s(ks[0], (4, 1024, D), 1.0), 'dw_w': s(ks[1], (D, 1, K), 0.3), 'dw_b': jnp.zeros((D,), jnp.float32), 'pw_w': s(ks[2], (D, D), 1.0 / math.sqrt(D)), 'pw_b': jnp.zeros((D,), jnp.float32), 'conv_gamma': jnp.zeros((D,), jnp.float32), 'gru_gamma': jnp.zeros((D,), jnp.float32), 'ff_gamma': jnp.zeros((D,), jnp.float32), 'w_hg': s(ks[3], (H, HD, 2 * DI), 1.0 / math.sqrt(HD)), 'w_out': s(ks[4], (H, DI, HD), 1.0 / math.sqrt(DI)), 'w_gate': s(ks[5], (D, FF_INNER), 1.0 / math.sqrt(D)), 'w_value': s(ks[6], (D, FF_INNER), 1.0 / math.sqrt(D)), 'w_ff_out': s(ks[7], (FF_INNER, D), 1.0 / math.sqrt(FF_INNER))}
    _L1_attn_all = _L1_attn_setup()
    _L1_attn_in = {k: v for k, v in _L1_attn_all.items() if k in ('dw_w', 'dw_b', 'pw_w', 'pw_b', 'conv_gamma', 'gru_gamma', 'ff_gamma', 'w_hg', 'w_out', 'w_gate', 'w_value', 'w_ff_out')}
    del _L1_attn_all

    def _L1_ffn_setup():
        import jax, jax.numpy as jnp
        import numpy as np
        EMBED_DIM = 256
        HIDDEN = 4 * EMBED_DIM
        BATCH, SEQ = (4, 1024)
        EPS = 1e-05

        def _quant_weight(w):
            s = jnp.clip(jnp.mean(jnp.abs(w)), EPS, None)
            wq = jnp.clip(jnp.round(w / s), -1.0, 1.0) * s
            return w + jax.lax.stop_gradient(wq - w)

        def _quant_act(x):
            scale = 127.0 / jnp.clip(jnp.max(jnp.abs(x), axis=-1, keepdims=True), EPS, None)
            xq = jnp.clip(jnp.round(x * scale), -128.0, 127.0) / scale
            return x + jax.lax.stop_gradient(xq - x)

        def _bitlinear(x, w):
            return jnp.einsum('bsi,oi->bso', _quant_act(x), _quant_weight(w))
        key = jax.random.key(seed)
        k1, k2, k3 = jax.random.split(key, 3)
        x = jax.random.normal(k1, (BATCH, SEQ, EMBED_DIM), dtype=jnp.float32)
        w1 = jax.random.normal(k2, (HIDDEN, EMBED_DIM), dtype=jnp.float32) * (1.0 / np.sqrt(EMBED_DIM))
        w2 = jax.random.normal(k3, (EMBED_DIM, HIDDEN), dtype=jnp.float32) * (1.0 / np.sqrt(HIDDEN))
        return {'x': x, 'w1': w1, 'w2': w2}
    _L1_ffn_all = _L1_ffn_setup()
    _L1_ffn_in = {k: v for k, v in _L1_ffn_all.items() if k in ('w1', 'w2')}
    del _L1_ffn_all
    return {'x': x, 'ctx_1024': ctx_1024, 'L0_xattn_W': _L0_xattn_in['W'], 'L0_xattn_b': _L0_xattn_in['b'], 'L0_attn_Wq': _L0_attn_in['Wq'], 'L0_attn_bq': _L0_attn_in['bq'], 'L0_attn_Wk': _L0_attn_in['Wk'], 'L0_attn_bk': _L0_attn_in['bk'], 'L0_attn_Wv': _L0_attn_in['Wv'], 'L0_attn_bv': _L0_attn_in['bv'], 'L0_attn_Wo': _L0_attn_in['Wo'], 'L0_attn_bo': _L0_attn_in['bo'], 'L0_attn_slopes': _L0_attn_in['slopes'], 'L0_ffn_w_gate': _L0_ffn_in['w_gate'], 'L0_ffn_w1': _L0_ffn_in['w1'], 'L0_ffn_w2': _L0_ffn_in['w2'], 'L0_ffn_w3': _L0_ffn_in['w3'], 'L0_ffn_sw1': _L0_ffn_in['sw1'], 'L0_ffn_sw2': _L0_ffn_in['sw2'], 'L0_ffn_sw3': _L0_ffn_in['sw3'], 'L0_ffn_expert_bias': _L0_ffn_in['expert_bias'], 'L1_xattn_Wq': _L1_xattn_in['Wq'], 'L1_xattn_bq': _L1_xattn_in['bq'], 'L1_xattn_Wk': _L1_xattn_in['Wk'], 'L1_xattn_bk': _L1_xattn_in['bk'], 'L1_xattn_Wv': _L1_xattn_in['Wv'], 'L1_xattn_bv': _L1_xattn_in['bv'], 'L1_xattn_Wo': _L1_xattn_in['Wo'], 'L1_xattn_bo': _L1_xattn_in['bo'], 'L1_attn_dw_w': _L1_attn_in['dw_w'], 'L1_attn_dw_b': _L1_attn_in['dw_b'], 'L1_attn_pw_w': _L1_attn_in['pw_w'], 'L1_attn_pw_b': _L1_attn_in['pw_b'], 'L1_attn_conv_gamma': _L1_attn_in['conv_gamma'], 'L1_attn_gru_gamma': _L1_attn_in['gru_gamma'], 'L1_attn_ff_gamma': _L1_attn_in['ff_gamma'], 'L1_attn_w_hg': _L1_attn_in['w_hg'], 'L1_attn_w_out': _L1_attn_in['w_out'], 'L1_attn_w_gate': _L1_attn_in['w_gate'], 'L1_attn_w_value': _L1_attn_in['w_value'], 'L1_attn_w_ff_out': _L1_attn_in['w_ff_out'], 'L1_ffn_w1': _L1_ffn_in['w1'], 'L1_ffn_w2': _L1_ffn_in['w2']}

def reference(x, ctx_1024, L0_xattn_W, L0_xattn_b, L0_attn_Wq, L0_attn_bq, L0_attn_Wk, L0_attn_bk, L0_attn_Wv, L0_attn_bv, L0_attn_Wo, L0_attn_bo, L0_attn_slopes, L0_ffn_w_gate, L0_ffn_w1, L0_ffn_w2, L0_ffn_w3, L0_ffn_sw1, L0_ffn_sw2, L0_ffn_sw3, L0_ffn_expert_bias, L1_xattn_Wq, L1_xattn_bq, L1_xattn_Wk, L1_xattn_bk, L1_xattn_Wv, L1_xattn_bv, L1_xattn_Wo, L1_xattn_bo, L1_attn_dw_w, L1_attn_dw_b, L1_attn_pw_w, L1_attn_pw_b, L1_attn_conv_gamma, L1_attn_gru_gamma, L1_attn_ff_gamma, L1_attn_w_hg, L1_attn_w_out, L1_attn_w_gate, L1_attn_w_value, L1_attn_w_ff_out, L1_ffn_w1, L1_ffn_w2):
    import jax
    import jax.numpy as jnp

    def _L0_xattn_ref(x1, x2, W, b):
        import jax, jax.numpy as jnp
        import numpy as np
        D1, D2, D3 = (256, 256, 256)
        d1 = x1.shape[-1]
        W1 = W[:, :d1]
        W2 = W[:, d1:]
        part1 = jnp.einsum('bld,ed->ble', x1, W1)
        part2 = jnp.einsum('bld,ed->be', x2, W2) / x2.shape[1]
        return part1 + part2[:, None, :] + b

    def _L0_attn_ref(x, Wq, bq, Wk, bk, Wv, bv, Wo, bo, slopes):
        import jax, jax.numpy as jnp
        import numpy as np
        import math
        B, S, HID, H = (2, 512, 256, 16)
        D = HID // H

        def _get_slopes(n):
            start = 2 ** (-2 ** (-(math.log2(n) - 3)))
            return np.array([start * 2 ** (-i) for i in range(n)], dtype=np.float32)
        b, s, hid = x.shape
        h = slopes.shape[0]
        d = hid // h
        q = (x @ Wq.T + bq).reshape(b, s, h, d).transpose(0, 2, 1, 3)
        k = (x @ Wk.T + bk).reshape(b, s, h, d).transpose(0, 2, 1, 3)
        v = (x @ Wv.T + bv).reshape(b, s, h, d).transpose(0, 2, 1, 3)
        scores = jnp.einsum('bhqd,bhkd->bhqk', q, k) / jnp.sqrt(jnp.float32(d))
        pos = jnp.arange(s)
        dist = (pos[None, :] - pos[:, None]).astype(x.dtype)
        scores = scores + slopes[None, :, None, None] * dist[None, None]
        attn = jax.nn.softmax(scores, axis=-1)
        ctx = jnp.einsum('bhqk,bhkd->bhqd', attn, v)
        ctx = ctx.transpose(0, 2, 1, 3).reshape(b, s, hid)
        return ctx @ Wo.T + bo

    def _L0_ffn_ref(x, w_gate, w1, w2, w3, sw1, sw2, sw3, expert_bias):
        import jax, jax.numpy as jnp
        import numpy as np
        E = 8
        G = 4
        LG = 2
        TOPK = 2
        ROUTE_SCALE = 1.0

        def _grouped_mm(x, w, counts):
            counts = counts.astype(jnp.int32)
            if hasattr(jax.lax, 'ragged_dot'):
                return jax.lax.ragged_dot(x, w, counts)
            offs = jnp.cumsum(counts)
            eid = jnp.searchsorted(offs, jnp.arange(x.shape[0]), side='right')
            oh = jax.nn.one_hot(eid, w.shape[0], dtype=x.dtype)
            return jnp.einsum('nd,ne,edh->nh', x, oh, w)
        bs, slen, dim = x.shape
        xf = x.reshape(-1, dim)
        N = xf.shape[0]
        logits = xf @ w_gate.T
        scores = jax.nn.softmax(logits.astype(jnp.float32), axis=-1)
        original = scores
        s = (scores + expert_bias).reshape(N, G, E // G)
        group_scores = jax.lax.top_k(s, 2)[0].sum(-1)
        top_groups = jax.lax.top_k(group_scores, LG)[1]
        keep = jnp.zeros((N, G), bool).at[jnp.arange(N)[:, None], top_groups].set(True)
        masked = jnp.where(keep[:, :, None], s, -jnp.inf).reshape(N, E)
        topk_idx = jax.lax.top_k(masked, TOPK)[1]
        weights = (jnp.take_along_axis(original, topk_idx, axis=1) * ROUTE_SCALE).astype(x.dtype)
        counts = jnp.bincount(topk_idx.reshape(-1), length=E)
        flat_idx = topk_idx.reshape(-1)
        routed_in = xf[flat_idx]
        routed_in = (routed_in.astype(jnp.float32) * weights.reshape(-1, 1)).astype(x.dtype)
        h = jax.nn.silu(_grouped_mm(routed_in, w1, counts)) * _grouped_mm(routed_in, w3, counts)
        routed_out = _grouped_mm(h, w2, counts)
        shared = jax.nn.silu(xf @ sw1.T) * (xf @ sw3.T) @ sw2.T
        out = shared.at[flat_idx].add(routed_out)
        return out.reshape(bs, slen, dim)

    def _L1_xattn_ref(query, bank, Wq, bq, Wk, bk, Wv, bv, Wo, bo):
        import jax, jax.numpy as jnp
        import numpy as np
        MODEL_DIM = 256
        HEADS = 16
        HEAD_DIM = MODEL_DIM // HEADS
        OUT_DIM = 256
        B, S = (2, 512)

        def _split_heads(x):
            b, s, _ = x.shape
            return x.reshape(b, s, HEADS, HEAD_DIM).transpose(0, 2, 1, 3)
        q = _split_heads(query @ Wq.T + bq)
        k = _split_heads(bank @ Wk.T + bk)
        v = _split_heads(bank @ Wv.T + bv)
        score_scale = jnp.sqrt(jnp.float32(HEAD_DIM))
        scores = jnp.einsum('bhqd,bhkd->bhqk', q / score_scale, k)
        attn = jax.nn.softmax(scores, axis=-1)
        ctx = jnp.einsum('bhqk,bhkd->bhqd', attn, v)
        b, h, sq, hd = ctx.shape
        ctx = ctx.transpose(0, 2, 1, 3).reshape(b, sq, MODEL_DIM)
        return ctx @ Wo.T + bo

    def _L1_attn_ref(x, dw_w, dw_b, pw_w, pw_b, conv_gamma, gru_gamma, ff_gamma, w_hg, w_out, w_gate, w_value, w_ff_out):
        import jax, jax.numpy as jnp
        import numpy as np
        import math
        D = 256
        H = 4
        HD = D // H
        DI = int(HD * 1.5)
        FF_INNER = int(D * 4 * 2 / 3)
        K = 4
        RES_SCALE = 1.0

        def _rmsnorm(x, gamma):
            n = jnp.sqrt(jnp.sum(x * x, axis=-1, keepdims=True))
            return x / jnp.maximum(n, 1e-12) * math.sqrt(x.shape[-1]) * (gamma + 1.0)

        def _log_g(x):
            return jnp.where(x >= 0, jnp.log(jax.nn.relu(x) + 0.5), -jax.nn.softplus(-x))

        def _causal_conv(x, dw_w, dw_b, pw_w, pw_b):
            xt = jnp.transpose(x, (0, 2, 1))
            xt = jnp.pad(xt, ((0, 0), (0, 0), (K - 1, 0)))
            y = jax.lax.conv_general_dilated(xt, dw_w, (1,), 'VALID', dimension_numbers=('NCH', 'OIH', 'NCH'), feature_group_count=D) + dw_b[None, :, None]
            y = jnp.einsum('bdl,ed->bel', y, pw_w) + pw_b[None, :, None]
            return jnp.transpose(y, (0, 2, 1))

        def _reference_tuple_inner(x, dw_w, dw_b, pw_w, pw_b, conv_gamma, gru_gamma, ff_gamma, w_hg, w_out, w_gate, w_value, w_ff_out):
            B, L, _ = x.shape
            x = _causal_conv(_rmsnorm(x, conv_gamma), dw_w, dw_b, pw_w, pw_b) * RES_SCALE + x
            normed = _rmsnorm(x, gru_gamma).reshape(B, L, H, HD)
            hg = jnp.einsum('blhd,hde->blhe', normed, w_hg)
            hidden, gate = (hg[..., :DI], hg[..., DI:])
            log_coeffs = -jax.nn.softplus(gate)
            log_values = -jax.nn.softplus(-gate) + _log_g(hidden)
            a_star = jnp.cumsum(log_coeffs, axis=1)
            log_h = a_star + jax.lax.cumlogsumexp(log_values - a_star, axis=1)
            h = jnp.exp(log_h)
            next_hidden = h[:, -1:].reshape(B, 1, H * DI)
            gru_out = jnp.einsum('blhe,heo->blho', h, w_out).reshape(B, L, D)
            x = gru_out * RES_SCALE + x
            n = _rmsnorm(x, ff_gamma)
            ff = jax.nn.silu(n @ w_gate) * (n @ w_value) @ w_ff_out
            x = ff * RES_SCALE + x
            return (x, next_hidden)
        return _reference_tuple_inner(x, dw_w, dw_b, pw_w, pw_b, conv_gamma, gru_gamma, ff_gamma, w_hg, w_out, w_gate, w_value, w_ff_out)[0]

    def _L1_ffn_ref(x, w1, w2):
        import jax, jax.numpy as jnp
        import numpy as np
        EMBED_DIM = 256
        HIDDEN = 4 * EMBED_DIM
        BATCH, SEQ = (4, 1024)
        EPS = 1e-05

        def _quant_weight(w):
            s = jnp.clip(jnp.mean(jnp.abs(w)), EPS, None)
            wq = jnp.clip(jnp.round(w / s), -1.0, 1.0) * s
            return w + jax.lax.stop_gradient(wq - w)

        def _quant_act(x):
            scale = 127.0 / jnp.clip(jnp.max(jnp.abs(x), axis=-1, keepdims=True), EPS, None)
            xq = jnp.clip(jnp.round(x * scale), -128.0, 127.0) / scale
            return x + jax.lax.stop_gradient(xq - x)

        def _bitlinear(x, w):
            return jnp.einsum('bsi,oi->bso', _quant_act(x), _quant_weight(w))
        h = jax.nn.gelu(_bitlinear(x, w1), approximate=False)
        return _bitlinear(h, w2)
    x = x + _L0_xattn_ref(_layernorm(x, axis=-1), ctx_1024, L0_xattn_W, L0_xattn_b)
    x = x + _L0_attn_ref(_layernorm(x, axis=-1), L0_attn_Wq, L0_attn_bq, L0_attn_Wk, L0_attn_bk, L0_attn_Wv, L0_attn_bv, L0_attn_Wo, L0_attn_bo, L0_attn_slopes)
    x = x + _L0_ffn_ref(_layernorm(x, axis=-1), L0_ffn_w_gate, L0_ffn_w1, L0_ffn_w2, L0_ffn_w3, L0_ffn_sw1, L0_ffn_sw2, L0_ffn_sw3, L0_ffn_expert_bias)
    x = x + _L1_xattn_ref(_layernorm(x, axis=-1), ctx_1024, L1_xattn_Wq, L1_xattn_bq, L1_xattn_Wk, L1_xattn_bk, L1_xattn_Wv, L1_xattn_bv, L1_xattn_Wo, L1_xattn_bo)
    x = x + _L1_attn_ref(_layernorm(x, axis=-1), L1_attn_dw_w, L1_attn_dw_b, L1_attn_pw_w, L1_attn_pw_b, L1_attn_conv_gamma, L1_attn_gru_gamma, L1_attn_ff_gamma, L1_attn_w_hg, L1_attn_w_out, L1_attn_w_gate, L1_attn_w_value, L1_attn_w_ff_out)
    x = x + _L1_ffn_ref(_layernorm(x, axis=-1), L1_ffn_w1, L1_ffn_w2)
    return x

_drawn_inputs = setup_inputs


def setup_inputs(seed=0):
    import zlib

    import numpy as np

    out = dict(_drawn_inputs(seed))
    spreads = {'L0_attn_bq': (0.0, 0.481),
     'L0_attn_bk': (0.0, 2.0),
     'L0_attn_bv': (0.0, 0.1),
     'L0_attn_bo': (0.0, 0.1),
     'L0_ffn_expert_bias': (0.0, 0.8),
     'L1_xattn_bq': (0.0, 2.0),
     'L1_xattn_bk': (0.0, 2.0),
     'L1_xattn_bv': (0.0, 0.8),
     'L1_xattn_bo': (0.0, 0.8),
     'L1_attn_dw_b': (0.0, 0.8),
     'L1_attn_pw_b': (0.0, 0.8),
     'L1_attn_conv_gamma': (0.0, 0.8),
     'L1_attn_gru_gamma': (0.0, 2.0),
     'L1_attn_ff_gamma': (0.0, 0.8)}
    factors = {'L0_ffn_w_gate': 8.0,
     'L0_ffn_w1': 8.0,
     'L0_ffn_w2': 8.0,
     'L0_ffn_w3': 8.0,
     'L0_ffn_sw1': 4.274,
     'L0_ffn_sw2': 4.237,
     'L0_ffn_sw3': 4.224,
     'L1_xattn_Wq': 2.959,
     'L1_xattn_Wk': 2.704,
     'L1_ffn_w1': 3.888,
     'L1_ffn_w2': 3.643}
    for name, (base, spread) in spreads.items():
        noise = np.random.default_rng([zlib.crc32(name.encode()), seed]).standard_normal(out[name].shape)
        drawn = base * np.exp(spread * noise) if base else spread * noise
        out[name] = jnp.asarray(drawn.astype(out[name].dtype))
    for name, factor in factors.items():
        out[name] = (out[name] * factor).astype(out[name].dtype)
    return out
```

```python
from contextlib import ExitStack

import concourse.bass as bass
from concourse import mybir

F32 = mybir.dt.float32
BF16 = mybir.dt.bfloat16
ACT = mybir.ActivationFunctionType
ALU = mybir.AluOpType
AX = mybir.AxisListType

P = 128
B, S, D = 32, 64, 256
KEYS = 1601
H, HD = 16, 16
C = D // P
NT = B * S // P
G = 4
NG = NT // G
GT = G * P
LN_EPS = 1e-5
KT = (KEYS + P - 1) // P
KF = KEYS // P
KR = KEYS - KF * P
KP = KT * P
NCH = (KEYS + 511) // 512
KCH = [(KEYS * n // NCH, KEYS * (n + 1) // NCH - KEYS * n // NCH) for n in range(NCH)]
E, EH = 8, 128
DI = 96
FF = 682
FC = (FF + P - 1) // P
F1 = 1024
F1C = F1 // P
MAGIC = 12582912.0

L0_W = ["xa_w1", "xa_w2", "wq", "wk", "wv", "wo", "sw1", "sw3", "sw2"]
L1_W = ["wq", "wk", "wv", "wo", "pw"]


class Chain:

    def __init__(self, eng, sem, base=0):
        self.eng, self.sem, self.base, self.n = eng, sem, base, 0

    def __call__(self, ins):
        self.n += 1
        ins.then_inc(self.sem, 1)

    def wait(self, met=None):
        if met:
            hold(self.eng, self.sem, self.base + self.n, met)
        else:
            self.eng.wait_ge(self.sem, self.base + self.n)


def hold(eng, sem, value, passed):
    eng.wait_ge(sem, value)
    eng.sem_inc(passed)


class Space:

    def __init__(self, nc, ctx, tag):
        self.nc, self.ctx, self.tag = nc, ctx, tag

    def sem(self, name):
        return self.ctx.enter_context(self.nc.semaphore(f"{self.tag}_{name}"))

    def sb(self, name, shape, dt=F32):
        return self.ctx.enter_context(self.nc.sbuf_tensor(f"{self.tag}_{name}", shape, dt))

    def ps(self, name, shape, dt=F32):
        return self.ctx.enter_context(self.nc.psum_tensor(f"{self.tag}_{name}", shape, dt))


def phase_context_sums(nc, d, keep):
    with ExitStack() as ctx:
        sp = Space(nc, ctx, "p0")
        NB = 4
        buf = [sp.sb(f"ctx{n}", [P, KT, D]) for n in range(NB)]
        part = [sp.sb(f"part{n}", [P, D]) for n in range(2)]
        w2 = sp.sb("w2", [P, C, D])
        bias = sp.sb("bias", [B, D])
        sumT = sp.sb("sumT", [P, C, B])
        c2 = sp.sb("c2", [B, D])
        sum_ps = sp.ps("sum_ps", [P, C, B])
        c2_ps = sp.ps("c2_ps", [B, D])
        landed = [sp.sem(f"ctx_landed{n}") for n in range(NB)]
        summed = [sp.sem(f"summed{n}") for n in range(NB)]
        reduced = [sp.sem(f"reduced{n}") for n in range(NB)]
        weights_in, zeroed, sumT_ready = (sp.sem(n) for n in ("weights_in", "zeroed", "sumT_ready"))
        passed = sp.sem("passed")
        c2_mm, c2_ready, c2_stored, keep_in, bc_in = (sp.sem(n) for n in (
            "c2_mm", "c2_ready", "c2_stored", "keep_in", "bc_in"))

        with nc.Block() as block:
            @block.sync
            def _(sync):
                sync.dma_start(keep.x[:, :, :], d["x"].rearrange("(t p) f -> p t f", p=P)).then_inc(keep_in, 16)
                sync.dma_start(keep.ident[:, :], d["ident"]).then_inc(keep_in, 16)
                sync.dma_start(keep.mask[:, :], d["mask"]).then_inc(keep_in, 16)
                sync.dma_start(w2[:, :, :], d["l0w"][:, L0_W.index("xa_w2"), :, :]).then_inc(weights_in, 16)
                sync.dma_start(bias[:, :], d["xa_b"].partition_broadcast(B)).then_inc(weights_in, 16)
                for n in range(NB):
                    sync.sem_inc(reduced[n], 1)
                sync.wait_ge(zeroed, 1)
                with sync.Fori(0, B // NB) as i:
                    for n in range(NB):
                        sync.wait_ge(reduced[n], i + 1)
                        src = d["ctx"][bass.ds(i * (NB * KEYS) + n * KEYS, KF * P), :]
                        sync.dma_start(buf[n][:, 0:KF, :], src.rearrange("(p t) f -> p t f", p=P)).then_inc(landed[n], 16)
                        tail = d["ctx"][bass.ds(i * (NB * KEYS) + n * KEYS + KF * P, KR), :]
                        sync.dma_start(buf[n][0:KR, KF, :], tail).then_inc(landed[n], 16)
                for buf_, src in keep.l0_loads:
                    sync.dma_start(buf_, src, allow_slow_non_contiguous=True).then_inc(keep.l0_in, 16)
                sync.wait_ge(c2_ready, 1)
                sync.dma_start(d["c2_scratch"], c2[:, :]).then_inc(c2_stored, 16)
                sync.wait_ge(c2_stored, 16)
                for h in range(2):
                    src = d["c2_scratch"].rearrange("(t h) f -> h t f", h=2)[h].partition_broadcast(S)
                    sync.dma_start(keep.c2bc[h * S:(h + 1) * S, :, :], src).then_inc(bc_in, 16)
                sync.wait_ge(bc_in, 32)
                sync.wait_ge(keep_in, 48)

            @block.gpsimd
            def _(pool):
                for n in range(NB):
                    z = pool.memset(buf[n][:, KF, :], 0.0)
                pool.memset(keep.ones[:, :], 1.0)
                z = pool.memset(keep.neg_half[:, :], -0.5)
                z.then_inc(zeroed, 1)

            @block.tensor
            def _(pe):
                pe.wait_ge(zeroed, 1)
                with pe.Fori(0, B // NB) as i:
                    for n in range(NB):
                        pe.wait_ge(reduced[n], i + 2)
                        for c in range(C):
                            mm = pe.matmul(sum_ps[:, c, bass.ds(i * NB + n, 1)], part[n % 2][:, c * P:(c + 1) * P],
                                           keep.ones[:, 0:1], start=True, stop=True)
                        mm.then_inc(summed[n], 1)
                pe.wait_ge(sumT_ready, 1)
                pe.wait_ge(weights_in, 32)
                for c in range(C):
                    mm = pe.matmul(c2_ps[:, :], sumT[:, c, :], w2[:, c, :], start=(c == 0), stop=(c == C - 1))
                mm.then_inc(c2_mm, 1)

            @block.vector
            def _(dve):
                for n in (NB - 2, NB - 1):
                    dve.sem_inc(summed[n], 1)
                with dve.Fori(0, B // NB) as i:
                    for n in range(NB):
                        hold(dve, landed[n], i * 32 + 32, passed)
                        hold(dve, summed[(n - 2) % NB], i + 1, passed)
                        dve.tensor_reduce(part[n % 2][:, :], buf[n][:, :, :].rearrange("p t f -> p f t"), AX.X, ALU.add)\
                            .then_inc(reduced[n], 1)
                for n in range(NB):
                    dve.wait_ge(summed[n], B // NB + (1 if n >= NB - 2 else 0))
                dve.tensor_copy(sumT[:, :, :], sum_ps[:, :, :]).then_inc(sumT_ready, 1)
                dve.wait_ge(c2_mm, 1)
                dve.wait_ge(weights_in, 32)
                dve.scalar_tensor_tensor(out=c2[:, :], in0=c2_ps[:, :], scalar=1.0 / KEYS, in1=bias[:, :],
                                         op0=ALU.mult, op1=ALU.add).then_inc(c2_ready, 1)


class LayerNorm:

    def __init__(self, sp, keep, per, met):
        self.met = met
        self.per, self.keep = per, keep
        self.stats = sp.sb("ln_stats", [P, G, 6])
        self.mv = sp.sb("ln_mv", [P, G, 2])
        self.rstd = sp.sb("ln_rstd", [P, G])
        self.stats_ready, self.rstd_ready, self.norm_ready, self.turned, self.nT_ready, self.pool_eps = (
            sp.sem(n) for n in ("ln_stats_ready", "ln_rstd_ready", "ln_norm_ready", "ln_turned", "ln_nT_ready", "ln_eps"))

    def at(self, i, k):
        return i * self.per + (k + 1)

    def dve(self, dve, chain, i, k, x, out):
        for j in range(G):
            chain(dve.bn_stats(self.stats[:, j, :], x(j)))
        chain.wait(self.met)
        for j in range(G):
            last = dve.bn_aggr(self.mv[:, j, :], self.stats[:, j, :])
        last.then_inc(self.stats_ready, 1)
        dve.wait_ge(self.rstd_ready, self.at(i, k))
        for j in range(G):
            last = dve.tensor_scalar(out(j), x(j), self.mv[:, j, 0:1], self.rstd[:, j:j + 1], ALU.subtract, ALU.mult)
        last.then_inc(self.norm_ready, 1)

    def pool(self, pool, i, k):
        hold(pool, self.stats_ready, self.at(i, k), self.met)
        pool.tensor_scalar(self.rstd[:, :], self.mv[:, :, 1], LN_EPS, None, ALU.add).then_inc(self.pool_eps, 1)
        pool.wait_ge(self.pool_eps, self.at(i, k))
        pool.tensor_tensor(self.rstd[:, :], self.rstd[:, :], self.keep.neg_half[:, 0:G], ALU.pow)\
            .then_inc(self.rstd_ready, 1)


def phase_layer0(nc, d, keep):
    with ExitStack() as ctx:
        sp = Space(nc, ctx, "p1")
        W, wg, bq, bk, bv, bo, dist, slopes = keep.l0
        weights_in = keep.l0_in
        bqm = sp.sb("bqm", [P, C, 2])
        alibi = sp.sb("alibi", [P, 8, S])
        nb = sp.sb("n", [P, G, D])
        nT = sp.sb("nT", [P, C, GT])
        bdq = sp.sb("bdq", [P, C, GT // S, 2, S])
        kT = sp.sb("kT", [P, C, GT])
        V = sp.sb("V", [P, G, D])
        SA = [sp.sb(f"SA{n}", [P, 4, 8, S]) for n in range(2)]
        rowmax = [sp.sb(f"rowmax{n}", [P, 32]) for n in range(2)]
        rowsum = [sp.sb(f"rowsum{n}", [P, 32]) for n in range(2)]
        PT = sp.sb("PT", [P, 2, 8, P])
        O0 = sp.sb("O0", [P, 2, 4, S])
        oT = sp.sb("oT", [P, 2, 4, 2, S])
        th = sp.sb("th", [P, C, GT])
        u = sp.sb("u", [P, C, GT])
        hT = sp.sb("hT", [P, C, GT])
        A = sp.ps("A", [P, 4, 512])
        Q = sp.ps("Q", [P, 4, 512])
        Y = A[:, 2:4, :]
        (prep_done, x_biased, y_ready, y_used, q_ready, k_ready, q_evac, k_evac, s_ready, s_used,
         shifted, exp_ready, p_ready, pt_turned, pt_ready, o_ready, o0_ready, oT_ready, hh_ready, th_ready,
         hT_ready, lg_ready, lg_used, dve_self, prep_self, first_kept) = (sp.sem(n) for n in (
             "prep_done", "x_biased", "y_ready", "y_used", "q_ready", "k_ready", "q_evac", "k_evac",
             "s_ready", "s_used", "shifted", "exp_ready", "p_ready", "pt_turned", "pt_ready", "o_ready", "o0_ready",
             "oT_ready", "hh_ready", "th_ready", "hT_ready", "lg_ready", "lg_used", "dve_self", "prep_self", "first_kept"))
        n_in = len(keep.l0_loads)
        met = sp.sem("passed")
        ln = LayerNorm(sp, keep, 3, met)

        def xt(i, j):
            return keep.x.rearrange("p t f -> p (t f)")[:, bass.ds(i * (G * D) + j * D, D)]

        def group(t, i):
            return t[:, bass.ds(i * G, G), :]

        with nc.Block() as block:
            @block.gpsimd
            def _(pool):
                pool.wait_ge(weights_in, 16 * n_in)
                with pool.Fori(0, NG) as i:
                    ln.pool(pool, i, 0)
                    hold(pool, ln.norm_ready, ln.at(i, 0), met)
                    pool.tensor_tensor(group(keep.x, i), group(keep.x, i), group(keep.c2bc, i), ALU.add)\
                        .then_inc(x_biased, 1)
                    ln.pool(pool, i, 1)
                    hold(pool, ln.norm_ready, ln.at(i, 1), met)
                    pool.tensor_tensor(group(keep.x, i), group(keep.x, i),
                                       bo[:, :].unsqueeze(1).to_broadcast([P, G, D]), ALU.add).then_inc(x_biased, 1)
                    ln.pool(pool, i, 2)
                    hold(pool, ln.norm_ready, ln.at(i, 2), met)
                    pool.tensor_copy(keep.first[:, bass.ds(i, 1), :], nb[0:E, 0:1, :]).then_inc(first_kept, 1)

            @block.scalar
            def _(act):
                act.wait_ge(prep_done, 1)
                with act.Fori(0, NG) as i:
                    def turn(k):
                        act.wait_ge(ln.turned, ln.at(i, k))
                        act.activation(nT[:, 0, :], A[:, 0, :], ACT.Copy).then_inc(ln.nT_ready, 1)

                    turn(0)
                    turn(1)
                    act.wait_ge(q_ready, i + 1)
                    for c in range(C):
                        for par in range(2):
                            last = act.activation(bdq[:, c, :, par, :], Q[:, c, :].rearrange("p (b q) -> p b q", q=S), ACT.Identity,
                                                  bias=bqm[:, c, par:par + 1], scale=keep.mask[:, 2 + par:3 + par])
                    last.then_inc(q_evac, 1)
                    for h in range(2):
                        act.wait_ge(shifted, 2 * i + h + 1)
                        act.activation(SA[h][:, :, :, :], SA[h][:, :, :, :], ACT.Exp).then_inc(exp_ready, 1)
                    for h in range(2):
                        act.wait_ge(pt_turned, 2 * i + h + 1)
                        act.activation(PT[:, 0, :, :].rearrange("p (c j) q -> p c (j q)", c=2), A[:, 0:2, :], ACT.Copy)\
                            .then_inc(pt_ready, 1)
                        act.wait_ge(o_ready, 2 * i + h + 1)
                        act.wait_ge(oT_ready, 2 * i + h + 1)
                        act.activation(O0[:, :, :, :].rearrange("p a g q -> p (a g) q"), Q[:, 2 * h:2 * h + 2, :].rearrange("p a (g e q) -> p (a g) e q", e=2, q=S)[:, :, 0, :],
                                       ACT.Copy, scale=keep.mask[:, 0:1]).then_inc(o0_ready, 1)
                    turn(2)
                    act.wait_ge(hh_ready, i + 1)
                    act.activation(th[:, :, :], Q[:, 0:2, :], ACT.Tanh, scale=0.5).then_inc(th_ready, 1)

            @block.tensor
            def _(pe):
                pe.wait_ge(weights_in, 16 * n_in)
                with pe.Fori(0, NG) as i:
                    def turn(k):
                        pe.wait_ge(ln.norm_ready, ln.at(i, k))
                        for c in range(C):
                            for j in range(G):
                                mm = pe.transpose(A[:, c, j * P:(j + 1) * P],
                                                  nb[:, j, c * P:(c + 1) * P],
                                                  keep.ident[:, :])
                        mm.then_inc(ln.turned, 1)
                        pe.wait_ge(ln.nT_ready, 2 * ln.at(i, k))

                    def rows(src, w, k):
                        pe.wait_ge(y_used, 4 * i + k + 1)
                        for j in range(G):
                            for c in range(C):
                                mm = pe.matmul(Y[:, j // 2, (j % 2) * D:(j % 2 + 1) * D], src(c, j), w[:, c, :],
                                               start=(c == 0), stop=(c == C - 1))
                        mm.then_inc(y_ready, 1)

                    def columns(out, w):
                        for m in range(C):
                            for c in range(C):
                                mm = pe.matmul(out[:, m, :], w[:, c, m * P:(m + 1) * P], nT[:, c, :],
                                               start=(c == 0), stop=(c == C - 1))
                        return mm

                    def tok(c, j):
                        return nT[:, c, j * P:(j + 1) * P]

                    turn(0)
                    rows(tok, W["xa_w1"], 0)
                    turn(1)
                    pe.wait_ge(hT_ready, i + 1)
                    columns(Q[:, 0:2, :], W["wq"]).then_inc(q_ready, 1)
                    columns(Q[:, 2:4, :], W["wk"]).then_inc(k_ready, 1)
                    rows(tok, W["wv"], 1)
                    pe.wait_ge(q_evac, i + 1)
                    pe.wait_ge(k_evac, i + 1)
                    for h in range(2):
                        pe.wait_ge(s_used, 2 * i + h + 1)
                        for c in range(C):
                            for b in range(4):
                                for j in range(4):
                                    r, t0 = slice(32 * j, 32 * j + 32), (4 * h + b) * S
                                    mm = pe.matmul(Q[:, j, (4 * c + b) * S:(4 * c + b + 1) * S],
                                                   bdq[r, c, 4 * h + b, :, :].rearrange("p e q -> p (e q)"), kT[r, c, t0:t0 + S],
                                                   start=True, stop=True, skip_group_check=True)
                        mm.then_inc(s_ready, 1)
                    pe.wait_ge(y_used, 4 * i + 3)
                    pe.wait_ge(s_used, 2 * i + 3)
                    for h in range(2):
                        pe.wait_ge(p_ready, 2 * i + h + 1)
                        for t in range(2):
                            for c in range(C):
                                for j in range(4):
                                    mm = pe.transpose(A[:, 2 * t + c, j * P:(j + 1) * P],
                                                      SA[h][:, j, 4 * c + 2 * t:4 * c + 2 * t + 2, :], keep.ident[:, :])
                        mm.then_inc(pt_turned, 1)
                        hold(pe, pt_ready, 4 * i + 2 * h + 2, met)
                        for t in range(2):
                            for c in range(C):
                                for e in range(2):
                                    for j in range(4):
                                        r = slice(S * e, S * e + S)
                                        mm = pe.matmul(Q[32 * j:32 * j + 32, 2 * h + e, (2 * t + c) * P:(2 * t + c + 1) * P],
                                                       V[r, 2 * h + t, c * P + 32 * j:c * P + 32 * j + 32],
                                                       PT[r, t, 4 * c + j, :], start=True, stop=True, skip_group_check=True)
                        mm.then_inc(o_ready, 1)
                    pe.wait_ge(oT_ready, 2 * i + 3)
                    rows(lambda c, j: oT[:, j // 2, 2 * (j % 2) + c, :, :].rearrange("p e q -> p (e q)"), W["wo"], 2)
                    turn(2)
                    columns(Q[:, 0:2, :], W["sw1"])
                    columns(Q[:, 2:4, :], W["sw3"]).then_inc(hh_ready, 1)
                    for j in range(G):
                        for c in range(C):
                            mm = pe.matmul(A[:, 0, j * E:(j + 1) * E], tok(c, j), wg[:, c, :],
                                           start=(c == 0), stop=(c == C - 1))
                    mm.then_inc(lg_ready, 1)
                    pe.wait_ge(hT_ready, i + 2)
                    rows(lambda c, j: hT[:, c, j * P:(j + 1) * P], W["sw2"], 3)
                    pe.wait_ge(lg_used, i + 1)

            @block.vector
            def _(dve):
                for free in (y_used, hT_ready, s_used, oT_ready, first_kept):
                    dve.sem_inc(free, 1)
                dve.wait_ge(weights_in, 16 * n_in)
                prep = Chain(dve, prep_self)
                for c in range(C):
                    for par in range(2):
                        prep(dve.tensor_tensor(bqm[:, c, par:par + 1], bq[:, c:c + 1], keep.mask[:, 2 + par:3 + par], ALU.mult))
                prep(dve.tensor_tensor(alibi[:, :, :], dist[:, :].unsqueeze(1).to_broadcast([P, 8, S]),
                                       slopes[:, :].unsqueeze(2).to_broadcast([P, 8, S]), ALU.mult))
                prep.wait()
                dve.engine_nop().then_inc(prep_done, 1)
                PER = 19
                with dve.Fori(0, NG) as i:
                    ch = Chain(dve, dve_self, i * PER)

                    def norm(k):
                        ln.dve(dve, ch, i, k, lambda j: xt(i, j), lambda j: nb[:, j, :])
                        dve.wait_ge(ln.turned, ln.at(i, k))
                        dve.tensor_copy(nT[:, 1, :], A[:, 1, :]).then_inc(ln.nT_ready, 1)

                    def add_rows(k):
                        dve.wait_ge(y_ready, 4 * i + k + 1)
                        ins = dve.tensor_tensor(group(keep.x, i), Y.rearrange("p a (b f) -> p (a b) f", b=2), group(keep.x, i), ALU.add)
                        ins.then_inc(y_used, 1)
                        hold(dve, y_used, 4 * i + k + 2, met)

                    hold(dve, first_kept, i + 1, met)
                    norm(0)
                    dve.wait_ge(x_biased, 2 * i + 1)
                    add_rows(0)
                    norm(1)
                    dve.wait_ge(k_ready, i + 1)
                    for c in range(C):
                        last = dve.tensor_scalar(kT[:, c, :], Q[:, 2 + c, :], bk[:, c:c + 1], None, ALU.add)
                    last.then_inc(k_evac, 1)
                    dve.wait_ge(y_ready, 4 * i + 2)
                    dve.tensor_tensor(V[:, :, :], Y.rearrange("p a (b f) -> p (a b) f", b=2),
                                      bv[:, :].unsqueeze(1).to_broadcast([P, G, D]), ALU.add).then_inc(y_used, 1)
                    for h in range(2):
                        sa = SA[h][:, :, :, :].rearrange("p j g k -> p (j g) k")
                        dve.wait_ge(s_ready, 2 * i + h + 1)
                        for c in range(C):
                            ins = dve.tensor_tensor(
                                SA[h][:, :, 4 * c:4 * c + 4, :], Q[:, :, 4 * c * S:(4 * c + 4) * S].rearrange("p j (b k) -> p j b k", b=4),
                                alibi[:, 4 * c:4 * c + 4, :].unsqueeze(2).to_broadcast([P, 4, 4, S]), ALU.add)
                        ins.then_inc(s_used, 1)
                        dve.wait_ge(s_used, 2 * i + h + 2)
                        ch(dve.tensor_reduce(rowmax[h][:, :], sa, AX.X, ALU.max))
                        ch.wait()
                        dve.tensor_tensor(sa, sa, rowmax[h][:, :].unsqueeze(2).to_broadcast([P, 32, S]), ALU.subtract)\
                            .then_inc(shifted, 1)
                    for h in range(2):
                        sa = SA[h][:, :, :, :].rearrange("p j g k -> p (j g) k")
                        dve.wait_ge(exp_ready, 2 * i + h + 1)
                        ch(dve.tensor_reduce(rowsum[h][:, :], sa, AX.X, ALU.add))
                        ch.wait()
                        ch(dve.reciprocal(rowsum[h][:, :], rowsum[h][:, :]))
                        ch.wait()
                        dve.tensor_tensor(sa, sa, rowsum[h][:, :].unsqueeze(2).to_broadcast([P, 32, S]), ALU.mult)\
                            .then_inc(p_ready, 1)
                    for h in range(2):
                        dve.wait_ge(pt_turned, 2 * i + h + 1)
                        dve.tensor_copy(PT[:, 1, :, :].rearrange("p (c j) q -> p c (j q)", c=2), A[:, 2:4, :])\
                            .then_inc(pt_ready, 1)
                        dve.wait_ge(o0_ready, 2 * i + h + 1)
                        for e in range(2):
                            ins = dve.scalar_tensor_tensor(
                                out=oT[:, h, :, e, :], in0=Q[:, 2 * h + e, :].rearrange("p (g a q) -> p g a q", a=2, q=S)[:, :, 1, :],
                                scalar=keep.mask[:, 1:2], in1=O0[:, e, :, :], op0=ALU.mult, op1=ALU.add)
                        ins.then_inc(oT_ready, 1)
                    dve.wait_ge(x_biased, 2 * i + 2)
                    add_rows(2)
                    norm(2)
                    dve.wait_ge(th_ready, i + 1)
                    ch(dve.scalar_tensor_tensor(out=u[:, :, :], in0=th[:, :, :], scalar=1.0, in1=Q[:, 0:2, :],
                                                op0=ALU.add, op1=ALU.mult))
                    ch.wait()
                    dve.scalar_tensor_tensor(out=hT[:, :, :], in0=u[:, :, :], scalar=0.5, in1=Q[:, 2:4, :],
                                             op0=ALU.mult, op1=ALU.mult).then_inc(hT_ready, 1)
                    dve.wait_ge(lg_ready, i + 1)
                    dve.tensor_copy(group(keep.logits, i), A[:, 0, 0:G * E].rearrange("p (j e) -> p j e", j=G)).then_inc(lg_used, 1)
                    add_rows(3)
                    assert ch.n == PER, ch.n


def phase_experts(nc, d, keep):
    with ExitStack() as ctx:
        sp = Space(nc, ctx, "p2")
        GE = E * E
        w13 = sp.sb("w13", [P, C, E, D])
        w2 = sp.sb("w2", [P, E, D])
        ebias = sp.sb("ebias", [P, E])
        pair = sp.sb("pair", [P, NT, 2])
        below = sp.sb("below", [P, E, E])
        upto = sp.sb("upto", [P, E, E])
        score = sp.sb("score", [P, NT, E])
        bsc = sp.sb("bsc", [P, NT, E])
        m1, s1 = sp.sb("m1", [P, NT]), sp.sb("s1", [P, NT])
        gsc = sp.sb("gsc", [P, NT, 4])
        ggt, geq = sp.sb("ggt", [P, NT, 4, 4]), sp.sb("geq", [P, NT, 4, 4])
        grank, goff = sp.sb("grank", [P, NT, 4]), sp.sb("goff", [P, NT, 4])
        egt, eeq = sp.sb("egt", [P, NT, E, E]), sp.sb("eeq", [P, NT, E, E])
        erank = sp.sb("erank", [P, NT, E])
        sel = [sp.sb(f"sel{s}", [P, NT, E]) for s in range(2)]
        both = sp.sb("both", [P, NT, E])
        wsel = sp.sb("wsel", [P, NT, E])
        weight = [sp.sb(f"weight{s}", [P, NT]) for s in range(2)]
        cnt, tot, cum = sp.sb("cnt", [P, E]), sp.sb("tot", [P, E]), sp.sb("cum", [P, E])
        part = sp.sb("part", [P, E, E])
        past = sp.sb("past", [P, NT * 2, E + 1])
        stretch = sp.sb("stretch", [P, NT * 2, E])
        one = sp.sb("one", [P, NT, 2, E, E])
        onew = sp.sb("onew", [P, NT, 2, E, E])
        firstT = sp.sb("firstT", [P, C, E])
        tab = sp.sb("tab", [E, E, D])
        table = sp.sb("table", [P, D])
        oneT = [sp.sb(f"oneT{n}", [P, 4, P]) for n in range(2)]
        th = sp.sb("th", [P, 8, EH])
        u = sp.sb("u", [P, 8, EH])
        hid = [sp.sb(f"hid{n}", [P, 8, EH]) for n in range(2)]
        sT = sp.sb("sT", [P, GE])
        X = [sp.ps(f"X{n}", [P, 4, P]) for n in range(2)]
        HH = sp.ps("HH", [P, 4, 2, D])
        ST = sp.ps("ST", [P, 512])
        out8 = sp.ps("out8", [P, 512])
        (in_, shifted, exped, cnt_ready, tot_mm, first_mm, first_ready, tab_mm, tab_ready, table_in, onew_ready,
         one_ready, turned, oneT_ready, hh_ready, th_ready, hid_ready, sT_mm, sT_ready, out_mm, dve_self) = (
             sp.sem(n) for n in (
                 "in", "shifted", "exped", "cnt_ready", "tot_mm", "first_mm", "first_ready", "tab_mm", "tab_ready",
                 "table_in", "onew_ready", "one_ready", "turned", "oneT_ready", "hh_ready", "th_ready", "hid_ready",
                 "sT_mm", "sT_ready", "out_mm", "dve_self"))
        BIG = 3.0e38

        with nc.Block() as block:
            @block.sync
            def _(sync):
                sync.dma_start(w13[:, :, :, :], d["l0w13"]).then_inc(in_, 16)
                sync.dma_start(w2[:, :, :], d["l0w2"]).then_inc(in_, 16)
                sync.dma_start(ebias[:, :], d["l0eb"].partition_broadcast(P)).then_inc(in_, 16)
                sync.dma_start(pair[:, :, :], d["pair"]).then_inc(in_, 16)
                sync.dma_start(below[:, :, :], d["below"].partition_broadcast(P)).then_inc(in_, 16)
                sync.dma_start(upto[:, :, :], d["upto"].partition_broadcast(P)).then_inc(in_, 16)
                sync.wait_ge(tab_ready, 1)
                for s in range(2):
                    for g in range(E):
                        sync.dma_start(table[s * GE + g * E:s * GE + (g + 1) * E, :], tab[:, g, :]).then_inc(table_in, 16)

            @block.scalar
            def _(act):
                act.wait_ge(shifted, 1)
                act.activation(score[:, :, :], score[:, :, :], ACT.Exp).then_inc(exped, 1)
                act.wait_ge(tab_mm, 1)
                act.activation(tab[:, :, :], HH[0:E, :, :, :].rearrange("p a b f -> p (a b) f"), ACT.Copy).then_inc(tab_ready, 1)
                for q in range(NT // 4):
                    act.wait_ge(hh_ready, q + 1)
                    if q:
                        act.wait_ge(hid_ready, q)
                    act.activation(th[:, :, :], HH[:, :, :, 0:EH].rearrange("p a b f -> p (a b) f"), ACT.Tanh, scale=0.5)\
                       .then_inc(th_ready, 1)

            @block.tensor
            def _(pe):
                for c in range(C):
                    mm = pe.transpose(X[0][:, c, 0:E], keep.first[:, 0, c * P:(c + 1) * P], keep.ident[0:E, 0:E])
                mm.then_inc(first_mm, 1)
                pe.wait_ge(first_ready, 1)
                pe.wait_ge(in_, 96)
                for g in range(E):
                    for c in range(C):
                        mm = pe.matmul(HH[0:E, g // 2, g % 2, :], firstT[:, c, :], w13[:, c, g, :],
                                       start=(c == 0), stop=(c == C - 1))
                mm.then_inc(tab_mm, 1)
                pe.wait_ge(cnt_ready, 1)
                pe.matmul(X[1][:, 0, 0:E], keep.ones[:, :], cnt[:, :], start=True, stop=True).then_inc(tot_mm, 1)
                pe.wait_ge(onew_ready, 1)

                def turn(q):
                    if q >= 2:
                        pe.wait_ge(oneT_ready, q - 1)
                    for t in range(4):
                        mm = pe.transpose(X[q % 2][:, t, :], onew[:, 4 * q + t, :, :, :].rearrange("p s g e -> p (s g e)"),
                                          keep.ident[:, :])
                    mm.then_inc(turned, 1)

                turn(0)
                pe.wait_ge(table_in, 2 * E * 16)
                pe.wait_ge(tab_ready, 1)
                for q in range(NT // 4):
                    if q + 1 < NT // 4:
                        turn(q + 1)
                    pe.wait_ge(oneT_ready, q + 1)
                    if q:
                        pe.wait_ge(hid_ready, q)
                    for t in range(4):
                        for s in range(2):
                            r = slice(s * GE, (s + 1) * GE)
                            mm = pe.matmul(HH[:, 2 * s + t // 2, t % 2, :], oneT[q % 2][r, t, :], table[r, :], start=True, stop=True,
                                           skip_group_check=True)
                    mm.then_inc(hh_ready, 1)
                    pe.wait_ge(hid_ready, q + 1)
                    for t in range(4):
                        for s in range(2):
                            mm = pe.matmul(ST[:, 0:GE], hid[q % 2][:, 4 * s + t, :],
                                           one[:, 4 * q + t, s, :, :].rearrange("p g e -> p (g e)"),
                                           start=(q == t == s == 0), stop=(q == NT // 4 - 1 and t == 3 and s == 1))
                mm.then_inc(sT_mm, 1)
                pe.wait_ge(sT_ready, 1)
                for g in range(E):
                    mm = pe.matmul(out8[0:E, 0:D], sT[:, g * E:(g + 1) * E], w2[:, g, :], start=(g == 0), stop=(g == E - 1))
                mm.then_inc(out_mm, 1)

            @block.vector
            def _(dve):
                ch = Chain(dve, dve_self)

                def step(ins):
                    ch(ins)
                    ch.wait()

                def spread(t, n):
                    return t.unsqueeze(len(t.shape)).to_broadcast(list(t.shape) + [n])

                dve.wait_ge(in_, 96)
                dve.wait_ge(first_mm, 1)
                dve.tensor_copy(firstT[:, :, :], X[0][:, 0:C, 0:E]).then_inc(first_ready, 1)
                step(dve.tensor_reduce(m1[:, :], keep.logits[:, :, :], AX.X, ALU.max))
                dve.tensor_tensor(score[:, :, :], keep.logits[:, :, :], spread(m1[:, :], E), ALU.subtract).then_inc(shifted, 1)
                dve.wait_ge(exped, 1)
                step(dve.tensor_reduce(s1[:, :], score[:, :, :], AX.X, ALU.add))
                step(dve.reciprocal(s1[:, :], s1[:, :]))
                step(dve.tensor_tensor(score[:, :, :], score[:, :, :], spread(s1[:, :], E), ALU.mult))
                step(dve.tensor_tensor(bsc[:, :, :], score[:, :, :], ebias[:, :].unsqueeze(1).to_broadcast([P, NT, E]), ALU.add))
                pairs = bsc[:, :, :].rearrange("p t (g a) -> p t g a", a=2)
                step(dve.tensor_tensor(gsc[:, :, :], pairs[:, :, :, 0], pairs[:, :, :, 1], ALU.add))

                def ranks(sc, n, gt, eq, rank):
                    other, own = sc.unsqueeze(2).to_broadcast([P, NT, n, n]), spread(sc, n)
                    ch(dve.tensor_tensor(gt, other, own, ALU.is_gt))
                    step(dve.tensor_tensor(eq, other, own, ALU.is_equal))
                    step(dve.tensor_tensor(eq, eq, below[:, 0:n, 0:n].unsqueeze(1).to_broadcast([P, NT, n, n]), ALU.mult))
                    step(dve.tensor_tensor(gt, gt, eq, ALU.add))
                    step(dve.tensor_reduce(rank, gt, AX.X, ALU.add))

                ranks(gsc[:, :, :], 4, ggt[:, :, :, :], geq[:, :, :, :], grank[:, :, :])
                step(dve.tensor_scalar(grank[:, :, :], grank[:, :, :], 2.0, None, ALU.is_lt))
                ch(dve.tensor_scalar(goff[:, :, :], grank[:, :, :], -1.0, BIG, ALU.add, ALU.mult))
                step(dve.tensor_tensor(pairs, pairs, spread(grank[:, :, :], 2), ALU.mult))
                step(dve.tensor_tensor(pairs, pairs, spread(goff[:, :, :], 2), ALU.add))
                ranks(bsc[:, :, :], E, egt[:, :, :, :], eeq[:, :, :, :], erank[:, :, :])
                for s in range(2):
                    ch(dve.tensor_scalar(sel[s][:, :, :], erank[:, :, :], float(s), None, ALU.is_equal))
                ch.wait()
                step(dve.tensor_tensor(both[:, :, :], sel[0][:, :, :], sel[1][:, :, :], ALU.add))
                dve.tensor_reduce(cnt[:, :], both[:, :, :].rearrange("p t e -> p e t"), AX.X, ALU.add).then_inc(cnt_ready, 1)
                for s in range(2):
                    step(dve.tensor_tensor(wsel[:, :, :], score[:, :, :], sel[s][:, :, :], ALU.mult))
                    step(dve.tensor_reduce(weight[s][:, :], wsel[:, :, :], AX.X, ALU.add))
                dve.wait_ge(tot_mm, 1)
                step(dve.tensor_copy(tot[:, :], X[1][:, 0, 0:E]))
                step(dve.tensor_tensor(part[:, :, :], tot[:, :].unsqueeze(1).to_broadcast([P, E, E]), upto[:, :, :], ALU.mult))
                step(dve.tensor_reduce(cum[:, :], part[:, :, :], AX.X, ALU.add))
                ch(dve.memset(past[:, :, 0:1], 1.0))
                step(dve.tensor_tensor(past[:, :, 1:E + 1], spread(pair[:, :, :].rearrange("p t s -> p (t s)"), E),
                                       cum[:, :].unsqueeze(1).to_broadcast([P, 2 * NT, E]), ALU.is_ge))
                step(dve.tensor_tensor(stretch[:, :, :], past[:, :, 0:E], past[:, :, 1:E + 1], ALU.subtract))
                for s in range(2):
                    st = stretch[:, :, :].rearrange("p (t s) g -> p t s g", s=2)[:, :, s, :]
                    ch(dve.tensor_tensor(one[:, :, s, :, :], spread(st, E), sel[s][:, :, :].unsqueeze(2).to_broadcast([P, NT, E, E]), ALU.mult))
                ch.wait()
                for s in range(2):
                    last = dve.tensor_tensor(onew[:, :, s, :, :].rearrange("p t g e -> p t (g e)"),
                                             one[:, :, s, :, :].rearrange("p t g e -> p t (g e)"),
                                             spread(weight[s][:, :], GE), ALU.mult)
                last.then_inc(onew_ready, 1)

                def evac(q):
                    dve.wait_ge(turned, q + 1)
                    dve.tensor_copy(oneT[q % 2][:, :, :], X[q % 2][:, :, :]).then_inc(oneT_ready, 1)

                evac(0)
                for q in range(NT // 4):
                    if q + 1 < NT // 4:
                        evac(q + 1)
                    dve.wait_ge(th_ready, q + 1)
                    a, b = (HH[:, :, :, k * EH:(k + 1) * EH].rearrange("p a b f -> p (a b) f") for k in range(2))
                    step(dve.scalar_tensor_tensor(out=u[:, :, :], in0=th[:, :, :], scalar=1.0, in1=a, op0=ALU.add, op1=ALU.mult))
                    dve.scalar_tensor_tensor(out=hid[q % 2][:, :, :], in0=u[:, :, :], scalar=0.5, in1=b,
                                             op0=ALU.mult, op1=ALU.mult).then_inc(hid_ready, 1)
                dve.wait_ge(sT_mm, 1)
                dve.tensor_copy(sT[:, :], ST[:, 0:GE]).then_inc(sT_ready, 1)
                dve.wait_ge(out_mm, 1)
                step(dve.tensor_tensor(keep.x[0:E, 0, :], out8[0:E, 0:D], keep.x[0:E, 0, :], ALU.add))


def phase_queries(nc, d, keep):
    with ExitStack() as ctx:
        sp = Space(nc, ctx, "pq")
        wq, bq, bq4, bo = sp.sb("wq", [P, C, D]), sp.sb("bq", [P, C]), sp.sb("bq4", [P, C]), sp.sb("bo", [P, D])
        nb = sp.sb("n", [P, G, D])
        nT = sp.sb("nT", [P, C, GT])
        A, Q = sp.ps("A", [P, C, GT]), sp.ps("Q", [P, C, GT])
        in_, passed, bias_ready, q_ready, q_evac, x_biased, dve_self = (sp.sem(n) for n in (
            "in", "passed", "bias_ready", "q_ready", "q_evac", "x_biased", "dve_self"))
        ln = LayerNorm(sp, keep, 1, passed)

        def xt(i, j):
            return keep.x.rearrange("p t f -> p (t f)")[:, bass.ds(i * (G * D) + j * D, D)]

        with nc.Block() as block:
            @block.sync
            def _(sync):
                sync.dma_start(wq[:, :, :], d["l1w"][:, L1_W.index("wq"), :, :]).then_inc(in_, 16)
                sync.dma_start(bq[:, :], d["l1bq"]).then_inc(in_, 16)
                sync.dma_start(bo[:, :], d["l1bo"].partition_broadcast(P)).then_inc(in_, 16)

            @block.gpsimd
            def _(pool):
                pool.wait_ge(in_, 48)
                with pool.Fori(0, NG) as i:
                    ln.pool(pool, i, 0)
                    hold(pool, ln.norm_ready, ln.at(i, 0), passed)
                    g = keep.x[:, bass.ds(i * G, G), :]
                    pool.tensor_tensor(g, g, bo[:, :].unsqueeze(1).to_broadcast([P, G, D]), ALU.add).then_inc(x_biased, 1)

            @block.scalar
            def _(act):
                act.wait_ge(bias_ready, 1)
                with act.Fori(0, NG) as i:
                    act.wait_ge(ln.turned, ln.at(i, 0))
                    act.activation(nT[:, 0, :], A[:, 0, :], ACT.Copy).then_inc(ln.nT_ready, 1)
                    hold(act, q_ready, i + 1, passed)
                    for c in range(C):
                        last = act.activation(keep.qT[:, c:c + 1, bass.ds(i * GT, GT)], Q[:, c:c + 1, :], ACT.Identity,
                                              bias=bq4[:, c:c + 1], scale=HD ** -0.5)
                    last.then_inc(q_evac, 1)

            @block.tensor
            def _(pe):
                pe.wait_ge(in_, 48)
                with pe.Fori(0, NG) as i:
                    pe.wait_ge(ln.norm_ready, ln.at(i, 0))
                    for c in range(C):
                        for j in range(G):
                            mm = pe.transpose(A[:, c, j * P:(j + 1) * P], nb[:, j, c * P:(c + 1) * P], keep.ident[:, :])
                    mm.then_inc(ln.turned, 1)
                    pe.wait_ge(ln.nT_ready, 2 * ln.at(i, 0))
                    pe.wait_ge(q_evac, i + 1)
                    for m in range(C):
                        for c in range(C):
                            mm = pe.matmul(Q[:, m, :], wq[:, c, m * P:(m + 1) * P], nT[:, c, :], start=(c == 0), stop=(c == C - 1))
                    mm.then_inc(q_ready, 1)

            @block.vector
            def _(dve):
                dve.sem_inc(q_evac, 1)
                dve.wait_ge(in_, 48)
                dve.tensor_scalar(bq4[:, :], bq[:, :], HD ** -0.5, None, ALU.mult).then_inc(bias_ready, 1)
                PER = 4
                with dve.Fori(0, NG) as i:
                    ch = Chain(dve, dve_self, i * PER)
                    ln.dve(dve, ch, i, 0, lambda j: xt(i, j), lambda j: nb[:, j, :])
                    dve.wait_ge(ln.turned, ln.at(i, 0))
                    dve.tensor_copy(nT[:, 1, :], A[:, 1, :]).then_inc(ln.nT_ready, 1)
                    assert ch.n == PER


def phase_context_attention(nc, d, keep):
    with ExitStack() as ctx:
        sp = Space(nc, ctx, "p3")
        U = H // 2
        UC = U // C
        W = {n: sp.sb(f"w_{n}", [P, C, D]) for n in ("wk", "wv", "wo")}
        bk, bv = sp.sb("bk", [P, C]), sp.sb("bv", [P, D])
        mask8 = sp.sb("mask8", [P, 8])
        maskd = sp.sb("maskd", [P, 2 * HD])
        fold = sp.sb("fold", [P, S])
        zeros = sp.sb("zeros", [P, 512])
        rows = [sp.sb(f"rows{s}", [P, KT, D]) for s in range(2)]
        rowsT = sp.sb("rowsT", [P, C, KP])
        kT = [sp.sb(f"kT{s}", [P, C, KP]) for s in range(2)]
        V = [sp.sb(f"V{s}", [P, KT, D]) for s in range(2)]
        bdq = [sp.sb(f"bdq{s}", [P, C, 8, S]) for s in range(2)]
        prob = [sp.sb(f"prob{n}", [P, KP]) for n in range(4)]
        mx = [sp.sb(f"mx{n}", [P, len(KCH)]) for n in range(4)]
        nmx = [sp.sb(f"nmx{n}", [P, 1]) for n in range(4)]
        probT = [sp.sb(f"probT{j}", [P, KP]) for j in range(UC)]
        sums = [sp.sb(f"sums{s}", [P, U]) for s in range(2)]
        rsum = sp.sb("rsum", [P, U])
        spreadr = sp.sb("spreadr", [P, U, 2 * HD])
        o0, o1 = sp.sb("o0", [P, C, S]), sp.sb("o1", [P, C, S])
        oT = sp.sb("oT", [P, C, P])
        Sc = [sp.ps(f"Sc{n}", [P, 512]) for n in range(2)]
        M = [sp.ps(f"M{n}", [P, 512]) for n in range(2)]
        T = [sp.ps(f"T{n}", [P, 512]) for n in range(2)]
        O = sp.ps("O", [P, C, P])
        RY = sp.ps("RY", [P, 512])
        R, Y = RY[:, 0:C * S].rearrange("p (c q) -> p c q", c=C), RY[:, C * S:C * S + D]
        landed = [sp.sem(f"rows_landed{s}") for s in range(2)]
        turned = [sp.sem(f"rows_turned{s}") for s in range(2)]
        (in_, cleared, passed, m_filled, m_used, bd_ready, bd_free, s_filled, s_used, max_ready, exp_ready, t_filled, t_used,
         o_ready, o_used, spread_ready, r_ready, oT_ready, y_ready, y_used, dve_self) = (sp.sem(n) for n in (
             "in", "cleared", "passed", "m_filled", "m_used", "bd_ready", "bd_free", "s_filled", "s_used", "max_ready",
             "exp_ready", "t_filled", "t_used", "o_ready", "o_used", "spread_ready", "r_ready", "oT_ready", "y_ready",
             "y_used", "dve_self"))
        NI = NT
        NQ = len(KCH)
        NTG = (KT + 3) // 4
        assert NTG == NQ
        VF = (KT + 1) // 2
        FILLS = [("turn", g, c) for g in range(NTG) for c in range(C)] + \
                [("key", n, m) for n in range(NQ) for m in range(C)] + [("value", v, 0) for v in range(VF)]
        NFILL = len(FILLS)
        NTURN = NTG * C
        SLOTS = [2] * (U - 1) + [3] * 3
        assert sum(SLOTS) == NFILL

        def slot(k):
            return range(sum(SLOTS[:k]), sum(SLOTS[:k + 1]))


        def load(sync, s, batch):
            src = d["ctx"][bass.ds(batch * KEYS, KF * P), :]
            sync.dma_start(rows[s][:, 0:KF, :], src.rearrange("(p t) f -> p t f", p=P)).then_inc(landed[s], 16)
            sync.dma_start(rows[s][0:KR, KF, :], d["ctx"][bass.ds(batch * KEYS + KF * P, KR), :]).then_inc(landed[s], 16)

        def fill(pe, f, s, batch, n_landed):
            kind, a, b = FILLS[f]
            bank = M[(s + f) % 2]
            F = batch * NFILL + f
            if kind == "turn":
                if f == 0:
                    pe.wait_ge(landed[s], 32 * n_landed)
                pe.wait_ge(m_used, F + 1)
                for t in range(4 * a, min(4 * a + 4, KT)):
                    mm = pe.transpose(bank[:, (t - 4 * a) * P:(t - 4 * a + 1) * P], rows[s][:, t, b * P:(b + 1) * P], keep.ident[:, :])
                mm.then_inc(m_filled, 1)
                if f == NTURN - 1:
                    pe.wait_ge(m_filled, F + 1)
                    pe.sem_inc(turned[s], 1)
                return
            if kind == "key":
                pe.wait_ge(m_used, F + 1)
                if f == NTURN:
                    pe.wait_ge(m_used, batch * NFILL + NTURN + 2)
                k0, kn = KCH[a]
                for c in range(C):
                    mm = pe.matmul(bank[:, 0:kn], W["wk"][:, c, b * P:(b + 1) * P], rowsT[:, c, k0:k0 + kn],
                                   start=(c == 0), stop=(c == C - 1))
            else:
                pe.wait_ge(m_used, F + 1)
                for t in range(2 * a, min(2 * a + 2, KT)):
                    for c in range(C):
                        mm = pe.matmul(bank[:, (t - 2 * a) * D:(t - 2 * a + 1) * D], rowsT[:, c, t * P:(t + 1) * P], W["wv"][:, c, :],
                                       start=(c == 0), stop=(c == C - 1))
            mm.then_inc(m_filled, 1)

        def drain(dve, f, s, batch):
            kind, a, b = FILLS[f]
            bank = M[(s + f) % 2]
            dve.wait_ge(m_filled, batch * NFILL + f + 1)
            if kind == "turn":
                n = (min(4 * a + 4, KT) - 4 * a) * P
                ins = dve.tensor_copy(rowsT[:, b, 4 * a * P:4 * a * P + n], bank[:, 0:n])
            elif kind == "key":
                k0, kn = KCH[a]
                ins = dve.tensor_scalar(kT[s][:, b, k0:k0 + kn], bank[:, 0:kn], bk[:, b:b + 1], None, ALU.add)
            else:
                n = min(2 * a + 2, KT) - 2 * a
                ins = dve.tensor_tensor(V[s][:, 2 * a:2 * a + n, :], bank[:, 0:n * D].rearrange("p (t f) -> p t f", t=n),
                                        bv[:, :].unsqueeze(1).to_broadcast([P, n, D]), ALU.add)
            ins.then_inc(m_used, 1)

        def pairs_of_batches(eng, body):
            with eng.Fori(0, NI - 1) as i:
                body(i, False)
            body(NI - 1, True)

        with nc.Block() as block:
            @block.sync
            def _(sync):
                for n in W:
                    sync.dma_start(W[n][:, :, :], d["l1w"][:, L1_W.index(n), :, :]).then_inc(in_, 16)
                sync.dma_start(bk[:, :], d["l1bk"]).then_inc(in_, 16)
                sync.dma_start(bv[:, :], d["l1bv"].partition_broadcast(P)).then_inc(in_, 16)
                sync.dma_start(mask8[:, :], d["mask8"]).then_inc(in_, 16)
                sync.dma_start(maskd[:, :], d["maskd"]).then_inc(in_, 16)
                sync.dma_start(fold[:, :], d["fold"]).then_inc(in_, 16)
                sync.wait_ge(cleared, 1)
                for s in range(2):
                    load(sync, s, s)
                with sync.Fori(1, NI) as i:
                    for s in range(2):
                        sync.wait_ge(turned[s], i)
                        load(sync, s, 2 * i + s)

            @block.gpsimd
            def _(pool):
                for s in range(2):
                    pool.memset(rows[s][:, KF, :], 0.0)
                pool.memset(zeros[:, :], 0.0)
                for n in range(4):
                    last = pool.memset(prob[n][:, KEYS:KP], 0.0)
                last.then_inc(cleared, 1)
                pool.sem_inc(bd_free, 2)
                pool.wait_ge(in_, 128)

                def queries(i, last):
                    for s in range(2):
                        hold(pool, bd_free, 2 * i + s + 1, passed)
                        q = keep.qT[:, :, bass.ds(i * P + s * S, S)] if not last else keep.qT[:, :, i * P + s * S:i * P + s * S + S]
                        pool.tensor_tensor(bdq[s][:, :, :, :], q.unsqueeze(2).to_broadcast([P, C, 8, S]),
                                           mask8[:, :].unsqueeze(1).unsqueeze(3).to_broadcast([P, C, 8, S]), ALU.mult)\
                            .then_inc(bd_ready, 1)

                pairs_of_batches(pool, queries)

            @block.tensor
            def _(pe):
                pe.wait_ge(in_, 128)
                pe.wait_ge(cleared, 1)
                for f in range(NFILL):
                    fill(pe, f, 0, 0, 1)

                def score(i, s, u, n):
                    g = 16 * i + 8 * s + u
                    c, j = u // UC, u % UC
                    k0, kn = KCH[n]
                    if u == 0 and n == 0:
                        pe.wait_ge(bd_ready, 2 * i + s + 1)
                        pe.wait_ge(m_used, (2 * i + s + 1) * NFILL + 2)
                    pe.wait_ge(s_used, NQ * g + n + 1)
                    mm = pe.matmul(Sc[n % 2][:, 0:kn], bdq[s][:, c, 2 * j:2 * j + 2, :].rearrange("p a q -> p (a q)"),
                                   kT[s][:, c, k0:k0 + kn], start=True, stop=True)
                    mm.then_inc(s_filled, 1)
                    if u == U - 1 and n == NQ - 1:
                        pe.wait_ge(s_filled, NQ * (g + 1))
                        pe.sem_inc(bd_free, 1)

                def turn_probs(i, s, u, n):
                    g = 16 * i + 8 * s + u
                    if n == 0:
                        pe.wait_ge(exp_ready, g + 1)
                    pe.wait_ge(t_used, NQ * g + n + 1)
                    for t in range(4 * n, min(4 * n + 4, KT)):
                        mm = pe.transpose(T[n % 2][:, (t - 4 * n) * P:(t - 4 * n + 1) * P], prob[u % 4][:, t * P:(t + 1) * P], keep.ident[:, :])
                    mm.then_inc(t_filled, 1)

                def weigh(i, s, c):
                    g = 16 * i + 8 * s + UC * (c + 1)
                    if c == 0:
                        pe.wait_ge(o_used, 2 * i + s + 1)
                    hold(pe, t_used, NQ * g + 2, passed)
                    for t in range(KT):
                        for j in range(UC):
                            mm = pe.matmul(O[32 * j:32 * j + 32, c, :], V[s][:, t, c * P + 32 * j:c * P + 32 * j + 32],
                                           probT[j][:, t * P:(t + 1) * P], start=(t == 0), stop=(t == KT - 1))
                    mm.then_inc(o_ready, 1)

                def body(i, last):
                    for s in range(2):
                        def prepare(k, m=None):
                            for f in list(slot(k))[m]:
                                if not (last and s == 1):
                                    fill(pe, f, 1 - s, 2 * i + s + 1, i + 1 + s)

                        for u in range(U):
                            score(i, s, u, 0)
                            for n in range(1, NQ):
                                score(i, s, u, n)
                                if u:
                                    turn_probs(i, s, u - 1, n - 1)
                            prepare(u, slice(0, 1))
                            if u:
                                turn_probs(i, s, u - 1, NQ - 1)
                            prepare(u, slice(1, None))
                            if u == UC:
                                weigh(i, s, 0)
                        for n in range(NQ):
                            turn_probs(i, s, U - 1, n)
                        prepare(U, slice(None))
                        weigh(i, s, 1)
                        prepare(U + 1, slice(None))
                        pe.wait_ge(spread_ready, 2 * i + s + 1)
                        for c in range(C):
                            mm = pe.matmul(R[:, c, :], spreadr[:, UC * c:UC * c + UC, :].rearrange("p a e -> p (a e)"), fold[:, :],
                                           start=True, stop=True)
                        mm.then_inc(r_ready, 1)
                    pe.wait_ge(oT_ready, 2 * i + 2)
                    pe.wait_ge(y_used, i + 1)
                    for c in range(C):
                        mm = pe.matmul(Y, oT[:, c, :], W["wo"][:, c, :], start=(c == 0), stop=(c == C - 1))
                    mm.then_inc(y_ready, 1)

                pairs_of_batches(pe, body)

            @block.scalar
            def _(act):
                act.sem_inc(t_used, 2)
                act.wait_ge(cleared, 1)

                def exps(i, s, u):
                    g = 16 * i + 8 * s + u
                    act.wait_ge(max_ready, g + 1)
                    act.activation(prob[u % 4][:, 0:KEYS], prob[u % 4][:, 0:KEYS], ACT.Exp, bias=nmx[u % 4][:, 0:1],
                                   accum_out=sums[s][:, u:u + 1]).then_inc(exp_ready, 1)

                def turned_out(i, s, u):
                    g = 16 * i + 8 * s + u
                    for n in range(NQ):
                        w = (min(4 * n + 4, KT) - 4 * n) * P
                        act.wait_ge(t_filled, NQ * g + n + 1)
                        act.activation(probT[u % UC][:, 4 * n * P:4 * n * P + w], T[n % 2][:, 0:w], ACT.Copy).then_inc(t_used, 1)

                def body(i, last):
                    for s in range(2):
                        for u in range(U):
                            if u:
                                turned_out(i, s, u - 1)
                            exps(i, s, u)
                        turned_out(i, s, U - 1)

                pairs_of_batches(act, body)

            @block.vector
            def _(dve):
                dve.sem_inc(m_used, 2)
                dve.sem_inc(s_used, 2)
                dve.sem_inc(o_used, 1)
                dve.sem_inc(y_used, 1)
                dve.wait_ge(in_, 128)
                dve.wait_ge(cleared, 1)
                for f in range(NFILL):
                    drain(dve, f, 0, 0)
                PER = 4

                def body(i, last):
                    ch = Chain(dve, dve_self, i * PER)
                    for s in range(2):
                        def prepared(k):
                            for f in slot(k):
                                if not (last and s == 1):
                                    drain(dve, f, 1 - s, 2 * i + s + 1)

                        for u in range(U):
                            g = 16 * i + 8 * s + u
                            for n, (k0, kn) in enumerate(KCH):
                                hold(dve, s_filled, NQ * g + n + 1, passed)
                                ins = dve.tensor_tensor_reduce(prob[u % 4][:, k0:k0 + kn], Sc[n % 2][:, 0:kn], zeros[:, 0:kn], 1.0, -3.0e38,
                                                               ALU.add, ALU.max, mx[u % 4][:, n:n + 1])
                                ins.then_inc(s_used, 1)
                            dve.wait_ge(s_used, NQ * (g + 1) + 2)
                            dve.tensor_reduce(nmx[u % 4][:, :], mx[u % 4][:, :], AX.X, ALU.max, negate=True).then_inc(max_ready, 1)
                            prepared(u)
                        prepared(U)
                        dve.wait_ge(exp_ready, 16 * i + 8 * (s + 1))
                        ch(dve.reciprocal(rsum[:, :], sums[s][:, :]))
                        ch.wait()
                        dve.tensor_tensor(spreadr[:, :, :], rsum[:, :].unsqueeze(2).to_broadcast([P, U, 2 * HD]),
                                          maskd[:, :].unsqueeze(1).to_broadcast([P, U, 2 * HD]), ALU.mult).then_inc(spread_ready, 1)
                        prepared(U + 1)
                        dve.wait_ge(o_ready, 2 * (2 * i + s) + 2)
                        ch(dve.tensor_scalar(o0[:, :, :], O[:, :, 0:S], keep.mask[:, 0:1], None, ALU.mult))
                        ch.wait()
                        ins = dve.scalar_tensor_tensor(out=o1[:, :, :], in0=O[:, :, S:P], scalar=keep.mask[:, 1:2], in1=o0[:, :, :],
                                                       op0=ALU.mult, op1=ALU.add)
                        ins.then_inc(o_used, 1)
                        dve.wait_ge(o_used, 2 * i + s + 2)
                        dve.wait_ge(r_ready, 2 * i + s + 1)
                        dve.tensor_tensor(oT[:, :, s * S:(s + 1) * S], R, o1[:, :, :], ALU.mult).then_inc(oT_ready, 1)
                    hold(dve, y_ready, i + 1, passed)
                    xi = keep.x.rearrange("p t f -> p (t f)")
                    xi = xi[:, i * D:(i + 1) * D] if last else xi[:, bass.ds(i * D, D)]
                    dve.tensor_tensor(xi, Y, xi, ALU.add).then_inc(y_used, 1)
                    assert ch.n == PER, ch.n

                pairs_of_batches(dve, body)


def phase_layer1(nc, d, keep):
    with ExitStack() as ctx:
        sp = Space(nc, ctx, "p4")
        NB = GT // S
        K = 4
        pw = sp.sb("pw", [P, C, D])
        hgw = sp.sb("hgw", [P, 4, 2, P])
        gow = sp.sb("gow", [P, 4, S])
        fgw, fvw = sp.sb("fgw", [P, C, FC * P]), sp.sb("fvw", [P, C, FC * P])
        fow = sp.sb("fow", [P, FC, D])
        pwb = sp.sb("pwb", [P, D])
        dw, dwb = sp.sb("dw", [P, C, K]), sp.sb("dwb", [P, C])
        gam = sp.sb("gam", [P, 3, C])
        w1, w2 = sp.sb("w1", [P, C, F1]), sp.sb("w2", [P, F1C, D])
        w1q, w2q = sp.sb("w1q", [P, C, F1], BF16), sp.sb("w2q", [P, F1C, D], BF16)
        wabs, wsc, wfac = (sp.sb(n, [P, 2]) for n in ("wabs", "wsc", "wfac"))
        whalf = sp.sb("whalf", [P, 4])
        y = sp.sb("y", [P, G, D])
        rb = sp.sb("rb", [P, G, D])
        ss, rs = sp.sb("ss", [P, G]), sp.sb("rs", [P, G])
        floor = sp.sb("floor", [P, G])
        uT = sp.sb("uT", [P, C, NB, S + K - 1])
        cv = sp.sb("cv", [P, C, GT])
        nT = sp.sb("nT", [P, C, GT])
        tg, thid = ([sp.sb(f"{n}{k}", [P, 2, GT]) for k in range(2)] for n in ("tg", "thid"))
        z, q, a, v = ([sp.sb(f"{n}{k}", [P, 2, GT]) for k in range(2)] for n in ("z", "q", "a", "v"))
        h = sp.sb("h", [P, 4, GT])
        tf, fu = ([sp.sb(f"{n}{k}", [P, GT]) for k in range(2)] for n in ("tf", "fu"))
        ff = sp.sb("ff", [P, FC, GT])
        am, s1, gs = (sp.sb(n, [P, G]) for n in ("am", "s1", "gs"))
        xq = sp.sb("xq", [P, G, D], BF16)
        xqT = sp.sb("xqT", [P, C, GT], BF16)
        hb = [sp.sb(f"hb{k}", [P, F1]) for k in range(2)]
        hr = sp.sb("hr", [P, F1])
        am2, s2, es = (sp.sb(n, [P, G]) for n in ("am2", "s2", "es"))
        hq = [sp.sb(f"hq{k}", [P, F1], BF16) for k in range(2)]
        hqT = [sp.sb(f"hqT{k}", [P, F1C, P], BF16) for k in range(2)]
        identb = sp.sb("identb", [P, P], BF16)
        A, Q = sp.ps("A", [P, 4, 512]), sp.ps("Q", [P, 4, 512])
        Y = A[:, 2:4, :]
        (in_, passed, cleared, prep, wsum_ready, wsum_mm, sq_ready, floor_ready, rs_ready, rb_ready, turned, nT_ready, cv_ready, y_biased,
         x_joined, y_ready, y_used, hg_ready, tanh_ready, zq_ready, h_ready, ff_filled, tf_ready, ff_ready, xq_ready, xq_turned,
         xqT_ready, up_ready, gelu_ready, hq_ready, hq_turned, hqT_ready, dve_self, pool_self) = (sp.sem(n) for n in (
             "in", "passed", "cleared", "prep", "wsum_ready", "wsum_mm", "sq_ready", "floor_ready", "rs_ready", "rb_ready", "turned",
             "nT_ready", "cv_ready", "y_biased", "x_joined", "y_ready", "y_used", "hg_ready", "tanh_ready", "zq_ready", "h_ready",
             "ff_filled", "tf_ready", "ff_ready", "xq_ready", "xq_turned", "xqT_ready", "up_ready", "gelu_ready", "hq_ready",
             "hq_turned", "hqT_ready", "dve_self", "pool_self"))
        ln = LayerNorm(sp, keep, 2, passed)
        loads = [(pw, d["l1w"][:, L1_W.index("pw"), :, :]), (hgw, d["hgw"]), (gow, d["gow"]), (fgw, d["fgw"]), (fvw, d["fvw"]),
                 (fow, d["fow"]), (pwb, d["pwb"].partition_broadcast(P)), (dw, d["dw"]), (dwb, d["dwb"]), (gam, d["gam"]),
                 (w1, d["w1"]), (w2, d["w2"])]
        n_in = 16 * len(loads)
        YU = 7

        def full(t):
            return t[tuple(slice(None) for _ in t.shape)]

        def xt(i, j):
            return keep.x.rearrange("p t f -> p (t f)")[:, bass.ds(i * (G * D) + j * D, D)]

        def xg(i):
            return keep.x[:, bass.ds(i * G, G), :]

        with nc.Block() as block:
            @block.sync
            def _(sync):
                for t, src in loads:
                    sync.dma_start(full(t), src).then_inc(in_, 16)

            @block.gpsimd
            def _(pool):
                pool.memset(uT[:, :, :, 0:K - 1], 0.0)
                pool.tensor_copy(identb[:, :], keep.ident[:, :]).then_inc(cleared, 1)
                pool.wait_ge(in_, n_in)
                with pool.Fori(0, NG) as i:
                    ch = Chain(pool, pool_self, i * 3)

                    def rms(k):
                        hold(pool, sq_ready, 3 * i + k + 1, passed)
                        ch(pool.tensor_scalar(floor[:, :], ss[:, :], 1e-24, None, ALU.max))
                        hold(pool, pool_self, i * 3 + ch.n, passed)
                        pool.tensor_tensor(rs[:, :], floor[:, :], keep.neg_half[:, 0:G], ALU.pow).then_inc(rs_ready, 1)

                    ln.pool(pool, i, 0)
                    rms(0)
                    hold(pool, rb_ready, 3 * i + 1, passed)
                    pool.tensor_tensor(y[:, :, :], y[:, :, :], pwb[:, :].unsqueeze(1).to_broadcast([P, G, D]), ALU.add).then_inc(y_biased, 1)
                    rms(1)
                    for r in range(2):
                        hold(pool, tanh_ready, 2 * i + r + 1, passed)
                        pool.tensor_scalar(z[r][:, :, :], tg[r][:, :, :], 0.5, 0.5, ALU.mult, ALU.add)
                        pool.tensor_scalar(q[r][:, :, :], thid[r][:, :, :], 0.0, 0.5, ALU.min, ALU.mult).then_inc(zq_ready, 1)
                    rms(2)
                    hold(pool, rb_ready, 3 * i + 3, passed)
                    pool.tensor_tensor(y[:, :, :], y[:, :, :], xg(i), ALU.add).then_inc(x_joined, 1)
                    ln.pool(pool, i, 1)
                    assert ch.n == 3

            @block.scalar
            def _(act):
                act.wait_ge(prep, 1)
                with act.Fori(0, NG) as i:
                    act.wait_ge(turned, 3 * i + 1)
                    act.activation(uT[:, 0, :, K - 1:], A[:, 0, :].rearrange("p (b l) -> p b l", l=S), ACT.Copy).then_inc(nT_ready, 1)
                    act.wait_ge(turned, 3 * i + 2)
                    act.activation(nT[:, 0, :], A[:, 0, :], ACT.Copy, scale=gam[:, 1, 0:1]).then_inc(nT_ready, 1)
                    for r in range(2):
                        src = (Q, A)[r]
                        act.wait_ge(hg_ready, 2 * i + r + 1)
                        act.activation(tg[r][:, :, :], src[:, 2:4, :], ACT.Tanh, scale=0.5)
                        act.activation(thid[r][:, :, :], src[:, 0:2, :], ACT.Tanh, scale=0.5).then_inc(tanh_ready, 1)
                    act.wait_ge(turned, 3 * i + 3)
                    act.activation(nT[:, 0, :], A[:, 0, :], ACT.Copy, scale=gam[:, 2, 0:1]).then_inc(nT_ready, 1)
                    for f in range(FC):
                        act.wait_ge(ff_filled, FC * i + f + 1)
                        act.activation(tf[f % 2][:, :], Q[:, 2 * (f % 2), :], ACT.Tanh, scale=0.5).then_inc(tf_ready, 1)

                    def turned_hidden(j):
                        act.wait_ge(hq_turned, G * i + j + 1)
                        act.activation(hqT[j % 2][:, :, :].rearrange("p c t -> p (c t)"), A[:, 1, :].bitcast(BF16), ACT.Copy).then_inc(hqT_ready, 1)

                    for j in range(G):
                        act.wait_ge(up_ready, G * i + j + 1)
                        act.activation(hb[j % 2][:, :], Q[:, 2 * (j % 2):2 * (j % 2) + 2, :], ACT.Gelu, scale=gs[:, j:j + 1])\
                           .then_inc(gelu_ready, 1)
                        if j:
                            turned_hidden(j - 1)
                    turned_hidden(G - 1)

            @block.tensor
            def _(pe):
                pe.wait_ge(in_, n_in)
                pe.wait_ge(wsum_ready, 1)
                pe.matmul(Q[:, 0, 0:2], keep.ones[:, :], wabs[:, :], start=True, stop=True).then_inc(wsum_mm, 1)
                pe.wait_ge(prep, 1)
                with pe.Fori(0, NG) as i:
                    def turn(k):
                        pe.wait_ge(rb_ready, 3 * i + k + 1)
                        for c in range(C):
                            for j in range(G):
                                mm = pe.transpose(A[:, c, j * P:(j + 1) * P], rb[:, j, c * P:(c + 1) * P], keep.ident[:, :])
                        mm.then_inc(turned, 1)

                    turn(0)
                    pe.wait_ge(y_used, YU * i + 1)
                    pe.wait_ge(cv_ready, i + 1)
                    for j in range(G):
                        for c in range(C):
                            mm = pe.matmul(Y[:, j // 2, (j % 2) * D:(j % 2 + 1) * D], cv[:, c, j * P:(j + 1) * P], pw[:, c, :],
                                           start=(c == 0), stop=(c == C - 1))
                    mm.then_inc(y_ready, 1)
                    turn(1)
                    pe.wait_ge(nT_ready, 6 * i + 4)
                    for r in range(2):
                        dst = (Q, A)[r]
                        for kind in range(2):
                            for hh in range(2):
                                head = 2 * r + hh
                                mm = pe.matmul(dst[:, 2 * kind + hh, :], hgw[:, head, kind, :], nT[:, head // 2, :], start=True, stop=True)
                        mm.then_inc(hg_ready, 1)
                    pe.wait_ge(h_ready, 2 * i + 2)
                    for j in range(G):
                        for head in range(4):
                            mm = pe.matmul(Y[:, j // 2, (j % 2) * D + head * S:(j % 2) * D + (head + 1) * S],
                                           h[:, head, j * P:(j + 1) * P], gow[:, head, :], start=True, stop=True)
                    mm.then_inc(y_ready, 1)
                    turn(2)
                    pe.wait_ge(nT_ready, 6 * i + 6)
                    for f in range(FC):
                        if f >= 2:
                            pe.wait_ge(ff_ready, FC * i + f - 1)
                        for k, w in enumerate((fgw, fvw)):
                            for c in range(C):
                                mm = pe.matmul(Q[:, 2 * (f % 2) + k, :], w[:, c, f * P:(f + 1) * P], nT[:, c, :],
                                               start=(c == 0), stop=(c == C - 1))
                        mm.then_inc(ff_filled, 1)
                    pe.wait_ge(ff_ready, FC * i + FC)
                    for j in range(G):
                        for f in range(FC):
                            mm = pe.matmul(Y[:, j // 2, (j % 2) * D:(j % 2 + 1) * D], ff[:, f, j * P:(j + 1) * P], fow[:, f, :],
                                           start=(f == 0), stop=(f == FC - 1))
                    mm.then_inc(y_ready, 1)
                    pe.wait_ge(xq_ready, i + 1)
                    for c in range(C):
                        for j in range(G):
                            mm = pe.transpose(A[:, 0, :].bitcast(BF16)[:, (c * G + j) * P:(c * G + j + 1) * P],
                                              xq[:, j, c * P:(c + 1) * P], identb[:, :])
                    mm.then_inc(xq_turned, 1)
                    pe.wait_ge(xqT_ready, i + 1)

                    def up(j):
                        if j >= 2:
                            pe.wait_ge(gelu_ready, G * i + j - 1)
                        for o in range(2):
                            for c in range(C):
                                mm = pe.matmul(Q[:, 2 * (j % 2) + o, :], xqT[:, c, j * P:(j + 1) * P], w1q[:, c, o * 512:(o + 1) * 512],
                                               start=(c == 0), stop=(c == C - 1))
                        mm.then_inc(up_ready, 1)

                    up(0)
                    up(1)
                    for j in range(G):
                        pe.wait_ge(hq_ready, G * i + j + 1)
                        for c in range(F1C):
                            mm = pe.transpose(A[:, 1, :].bitcast(BF16)[:, c * P:(c + 1) * P], hq[j % 2][:, c * P:(c + 1) * P], identb[:, :])
                        mm.then_inc(hq_turned, 1)
                        if j + 2 < G:
                            up(j + 2)
                        pe.wait_ge(hqT_ready, G * i + j + 1)
                        if j >= 2:
                            pe.wait_ge(y_used, YU * i + 3 + j)
                        for c in range(F1C):
                            mm = pe.matmul(Y[:, j % 2, 0:D], hqT[j % 2][:, c, :], w2q[:, c, :],
                                           start=(c == 0), stop=(c == F1C - 1))
                        mm.then_inc(y_ready, 1)

            @block.vector
            def _(dve):
                dve.sem_inc(y_used, 1)
                dve.wait_ge(in_, n_in)
                dve.wait_ge(cleared, 1)
                pc = Chain(dve, dve_self)

                def step(ins):
                    pc(ins)
                    pc.wait()

                step(dve.tensor_scalar(gam[:, :, :], gam[:, :, :], 1.0, None, ALU.add))
                pc(dve.tensor_tensor(dw[:, :, :], dw[:, :, :], gam[:, 0, :].unsqueeze(2).to_broadcast([P, C, K]), ALU.mult))
                for k, w in enumerate((w1, w2)):
                    last = dve.tensor_reduce(wabs[:, k:k + 1], w[:, :, :].rearrange("p a b -> p (a b)"), AX.X, ALU.add, apply_absolute_value=True)
                last.then_inc(wsum_ready, 1)
                dve.wait_ge(wsum_mm, 1)
                step(dve.tensor_scalar(wsc[:, :], Q[:, 0, 0:2], 1.0 / (F1 * D), 1e-5, ALU.mult, ALU.max))
                pc(dve.tensor_scalar(wfac[:, :], wsc[:, :], 1.0 / 127.0, None, ALU.mult))
                pc(dve.tensor_scalar(whalf[:, 0:2], wsc[:, :], 0.5, None, ALU.mult))
                step(dve.tensor_scalar(whalf[:, 2:4], wsc[:, :], -0.5, None, ALU.mult))
                for k, (w, wq) in enumerate(((w1, w1q), (w2, w2q))):
                    step(dve.tensor_scalar(wq[:, :, :], w[:, :, :], whalf[:, 2 + k:3 + k], None, ALU.is_lt))
                    step(dve.scalar_tensor_tensor(out=wq[:, :, :], in0=w[:, :, :], scalar=whalf[:, k:k + 1], in1=wq[:, :, :],
                                                  op0=ALU.is_gt, op1=ALU.subtract))
                dve.engine_nop().then_inc(prep, 1)
                BASE = pc.n
                PER = 64
                with dve.Fori(0, NG) as i:
                    ch = Chain(dve, dve_self, i * PER + BASE)

                    def go(ins):
                        ch(ins)
                        ch.wait()

                    def rms(k):
                        for j in range(G):
                            last = dve.tensor_tensor_reduce(rb[:, j, :], y[:, j, :], y[:, j, :], 1.0, 0.0, ALU.mult, ALU.add, ss[:, j:j + 1])
                        last.then_inc(sq_ready, 1)
                        dve.wait_ge(rs_ready, 3 * i + k + 1)
                        for j in range(G):
                            last = dve.tensor_scalar(rb[:, j, :], y[:, j, :], rs[:, j:j + 1], float(D) ** 0.5, ALU.mult, ALU.mult)
                        last.then_inc(rb_ready, 1)

                    def rows_in():
                        return Y.rearrange("p a (b f) -> p (a b) f", b=2)

                    ln.dve(dve, ch, i, 0, lambda j: xt(i, j), lambda j: y[:, j, :])
                    hold(dve, ln.norm_ready, ln.at(i, 0), passed)
                    rms(0)
                    dve.wait_ge(turned, 3 * i + 1)
                    dve.tensor_copy(uT[:, 1, :, K - 1:], A[:, 1, :].rearrange("p (b l) -> p b l", l=S)).then_inc(nT_ready, 1)
                    dve.wait_ge(nT_ready, 6 * i + 2)
                    cvv = cv[:, :, :].rearrange("p c (b l) -> p c b l", l=S)
                    for c in range(C):
                        ch(dve.tensor_scalar(cvv[:, c, :, :], uT[:, c, :, 0:S], dw[:, c, 0:1], dwb[:, c:c + 1], ALU.mult, ALU.add))
                    for k in range(1, K):
                        ch.wait()
                        for c in range(C):
                            ins = dve.scalar_tensor_tensor(out=cvv[:, c, :, :], in0=uT[:, c, :, k:k + S], scalar=dw[:, c, k:k + 1],
                                                           in1=cvv[:, c, :, :], op0=ALU.mult, op1=ALU.add)
                            if k < K - 1:
                                ch(ins)
                    ins.then_inc(cv_ready, 1)
                    dve.wait_ge(y_biased, i + 1)
                    dve.wait_ge(y_ready, YU * i + 1)
                    go(dve.tensor_tensor(y[:, :, :], rows_in(), y[:, :, :], ALU.add))
                    dve.sem_inc(y_used, 1)
                    rms(1)
                    dve.wait_ge(turned, 3 * i + 2)
                    dve.tensor_scalar(nT[:, 1, :], A[:, 1, :], gam[:, 1, 1:2], None, ALU.mult).then_inc(nT_ready, 1)
                    for r in range(2):
                        src = (Q, A)[r]
                        dve.wait_ge(tanh_ready, 2 * i + r + 1)
                        go(dve.tensor_scalar(a[r][:, :, :], tg[r][:, :, :], -0.5, 0.5, ALU.mult, ALU.add))
                        ch(dve.memset(a[r][:, :, :].rearrange("p a (b l) -> p (a b) l", l=S)[:, :, 0:1], 0.0))
                        dve.wait_ge(zq_ready, 2 * i + r + 1)
                        go(dve.scalar_tensor_tensor(out=v[r][:, :, :], in0=src[:, 0:2, :], scalar=0.0, in1=q[r][:, :, :], op0=ALU.max, op1=ALU.add))
                        go(dve.scalar_tensor_tensor(out=v[r][:, :, :], in0=v[r][:, :, :], scalar=0.5, in1=z[r][:, :, :], op0=ALU.add, op1=ALU.mult))
                        dve.tensor_tensor_scan(h[:, 2 * r:2 * r + 2, :].rearrange("p a t -> p (a t)"), a[r][:, :, :].rearrange("p a t -> p (a t)"),
                                               v[r][:, :, :].rearrange("p a t -> p (a t)"), 0.0, ALU.mult, ALU.add).then_inc(h_ready, 1)
                    dve.wait_ge(y_ready, YU * i + 2)
                    go(dve.tensor_tensor(y[:, :, :], rows_in(), y[:, :, :], ALU.add))
                    dve.sem_inc(y_used, 1)
                    rms(2)
                    dve.wait_ge(turned, 3 * i + 3)
                    dve.tensor_scalar(nT[:, 1, :], A[:, 1, :], gam[:, 2, 1:2], None, ALU.mult).then_inc(nT_ready, 1)
                    for f in range(FC):
                        dve.wait_ge(tf_ready, FC * i + f + 1)
                        go(dve.scalar_tensor_tensor(out=fu[f % 2][:, :], in0=tf[f % 2][:, :], scalar=1.0, in1=Q[:, 2 * (f % 2), :],
                                                    op0=ALU.add, op1=ALU.mult))
                        dve.scalar_tensor_tensor(out=ff[:, f, :], in0=fu[f % 2][:, :], scalar=0.5, in1=Q[:, 2 * (f % 2) + 1, :],
                                                 op0=ALU.mult, op1=ALU.mult).then_inc(ff_ready, 1)
                    dve.wait_ge(x_joined, i + 1)
                    dve.wait_ge(y_ready, YU * i + 3)
                    ch(dve.tensor_tensor(xg(i), rows_in(), y[:, :, :], ALU.add))
                    hold(dve, dve_self, i * PER + BASE + ch.n, passed)
                    dve.sem_inc(y_used, 1)
                    ln.dve(dve, ch, i, 1, lambda j: xt(i, j), lambda j: y[:, j, :])
                    dve.wait_ge(ln.norm_ready, ln.at(i, 1))
                    go(dve.tensor_reduce(am[:, :], y[:, :, :], AX.X, ALU.max, apply_absolute_value=True))
                    go(dve.tensor_scalar(am[:, :], am[:, :], 1e-5, None, ALU.max))
                    ch(dve.tensor_scalar(gs[:, :], am[:, :], wfac[:, 0:1], None, ALU.mult))
                    go(dve.reciprocal(s1[:, :], am[:, :]))
                    go(dve.tensor_scalar(s1[:, :], s1[:, :], 127.0, None, ALU.mult))
                    for j in range(G):
                        ch(dve.tensor_scalar(rb[:, j, :], y[:, j, :], s1[:, j:j + 1], MAGIC, ALU.mult, ALU.add))
                    ch.wait()
                    dve.tensor_scalar(xq[:, :, :], rb[:, :, :], MAGIC, 127.0, ALU.subtract, ALU.min).then_inc(xq_ready, 1)
                    dve.wait_ge(xq_turned, i + 1)
                    dve.tensor_copy(xqT[:, :, :].rearrange("p c t -> p (c t)"), A[:, 0, :].bitcast(BF16)).then_inc(xqT_ready, 1)

                    def down(j):
                        hold(dve, y_ready, YU * i + 4 + j, passed)
                        dve.scalar_tensor_tensor(out=xt(i, j), in0=Y[:, j % 2, 0:D], scalar=es[:, j:j + 1], in1=xt(i, j),
                                                 op0=ALU.mult, op1=ALU.add).then_inc(y_used, 1)

                    for j in range(G):
                        dve.wait_ge(gelu_ready, G * i + j + 1)
                        m = am2[:, j:j + 1]
                        go(dve.tensor_reduce(m, hb[j % 2][:, :], AX.X, ALU.max, apply_absolute_value=True))
                        go(dve.tensor_scalar(m, m, 1e-5, None, ALU.max))
                        ch(dve.tensor_scalar(es[:, j:j + 1], m, wfac[:, 1:2], None, ALU.mult))
                        go(dve.reciprocal(s2[:, j:j + 1], m))
                        go(dve.tensor_scalar(s2[:, j:j + 1], s2[:, j:j + 1], 127.0, None, ALU.mult))
                        go(dve.tensor_scalar(hr[:, :], hb[j % 2][:, :], s2[:, j:j + 1], MAGIC, ALU.mult, ALU.add))
                        dve.tensor_scalar(hq[j % 2][:, :], hr[:, :], MAGIC, 127.0, ALU.subtract, ALU.min).then_inc(hq_ready, 1)
                        if j:
                            down(j - 1)
                    down(G - 1)
                    hold(dve, y_used, YU * i + 1 + YU, passed)
                    assert ch.n == PER, ch.n


class Keep:

    def __init__(self, nc, ctx):
        def sb(name, shape):
            return ctx.enter_context(nc.sbuf_tensor(f"keep_{name}", shape, F32))

        self.x = sb("x", [P, NT, D])
        self.ident = sb("ident", [P, P])
        self.mask = sb("mask", [P, 4])
        self.ones = sb("ones", [P, P])
        self.neg_half = sb("neg_half", [P, NT])
        self.first = ctx.enter_context(nc.sbuf_tensor("keep_first", [E, NG, D], F32))
        self.logits = sb("logits", [P, NT, E])


def layer0_inputs(nc, d, keep, ctx):
    def sb(name, shape):
        return ctx.enter_context(nc.sbuf_tensor(f"l0_{name}", shape, F32))

    W = {n: sb(f"w_{n}", [P, C, D]) for n in L0_W if n != "xa_w2"}
    wg, bq, bk = sb("wg", [P, C, E]), sb("bq", [P, C]), sb("bk", [P, C])
    bv, bo = sb("bv", [P, D]), sb("bo", [P, D])
    dist, slopes = sb("dist", [P, S]), sb("slopes", [P, 8])
    head_pairs = d["slopes"].rearrange("(j a) -> a j", a=2)
    keep.l0 = W, wg, bq, bk, bv, bo, dist, slopes
    keep.l0_in = ctx.enter_context(nc.semaphore("l0_in"))
    keep.l0_loads = [(W[n][:, :, :], d["l0w"][:, L0_W.index(n), :, :]) for n in W] + [
        (wg[:, :, :], d["l0wg"]), (bq[:, :], d["l0bq"]), (bk[:, :], d["l0bk"]),
        (bv[:, :], d["l0bv"].partition_broadcast(P)), (bo[:, :], d["l0bo"].partition_broadcast(P)),
        (dist[:, :], d["dist"]),
        (slopes[0:S, :], head_pairs[0].partition_broadcast(S)), (slopes[S:P, :], head_pairs[1].partition_broadcast(S))]


def program(nc, d, out):
    with ExitStack() as ctx:
        keep = Keep(nc, ctx)
        with ExitStack() as early:
            keep.c2bc = early.enter_context(nc.sbuf_tensor("keep_c2bc", [P, NT, D], F32))
            layer0_inputs(nc, d, keep, early)
            phase_context_sums(nc, d, keep)
            phase_layer0(nc, d, keep)
        phase_experts(nc, d, keep)
        with ExitStack() as late:
            keep.qT = late.enter_context(nc.sbuf_tensor("keep_qT", [P, C, B * S], F32))
            phase_queries(nc, d, keep)
            phase_context_attention(nc, d, keep)
        phase_layer1(nc, d, keep)
        phase_store(nc, keep, out)


def phase_store(nc, keep, out):
    with nc.semaphore("out_stored") as stored, nc.Block() as block:
        @block.sync
        def _(sync):
            sync.dma_start(out.rearrange("(t p) f -> p t f", p=P), keep.x[:, :, :]).then_inc(stored, 16)
            sync.wait_ge(stored, 16)


def kernel(**inputs):
    import numpy as np
    import concourse.bacc as bacc
    from concourse.bass_utils import run_bass_kernel_spmd

    a = {k: np.ascontiguousarray(v) for k, v in inputs.items()}
    f = np.float32

    def lhs(w):
        return np.ascontiguousarray(w.reshape(-1, P, w.shape[1]).transpose(1, 0, 2))

    def col(v):
        return np.ascontiguousarray(v.reshape(-1, P).T)

    xw = a["L0_xattn_W"]
    l0 = {"xa_w1": xw[:, :D].T, "xa_w2": xw[:, D:].T, "wq": a["L0_attn_Wq"].T, "wk": a["L0_attn_Wk"].T,
          "wv": a["L0_attn_Wv"].T, "wo": a["L0_attn_Wo"].T, "sw1": a["L0_ffn_sw1"].T, "sw3": a["L0_ffn_sw3"].T,
          "sw2": a["L0_ffn_sw2"].T}
    l1 = {"wq": a["L1_xattn_Wq"].T, "wk": a["L1_xattn_Wk"].T, "wv": a["L1_xattn_Wv"].T, "wo": a["L1_xattn_Wo"].T,
          "pw": a["L1_attn_pw_w"].T}
    r = np.arange(P)
    own = np.stack([(r // HD) % 2 == 0, (r // HD) % 2 == 1], 1).astype(f)
    ins = {
        "x": a["x"].reshape(B * S, D),
        "ctx": a["ctx_1024"].reshape(B * KEYS, D),
        "ident": np.eye(P, dtype=f),
        "mask": np.concatenate([own, own * f(0.25)], 1),
        "l0w": np.ascontiguousarray(np.stack([lhs(l0[n]) for n in L0_W], 1)),
        "xa_b": a["L0_xattn_b"],
        "l0wg": lhs(a["L0_ffn_w_gate"].T),
        "l0bq": col(a["L0_attn_bq"]), "l0bk": col(a["L0_attn_bk"]), "l0bv": a["L0_attn_bv"], "l0bo": a["L0_attn_bo"],
        "dist": (np.arange(S)[None, :] - (r % S)[:, None]).astype(f),
        "slopes": a["L0_attn_slopes"],
        "l1w": np.ascontiguousarray(np.stack([lhs(l1[n]) for n in L1_W], 1)),
    }
    e = np.arange(E)
    ins.update({
        "l0w13": np.ascontiguousarray(np.concatenate([a["L0_ffn_w1"], a["L0_ffn_w3"]], 2).reshape(E, C, P, D).transpose(2, 1, 0, 3)),
        "l0w2": np.ascontiguousarray(a["L0_ffn_w2"].transpose(1, 0, 2)),
        "l0eb": a["L0_ffn_expert_bias"],
        "pair": (2 * (np.arange(NT)[None, :, None] * P + r[:, None, None]) + np.arange(2)[None, None, :]).astype(f),
        "below": (e[None, :] < e[:, None]).astype(f),
        "upto": (e[None, :] <= e[:, None]).astype(f),
    })
    ins.update({
        "l1bq": col(a["L1_xattn_bq"]), "l1bk": col(a["L1_xattn_bk"]), "l1bv": a["L1_xattn_bv"], "l1bo": a["L1_xattn_bo"],
        "mask8": (r[:, None] // HD == np.arange(8)[None, :]).astype(f),
        "maskd": (r[:, None] // S == np.arange(2 * HD)[None, :] // HD).astype(f),
        "fold": (r[:, None] % S == np.arange(S)[None, :]).astype(f),
    })
    def padded(w, rows, cols):
        out = np.zeros((rows, cols), f)
        out[:w.shape[0], :w.shape[1]] = w
        return out

    hgw = np.zeros((P, 4, 2, P), f)
    gow = np.zeros((P, 4, S), f)
    for h in range(4):
        lo = (h % 2) * S
        hgw[lo:lo + S, h, 0, :DI] = a["L1_attn_w_hg"][h][:, :DI]
        hgw[lo:lo + S, h, 1, :DI] = a["L1_attn_w_hg"][h][:, DI:]
        gow[:DI, h, :] = a["L1_attn_w_out"][h]
    ins.update({
        "hgw": hgw, "gow": gow,
        "fgw": lhs(padded(a["L1_attn_w_gate"], D, FC * P)), "fvw": lhs(padded(a["L1_attn_w_value"], D, FC * P)),
        "fow": lhs(padded(a["L1_attn_w_ff_out"], FC * P, D)), "pwb": a["L1_attn_pw_b"],
        "dw": lhs(a["L1_attn_dw_w"][:, 0, :]), "dwb": col(a["L1_attn_dw_b"]),
        "gam": np.ascontiguousarray(np.stack([col(a[f"L1_attn_{n}_gamma"]) for n in ("conv", "gru", "ff")], 1)),
        "w1": lhs(a["L1_ffn_w1"].T), "w2": lhs(a["L1_ffn_w2"].T),
    })
    nc = bacc.Bacc("TRN2", target_bir_lowering=False, num_devices=1)
    d = {k: nc.dram_tensor(f"in_{k}_dram", v.shape, mybir.dt.from_np(v.dtype), kind="ExternalInput").ap()
         for k, v in ins.items()}
    d["c2_scratch"] = nc.dram_tensor("c2_scratch", [B, D], F32).ap()
    out = nc.dram_tensor("out_0_dram", (B * S, D), F32, kind="ExternalOutput").ap()
    program(nc, d, out)
    res = run_bass_kernel_spmd(nc, [{f"in_{k}_dram": v for k, v in ins.items()}], core_ids=[0])
    return res.results[0]["out_0_dram"].reshape(B, S, D)
```

```python
from contextlib import ExitStack

import concourse.bass as bass
from concourse import mybir

F32 = mybir.dt.float32
BF16 = mybir.dt.bfloat16
ACT = mybir.ActivationFunctionType
ALU = mybir.AluOpType
AX = mybir.AxisListType

P = 128
B, S, D = 32, 64, 256
KEYS = 1601
H, HD = 16, 16
C = D // P
NT = B * S // P
G = 4
NG = NT // G
GT = G * P
LN_EPS = 1e-5
KT = (KEYS + P - 1) // P
KF = KEYS // P
KR = KEYS - KF * P
KP = KT * P
NCH = (KEYS + 511) // 512
KCH = [(KEYS * n // NCH, KEYS * (n + 1) // NCH - KEYS * n // NCH) for n in range(NCH)]
E, EH = 8, 128
DI = 96
FF = 682
FC = (FF + P - 1) // P
F1 = 1024
F1C = F1 // P
MAGIC = 12582912.0

L0_W = ["xa_w1", "xa_w2", "wq", "wk", "wv", "wo", "sw1", "sw3", "sw2"]
L1_W = ["wq", "wk", "wv", "wo", "pw"]


class Chain:

    def __init__(self, eng, sem, base=0):
        self.eng, self.sem, self.base, self.n = eng, sem, base, 0

    def __call__(self, ins):
        self.n += 1
        ins.then_inc(self.sem, 1)

    def wait(self, met=None):
        if met:
            hold(self.eng, self.sem, self.base + self.n, met)
        else:
            self.eng.wait_ge(self.sem, self.base + self.n)


def hold(eng, sem, value, passed):
    eng.wait_ge(sem, value)
    eng.sem_inc(passed)


class Space:

    def __init__(self, nc, ctx, tag):
        self.nc, self.ctx, self.tag = nc, ctx, tag

    def sem(self, name):
        return self.ctx.enter_context(self.nc.semaphore(f"{self.tag}_{name}"))

    def sb(self, name, shape, dt=F32):
        return self.ctx.enter_context(self.nc.sbuf_tensor(f"{self.tag}_{name}", shape, dt))

    def ps(self, name, shape, dt=F32):
        return self.ctx.enter_context(self.nc.psum_tensor(f"{self.tag}_{name}", shape, dt))


def phase_context_sums(nc, d, keep):
    with ExitStack() as ctx:
        sp = Space(nc, ctx, "p0")
        NB = 4
        buf = [sp.sb(f"ctx{n}", [P, KT, D]) for n in range(NB)]
        part = [sp.sb(f"part{n}", [P, D]) for n in range(2)]
        w2 = sp.sb("w2", [P, C, D])
        bias = sp.sb("bias", [B, D])
        sumT = sp.sb("sumT", [P, C, B])
        c2 = sp.sb("c2", [B, D])
        sum_ps = sp.ps("sum_ps", [P, C, B])
        c2_ps = sp.ps("c2_ps", [B, D])
        landed = [sp.sem(f"ctx_landed{n}") for n in range(NB)]
        summed = [sp.sem(f"summed{n}") for n in range(NB)]
        reduced = [sp.sem(f"reduced{n}") for n in range(NB)]
        weights_in, zeroed, sumT_ready = (sp.sem(n) for n in ("weights_in", "zeroed", "sumT_ready"))
        passed = keep.passed
        c2_mm, c2_ready, c2_stored, keep_in = (sp.sem(n) for n in (
            "c2_mm", "c2_ready", "c2_stored", "keep_in"))

        with nc.Block() as block:
            @block.sync
            def _(sync):
                sync.dma_start(keep.x[:, :, :], d["x"].rearrange("(t p) f -> p t f", p=P)).then_inc(keep_in, 16)
                sync.dma_start(keep.ident[:, :], d["ident"]).then_inc(keep_in, 16)
                sync.dma_start(keep.mask[:, :], d["mask"]).then_inc(keep_in, 16)
                sync.dma_start(w2[:, :, :], d["l0w"][:, L0_W.index("xa_w2"), :, :]).then_inc(weights_in, 16)
                sync.dma_start(bias[:, :], d["xa_b"].partition_broadcast(B)).then_inc(weights_in, 16)
                for n in range(NB):
                    sync.sem_inc(reduced[n], 1)
                sync.wait_ge(zeroed, 1)
                with sync.Fori(0, B // NB) as i:
                    for n in range(NB):
                        sync.wait_ge(reduced[n], i + 1)
                        src = d["ctx"][bass.ds(i * (NB * KEYS) + n * KEYS, KF * P), :]
                        sync.dma_start(buf[n][:, 0:KF, :], src.rearrange("(p t) f -> p t f", p=P)).then_inc(landed[n], 16)
                        tail = d["ctx"][bass.ds(i * (NB * KEYS) + n * KEYS + KF * P, KR), :]
                        sync.dma_start(buf[n][0:KR, KF, :], tail).then_inc(landed[n], 16)
                for buf_, src in keep.l0_loads:
                    sync.dma_start(buf_, src, allow_slow_non_contiguous=True).then_inc(keep.l0_in, 16)
                sync.wait_ge(c2_ready, 1)
                sync.dma_start(d["c2_scratch"], c2[:, :]).then_inc(c2_stored, 16)
                sync.wait_ge(c2_stored, 16)
                for h in range(2):
                    src = d["c2_scratch"].rearrange("(t h) f -> h t f", h=2)[h].partition_broadcast(S)
                    sync.dma_start(keep.c2bc[h * S:(h + 1) * S, :, :], src).then_inc(keep.c2_in, 16)
                sync.wait_ge(keep_in, 48)

            @block.gpsimd
            def _(pool):
                for n in range(NB):
                    z = pool.memset(buf[n][:, KF, :], 0.0)
                pool.memset(keep.ones[:, :], 1.0)
                z = pool.memset(keep.neg_half[:, :], -0.5)
                z.then_inc(zeroed, 1)

            @block.tensor
            def _(pe):
                pe.wait_ge(zeroed, 1)
                with pe.Fori(0, B // NB) as i:
                    for n in range(NB):
                        pe.wait_ge(reduced[n], i + 2)
                        for c in range(C):
                            mm = pe.matmul(sum_ps[:, c, bass.ds(i * NB + n, 1)], part[n % 2][:, c * P:(c + 1) * P],
                                           keep.ones[:, 0:1], start=True, stop=True)
                        mm.then_inc(summed[n], 1)
                pe.wait_ge(sumT_ready, 1)
                pe.wait_ge(weights_in, 32)
                for c in range(C):
                    mm = pe.matmul(c2_ps[:, :], sumT[:, c, :], w2[:, c, :], start=(c == 0), stop=(c == C - 1))
                mm.then_inc(c2_mm, 1)

            @block.vector
            def _(dve):
                for n in (NB - 2, NB - 1):
                    dve.sem_inc(summed[n], 1)
                with dve.Fori(0, B // NB) as i:
                    for n in range(NB):
                        hold(dve, landed[n], i * 32 + 32, passed)
                        hold(dve, summed[(n - 2) % NB], i + 1, passed)
                        dve.tensor_reduce(part[n % 2][:, :], buf[n][:, :, :].rearrange("p t f -> p f t"), AX.X, ALU.add)\
                            .then_inc(reduced[n], 1)
                for n in range(NB):
                    dve.wait_ge(summed[n], B // NB + (1 if n >= NB - 2 else 0))
                dve.tensor_copy(sumT[:, :, :], sum_ps[:, :, :]).then_inc(sumT_ready, 1)
                dve.wait_ge(c2_mm, 1)
                dve.wait_ge(weights_in, 32)
                dve.scalar_tensor_tensor(out=c2[:, :], in0=c2_ps[:, :], scalar=1.0 / KEYS, in1=bias[:, :],
                                         op0=ALU.mult, op1=ALU.add).then_inc(c2_ready, 1)


class LayerNorm:

    def __init__(self, sp, keep, per, met):
        self.met = met
        self.per, self.keep = per, keep
        self.stats = sp.sb("ln_stats", [P, G, 6])
        self.mv = sp.sb("ln_mv", [P, G, 2])
        self.rstd = sp.sb("ln_rstd", [P, G])
        self.stats_ready, self.rstd_ready, self.norm_ready, self.turned, self.nT_ready, self.pool_eps = (
            sp.sem(n) for n in ("ln_stats_ready", "ln_rstd_ready", "ln_norm_ready", "ln_turned", "ln_nT_ready", "ln_eps"))

    def at(self, i, k):
        return i * self.per + (k + 1)

    def dve(self, dve, chain, i, k, x, out):
        for j in range(G):
            chain(dve.bn_stats(self.stats[:, j, :], x(j)))
        chain.wait(self.met)
        for j in range(G):
            last = dve.bn_aggr(self.mv[:, j, :], self.stats[:, j, :])
        last.then_inc(self.stats_ready, 1)
        dve.wait_ge(self.rstd_ready, self.at(i, k))
        for j in range(G):
            last = dve.tensor_scalar(out(j), x(j), self.mv[:, j, 0:1], self.rstd[:, j:j + 1], ALU.subtract, ALU.mult)
        last.then_inc(self.norm_ready, 1)

    def pool(self, pool, i, k):
        hold(pool, self.stats_ready, self.at(i, k), self.met)
        pool.tensor_scalar(self.rstd[:, :], self.mv[:, :, 1], LN_EPS, None, ALU.add).then_inc(self.pool_eps, 1)
        pool.wait_ge(self.pool_eps, self.at(i, k))
        pool.tensor_tensor(self.rstd[:, :], self.rstd[:, :], self.keep.neg_half[:, 0:G], ALU.pow)\
            .then_inc(self.rstd_ready, 1)


def phase_layer0(nc, d, keep):
    with ExitStack() as ctx:
        sp = Space(nc, ctx, "p1")
        W, wg, bq, bk, bv, bo, dist, slopes = keep.l0
        weights_in = keep.l0_in
        bqm = sp.sb("bqm", [P, C, 2])
        alibi = sp.sb("alibi", [P, 8, S])
        nb = sp.sb("n", [P, G, D])
        nT = sp.sb("nT", [P, C, GT])
        bdq = sp.sb("bdq", [P, C, GT // S, 2, S])
        kT = sp.sb("kT", [P, C, GT])
        V = sp.sb("V", [P, G, D])
        SA = [sp.sb(f"SA{n}", [P, 4, 8, S]) for n in range(2)]
        rowmax = [sp.sb(f"rowmax{n}", [P, 32]) for n in range(2)]
        rowsum = [sp.sb(f"rowsum{n}", [P, 32]) for n in range(2)]
        PT = sp.sb("PT", [P, 2, 8, P])
        O0 = sp.sb("O0", [P, 2, 4, S])
        oT = sp.sb("oT", [P, 2, 4, 2, S])
        th = sp.sb("th", [P, C, GT])
        u = sp.sb("u", [P, C, GT])
        hT = sp.sb("hT", [P, C, GT])
        A = sp.ps("A", [P, 4, 512])
        Q = sp.ps("Q", [P, 4, 512])
        Y = A[:, 2:4, :]
        (prep_done, x_biased, y_ready, y_used, q_ready, k_ready, q_evac, k_evac, s_ready, s_used,
         shifted, exp_ready, p_ready, pt_turned, pt_ready, o_ready, o0_ready, oT_ready, hh_ready, th_ready,
         hT_ready, lg_ready, lg_used, dve_self, prep_self, first_kept) = (sp.sem(n) for n in (
             "prep_done", "x_biased", "y_ready", "y_used", "q_ready", "k_ready", "q_evac", "k_evac",
             "s_ready", "s_used", "shifted", "exp_ready", "p_ready", "pt_turned", "pt_ready", "o_ready", "o0_ready",
             "oT_ready", "hh_ready", "th_ready", "hT_ready", "lg_ready", "lg_used", "dve_self", "prep_self", "first_kept"))
        n_in = len(keep.l0_loads)
        met = keep.passed
        ln = LayerNorm(sp, keep, 3, met)

        def xt(i, j):
            return keep.x.rearrange("p t f -> p (t f)")[:, bass.ds(i * (G * D) + j * D, D)]

        def group(t, i):
            return t[:, bass.ds(i * G, G), :]

        def groups(eng, body):
            with eng.Fori(0, NG - 1) as i:
                body(i, False)
            body(NG - 1, True)

        with nc.Block() as block:
            @block.gpsimd
            def _(pool):
                ln.pool(pool, 0, 0)
                pool.wait_ge(weights_in, 16 * n_in)
                pool.wait_ge(keep.c2_in, 32)

                def body(i, last):
                    hold(pool, ln.norm_ready, ln.at(i, 0), met)
                    pool.tensor_tensor(group(keep.x, i), group(keep.x, i), group(keep.c2bc, i), ALU.add)\
                        .then_inc(x_biased, 1)
                    ln.pool(pool, i, 1)
                    hold(pool, ln.norm_ready, ln.at(i, 1), met)
                    pool.tensor_tensor(group(keep.x, i), group(keep.x, i),
                                       bo[:, :].unsqueeze(1).to_broadcast([P, G, D]), ALU.add).then_inc(x_biased, 1)
                    ln.pool(pool, i, 2)
                    hold(pool, ln.norm_ready, ln.at(i, 2), met)
                    pool.tensor_copy(keep.first[:, bass.ds(i, 1), :], nb[0:E, 0:1, :]).then_inc(first_kept, 1)
                    if not last:
                        ln.pool(pool, i, 3)

                groups(pool, body)

            @block.scalar
            def _(act):
                act.wait_ge(prep_done, 1)

                def body(i, last):
                    def turn(k):
                        act.wait_ge(ln.turned, ln.at(i, k))
                        act.activation(nT[:, 0, :], A[:, 0, :], ACT.Copy).then_inc(ln.nT_ready, 1)

                    turn(0)
                    turn(1)
                    act.wait_ge(q_ready, i + 1)
                    for c in range(C):
                        for par in range(2):
                            ins = act.activation(bdq[:, c, :, par, :], Q[:, c, :].rearrange("p (b q) -> p b q", q=S), ACT.Identity,
                                                  bias=bqm[:, c, par:par + 1], scale=keep.mask[:, 2 + par:3 + par])
                    ins.then_inc(q_evac, 1)
                    for h in range(2):
                        act.wait_ge(shifted, 2 * i + h + 1)
                        act.activation(SA[h][:, :, :, :], SA[h][:, :, :, :], ACT.Exp).then_inc(exp_ready, 1)
                    for h in range(2):
                        act.wait_ge(pt_turned, 2 * i + h + 1)
                        act.activation(PT[:, 0, :, :].rearrange("p (c j) q -> p c (j q)", c=2), A[:, 0:2, :], ACT.Copy)\
                            .then_inc(pt_ready, 1)
                        act.wait_ge(o_ready, 2 * i + h + 1)
                        act.wait_ge(oT_ready, 2 * i + h + 1)
                        act.activation(O0[:, :, :, :].rearrange("p a g q -> p (a g) q"), Q[:, 2 * h:2 * h + 2, :].rearrange("p a (g e q) -> p (a g) e q", e=2, q=S)[:, :, 0, :],
                                       ACT.Copy, scale=keep.mask[:, 0:1]).then_inc(o0_ready, 1)
                    turn(2)
                    act.wait_ge(hh_ready, i + 1)
                    act.activation(th[:, :, :], Q[:, 0:2, :], ACT.Tanh, scale=0.5).then_inc(th_ready, 1)

                groups(act, body)

            @block.tensor
            def _(pe):
                def turn_rows(i, k):
                    pe.wait_ge(ln.norm_ready, ln.at(i, k))
                    for c in range(C):
                        for j in range(G):
                            mm = pe.transpose(A[:, c, j * P:(j + 1) * P], nb[:, j, c * P:(c + 1) * P], keep.ident[:, :])
                    mm.then_inc(ln.turned, 1)

                turn_rows(0, 0)
                pe.wait_ge(weights_in, 16 * n_in)

                def body(i, last):
                    def turn(k):
                        turn_rows(i, k)
                        pe.wait_ge(ln.nT_ready, 2 * ln.at(i, k))

                    def rows(src, w, k):
                        pe.wait_ge(y_used, 4 * i + k + 1)
                        for j in range(G):
                            for c in range(C):
                                mm = pe.matmul(Y[:, j // 2, (j % 2) * D:(j % 2 + 1) * D], src(c, j), w[:, c, :],
                                               start=(c == 0), stop=(c == C - 1))
                        mm.then_inc(y_ready, 1)

                    def columns(out, w):
                        for m in range(C):
                            for c in range(C):
                                mm = pe.matmul(out[:, m, :], w[:, c, m * P:(m + 1) * P], nT[:, c, :],
                                               start=(c == 0), stop=(c == C - 1))
                        return mm

                    def tok(c, j):
                        return nT[:, c, j * P:(j + 1) * P]

                    pe.wait_ge(ln.nT_ready, 2 * ln.at(i, 0))
                    rows(tok, W["xa_w1"], 0)
                    turn(1)
                    pe.wait_ge(hT_ready, i + 1)
                    columns(Q[:, 0:2, :], W["wq"]).then_inc(q_ready, 1)
                    columns(Q[:, 2:4, :], W["wk"]).then_inc(k_ready, 1)
                    rows(tok, W["wv"], 1)
                    pe.wait_ge(q_evac, i + 1)
                    pe.wait_ge(k_evac, i + 1)
                    for h in range(2):
                        pe.wait_ge(s_used, 2 * i + h + 1)
                        for c in range(C):
                            for b in range(4):
                                for j in range(4):
                                    r, t0 = slice(32 * j, 32 * j + 32), (4 * h + b) * S
                                    mm = pe.matmul(Q[:, j, (4 * c + b) * S:(4 * c + b + 1) * S],
                                                   bdq[r, c, 4 * h + b, :, :].rearrange("p e q -> p (e q)"), kT[r, c, t0:t0 + S],
                                                   start=True, stop=True, skip_group_check=True)
                        mm.then_inc(s_ready, 1)
                    pe.wait_ge(y_used, 4 * i + 3)
                    pe.wait_ge(s_used, 2 * i + 3)
                    for h in range(2):
                        pe.wait_ge(p_ready, 2 * i + h + 1)
                        for t in range(2):
                            for c in range(C):
                                for j in range(4):
                                    mm = pe.transpose(A[:, 2 * t + c, j * P:(j + 1) * P],
                                                      SA[h][:, j, 4 * c + 2 * t:4 * c + 2 * t + 2, :], keep.ident[:, :])
                        mm.then_inc(pt_turned, 1)
                        hold(pe, pt_ready, 4 * i + 2 * h + 2, met)
                        for t in range(2):
                            for c in range(C):
                                for e in range(2):
                                    for j in range(4):
                                        r = slice(S * e, S * e + S)
                                        mm = pe.matmul(Q[32 * j:32 * j + 32, 2 * h + e, (2 * t + c) * P:(2 * t + c + 1) * P],
                                                       V[r, 2 * h + t, c * P + 32 * j:c * P + 32 * j + 32],
                                                       PT[r, t, 4 * c + j, :], start=True, stop=True, skip_group_check=True)
                        mm.then_inc(o_ready, 1)
                    pe.wait_ge(oT_ready, 2 * i + 3)
                    rows(lambda c, j: oT[:, j // 2, 2 * (j % 2) + c, :, :].rearrange("p e q -> p (e q)"), W["wo"], 2)
                    turn(2)
                    columns(Q[:, 0:2, :], W["sw1"])
                    columns(Q[:, 2:4, :], W["sw3"]).then_inc(hh_ready, 1)
                    for j in range(G):
                        for c in range(C):
                            mm = pe.matmul(A[:, 0, j * E:(j + 1) * E], tok(c, j), wg[:, c, :],
                                           start=(c == 0), stop=(c == C - 1))
                    mm.then_inc(lg_ready, 1)
                    pe.wait_ge(hT_ready, i + 2)
                    rows(lambda c, j: hT[:, c, j * P:(j + 1) * P], W["sw2"], 3)
                    pe.wait_ge(lg_used, i + 1)
                    if not last:
                        turn_rows(i, 3)

                groups(pe, body)

            @block.vector
            def _(dve):
                for free in (y_used, hT_ready, s_used, oT_ready, first_kept):
                    dve.sem_inc(free, 1)

                def start(ch, i, k, x):
                    hold(dve, first_kept, i + 1 + k // 3, met)
                    ln.dve(dve, ch, i, k, x, lambda j: nb[:, j, :])

                begin = Chain(dve, dve_self)
                start(begin, 0, 0, lambda j: xt(0, j))
                dve.wait_ge(weights_in, 16 * n_in)
                prep = Chain(dve, prep_self)
                for c in range(C):
                    for par in range(2):
                        prep(dve.tensor_tensor(bqm[:, c, par:par + 1], bq[:, c:c + 1], keep.mask[:, 2 + par:3 + par], ALU.mult))
                prep(dve.tensor_tensor(alibi[:, :, :], dist[:, :].unsqueeze(1).to_broadcast([P, 8, S]),
                                       slopes[:, :].unsqueeze(2).to_broadcast([P, 8, S]), ALU.mult))
                prep.wait()
                dve.engine_nop().then_inc(prep_done, 1)
                PER = 19

                def body(i, last):
                    ch = Chain(dve, dve_self, i * PER + begin.n)

                    def turned_out(k):
                        dve.wait_ge(ln.turned, ln.at(i, k))
                        dve.tensor_copy(nT[:, 1, :], A[:, 1, :]).then_inc(ln.nT_ready, 1)

                    def norm(k):
                        ln.dve(dve, ch, i, k, lambda j: xt(i, j), lambda j: nb[:, j, :])
                        turned_out(k)

                    def add_rows(k):
                        dve.wait_ge(y_ready, 4 * i + k + 1)
                        ins = dve.tensor_tensor(group(keep.x, i), Y.rearrange("p a (b f) -> p (a b) f", b=2), group(keep.x, i), ALU.add)
                        ins.then_inc(y_used, 1)
                        hold(dve, y_used, 4 * i + k + 2, met)

                    turned_out(0)
                    dve.wait_ge(x_biased, 2 * i + 1)
                    add_rows(0)
                    norm(1)
                    dve.wait_ge(k_ready, i + 1)
                    for c in range(C):
                        ins = dve.tensor_scalar(kT[:, c, :], Q[:, 2 + c, :], bk[:, c:c + 1], None, ALU.add)
                    ins.then_inc(k_evac, 1)
                    dve.wait_ge(y_ready, 4 * i + 2)
                    dve.tensor_tensor(V[:, :, :], Y.rearrange("p a (b f) -> p (a b) f", b=2),
                                      bv[:, :].unsqueeze(1).to_broadcast([P, G, D]), ALU.add).then_inc(y_used, 1)
                    for h in range(2):
                        sa = SA[h][:, :, :, :].rearrange("p j g k -> p (j g) k")
                        dve.wait_ge(s_ready, 2 * i + h + 1)
                        for c in range(C):
                            ins = dve.tensor_tensor(
                                SA[h][:, :, 4 * c:4 * c + 4, :], Q[:, :, 4 * c * S:(4 * c + 4) * S].rearrange("p j (b k) -> p j b k", b=4),
                                alibi[:, 4 * c:4 * c + 4, :].unsqueeze(2).to_broadcast([P, 4, 4, S]), ALU.add)
                        ins.then_inc(s_used, 1)
                        dve.wait_ge(s_used, 2 * i + h + 2)
                        ch(dve.tensor_reduce(rowmax[h][:, :], sa, AX.X, ALU.max))
                        ch.wait()
                        dve.tensor_tensor(sa, sa, rowmax[h][:, :].unsqueeze(2).to_broadcast([P, 32, S]), ALU.subtract)\
                            .then_inc(shifted, 1)
                    for h in range(2):
                        sa = SA[h][:, :, :, :].rearrange("p j g k -> p (j g) k")
                        dve.wait_ge(exp_ready, 2 * i + h + 1)
                        ch(dve.tensor_reduce(rowsum[h][:, :], sa, AX.X, ALU.add))
                        ch.wait()
                        ch(dve.reciprocal(rowsum[h][:, :], rowsum[h][:, :]))
                        ch.wait()
                        dve.tensor_tensor(sa, sa, rowsum[h][:, :].unsqueeze(2).to_broadcast([P, 32, S]), ALU.mult)\
                            .then_inc(p_ready, 1)
                    for h in range(2):
                        dve.wait_ge(pt_turned, 2 * i + h + 1)
                        dve.tensor_copy(PT[:, 1, :, :].rearrange("p (c j) q -> p c (j q)", c=2), A[:, 2:4, :])\
                            .then_inc(pt_ready, 1)
                        dve.wait_ge(o0_ready, 2 * i + h + 1)
                        for e in range(2):
                            ins = dve.scalar_tensor_tensor(
                                out=oT[:, h, :, e, :], in0=Q[:, 2 * h + e, :].rearrange("p (g a q) -> p g a q", a=2, q=S)[:, :, 1, :],
                                scalar=keep.mask[:, 1:2], in1=O0[:, e, :, :], op0=ALU.mult, op1=ALU.add)
                        ins.then_inc(oT_ready, 1)
                    dve.wait_ge(x_biased, 2 * i + 2)
                    add_rows(2)
                    norm(2)
                    if not last:
                        start(ch, i, 3, lambda j: xt(i + 1, j))
                    dve.wait_ge(th_ready, i + 1)
                    ch(dve.scalar_tensor_tensor(out=u[:, :, :], in0=th[:, :, :], scalar=1.0, in1=Q[:, 0:2, :],
                                                op0=ALU.add, op1=ALU.mult))
                    ch.wait()
                    dve.scalar_tensor_tensor(out=hT[:, :, :], in0=u[:, :, :], scalar=0.5, in1=Q[:, 2:4, :],
                                             op0=ALU.mult, op1=ALU.mult).then_inc(hT_ready, 1)
                    dve.wait_ge(lg_ready, i + 1)
                    dve.tensor_copy(group(keep.logits, i), A[:, 0, 0:G * E].rearrange("p (j e) -> p j e", j=G)).then_inc(lg_used, 1)
                    add_rows(3)
                    assert last or ch.n == PER, ch.n

                groups(dve, body)



def phase_experts(nc, d, keep):
    with ExitStack() as ctx:
        sp = Space(nc, ctx, "p2")
        GE = E * E
        w13 = sp.sb("w13", [P, C, E, D])
        w2 = sp.sb("w2", [P, E, D])
        ebias = sp.sb("ebias", [P, E])
        pair = sp.sb("pair", [P, NT, 2])
        below = sp.sb("below", [P, E, E])
        upto = sp.sb("upto", [P, E, E])
        score = sp.sb("score", [P, NT, E])
        bsc = sp.sb("bsc", [P, NT, E])
        m1, s1 = sp.sb("m1", [P, NT]), sp.sb("s1", [P, NT])
        gsc = sp.sb("gsc", [P, NT, 4])
        ggt, geq = sp.sb("ggt", [P, NT, 4, 4]), sp.sb("geq", [P, NT, 4, 4])
        grank, goff = sp.sb("grank", [P, NT, 4]), sp.sb("goff", [P, NT, 4])
        egt, eeq = sp.sb("egt", [P, NT, E, E]), sp.sb("eeq", [P, NT, E, E])
        erank = sp.sb("erank", [P, NT, E])
        sel = [sp.sb(f"sel{s}", [P, NT, E]) for s in range(2)]
        both = sp.sb("both", [P, NT, E])
        wsel = sp.sb("wsel", [P, NT, E])
        weight = [sp.sb(f"weight{s}", [P, NT]) for s in range(2)]
        cnt, tot, cum = sp.sb("cnt", [P, E]), sp.sb("tot", [P, E]), sp.sb("cum", [P, E])
        part = sp.sb("part", [P, E, E])
        past = sp.sb("past", [P, NT * 2, E + 1])
        stretch = sp.sb("stretch", [P, NT * 2, E])
        one = sp.sb("one", [P, NT, 2, E, E])
        onew = sp.sb("onew", [P, NT, 2, E, E])
        firstT = sp.sb("firstT", [P, C, E])
        tab = sp.sb("tab", [E, E, D])
        table = sp.sb("table", [P, D])
        oneT = [sp.sb(f"oneT{n}", [P, 4, P]) for n in range(2)]
        th = sp.sb("th", [P, 8, EH])
        u = sp.sb("u", [P, 8, EH])
        hid = [sp.sb(f"hid{n}", [P, 8, EH]) for n in range(2)]
        sT = sp.sb("sT", [P, GE])
        X = [sp.ps(f"X{n}", [P, 4, P]) for n in range(2)]
        HH = sp.ps("HH", [P, 4, 2, D])
        ST = sp.ps("ST", [P, 512])
        out8 = sp.ps("out8", [P, 512])
        (in_, shifted, exped, cnt_ready, tot_mm, first_mm, first_ready, tab_mm, tab_ready, table_in, onew_ready,
         one_ready, turned, oneT_ready, hh_ready, th_ready, hid_ready, sT_mm, sT_ready, out_mm, dve_self) = (
             sp.sem(n) for n in (
                 "in", "shifted", "exped", "cnt_ready", "tot_mm", "first_mm", "first_ready", "tab_mm", "tab_ready",
                 "table_in", "onew_ready", "one_ready", "turned", "oneT_ready", "hh_ready", "th_ready", "hid_ready",
                 "sT_mm", "sT_ready", "out_mm", "dve_self"))
        wsum_in, wsum_ready, wsum_mm = (sp.sem(n) for n in ("wsum_in", "wsum_ready", "wsum_mm"))
        bw = [sp.sb("bw1", [P, C * F1]), sp.sb("bw2", [P, F1C * D])]
        bwq = [keep.w1q[:, :, :].rearrange("p a b -> p (a b)"), keep.w2q[:, :, :].rearrange("p a b -> p (a b)")]
        wabs, wsc = sp.sb("wabs", [P, 2]), sp.sb("wsc", [P, 2])
        whalf = sp.sb("whalf", [P, 4])
        wsum = out8[:, D:D + 2]
        BIG = 3.0e38

        with nc.Block() as block:
            @block.sync
            def _(sync):
                sync.dma_start(w13[:, :, :, :], d["l0w13"]).then_inc(in_, 16)
                sync.dma_start(w2[:, :, :], d["l0w2"]).then_inc(in_, 16)
                sync.dma_start(ebias[:, :], d["l0eb"].partition_broadcast(P)).then_inc(in_, 16)
                sync.dma_start(pair[:, :, :], d["pair"]).then_inc(in_, 16)
                sync.dma_start(below[:, :, :], d["below"].partition_broadcast(P)).then_inc(in_, 16)
                sync.dma_start(upto[:, :, :], d["upto"].partition_broadcast(P)).then_inc(in_, 16)
                sync.dma_start(bw[0][:, :], d["w1"].rearrange("p a b -> p (a b)")).then_inc(wsum_in, 16)
                sync.dma_start(bw[1][:, :], d["w2"].rearrange("p a b -> p (a b)")).then_inc(wsum_in, 16)
                sync.wait_ge(tab_ready, 1)
                for s in range(2):
                    for g in range(E):
                        sync.dma_start(table[s * GE + g * E:s * GE + (g + 1) * E, :], tab[:, g, :]).then_inc(table_in, 16)

            @block.scalar
            def _(act):
                act.wait_ge(shifted, 1)
                act.activation(score[:, :, :], score[:, :, :], ACT.Exp).then_inc(exped, 1)
                act.wait_ge(tab_mm, 1)
                act.activation(tab[:, :, :], HH[0:E, :, :, :].rearrange("p a b f -> p (a b) f"), ACT.Copy).then_inc(tab_ready, 1)
                for q in range(NT // 4):
                    act.wait_ge(hh_ready, q + 1)
                    if q:
                        act.wait_ge(hid_ready, q)
                    act.activation(th[:, :, :], HH[:, :, :, 0:EH].rearrange("p a b f -> p (a b) f"), ACT.Tanh, scale=0.5)\
                       .then_inc(th_ready, 1)

            @block.tensor
            def _(pe):
                for c in range(C):
                    mm = pe.transpose(X[0][:, c, 0:E], keep.first[:, 0, c * P:(c + 1) * P], keep.ident[0:E, 0:E])
                mm.then_inc(first_mm, 1)
                pe.wait_ge(first_ready, 1)
                pe.wait_ge(in_, 96)
                for g in range(E):
                    for c in range(C):
                        mm = pe.matmul(HH[0:E, g // 2, g % 2, :], firstT[:, c, :], w13[:, c, g, :],
                                       start=(c == 0), stop=(c == C - 1))
                mm.then_inc(tab_mm, 1)
                pe.wait_ge(cnt_ready, 1)
                pe.matmul(X[1][:, 0, 0:E], keep.ones[:, :], cnt[:, :], start=True, stop=True).then_inc(tot_mm, 1)
                pe.wait_ge(onew_ready, 1)

                def turn(q):
                    if q >= 2:
                        pe.wait_ge(oneT_ready, q - 1)
                    for t in range(4):
                        mm = pe.transpose(X[q % 2][:, t, :], onew[:, 4 * q + t, :, :, :].rearrange("p s g e -> p (s g e)"),
                                          keep.ident[:, :])
                    mm.then_inc(turned, 1)

                turn(0)
                pe.wait_ge(table_in, 2 * E * 16)
                pe.wait_ge(tab_ready, 1)
                for q in range(NT // 4):
                    if q + 1 < NT // 4:
                        turn(q + 1)
                    pe.wait_ge(oneT_ready, q + 1)
                    if q:
                        pe.wait_ge(hid_ready, q)
                    for t in range(4):
                        for s in range(2):
                            r = slice(s * GE, (s + 1) * GE)
                            mm = pe.matmul(HH[:, 2 * s + t // 2, t % 2, :], oneT[q % 2][r, t, :], table[r, :], start=True, stop=True,
                                           skip_group_check=True)
                    mm.then_inc(hh_ready, 1)
                    if q == 0:
                        pe.wait_ge(wsum_ready, 1)
                        pe.matmul(wsum, keep.ones[:, :], wabs[:, :], start=True, stop=True).then_inc(wsum_mm, 1)
                    pe.wait_ge(hid_ready, q + 1)
                    for t in range(4):
                        for s in range(2):
                            mm = pe.matmul(ST[:, 0:GE], hid[q % 2][:, 4 * s + t, :],
                                           one[:, 4 * q + t, s, :, :].rearrange("p g e -> p (g e)"),
                                           start=(q == t == s == 0), stop=(q == NT // 4 - 1 and t == 3 and s == 1))
                mm.then_inc(sT_mm, 1)
                pe.wait_ge(sT_ready, 1)
                for g in range(E):
                    mm = pe.matmul(out8[0:E, 0:D], sT[:, g * E:(g + 1) * E], w2[:, g, :], start=(g == 0), stop=(g == E - 1))
                mm.then_inc(out_mm, 1)

            @block.vector
            def _(dve):
                ch = Chain(dve, dve_self)

                def step(ins):
                    ch(ins)
                    ch.wait()

                def spread(t, n):
                    return t.unsqueeze(len(t.shape)).to_broadcast(list(t.shape) + [n])

                dve.wait_ge(in_, 96)
                dve.wait_ge(first_mm, 1)
                dve.tensor_copy(firstT[:, :, :], X[0][:, 0:C, 0:E]).then_inc(first_ready, 1)
                step(dve.tensor_reduce(m1[:, :], keep.logits[:, :, :], AX.X, ALU.max))
                dve.tensor_tensor(score[:, :, :], keep.logits[:, :, :], spread(m1[:, :], E), ALU.subtract).then_inc(shifted, 1)
                dve.wait_ge(exped, 1)
                step(dve.tensor_reduce(s1[:, :], score[:, :, :], AX.X, ALU.add))
                step(dve.reciprocal(s1[:, :], s1[:, :]))
                step(dve.tensor_tensor(score[:, :, :], score[:, :, :], spread(s1[:, :], E), ALU.mult))
                step(dve.tensor_tensor(bsc[:, :, :], score[:, :, :], ebias[:, :].unsqueeze(1).to_broadcast([P, NT, E]), ALU.add))
                pairs = bsc[:, :, :].rearrange("p t (g a) -> p t g a", a=2)
                step(dve.tensor_tensor(gsc[:, :, :], pairs[:, :, :, 0], pairs[:, :, :, 1], ALU.add))

                def ranks(sc, n, gt, eq, rank):
                    other, own = sc.unsqueeze(2).to_broadcast([P, NT, n, n]), spread(sc, n)
                    ch(dve.tensor_tensor(gt, other, own, ALU.is_gt))
                    step(dve.tensor_tensor(eq, other, own, ALU.is_equal))
                    step(dve.tensor_tensor(eq, eq, below[:, 0:n, 0:n].unsqueeze(1).to_broadcast([P, NT, n, n]), ALU.mult))
                    step(dve.tensor_tensor(gt, gt, eq, ALU.add))
                    step(dve.tensor_reduce(rank, gt, AX.X, ALU.add))

                ranks(gsc[:, :, :], 4, ggt[:, :, :, :], geq[:, :, :, :], grank[:, :, :])
                step(dve.tensor_scalar(grank[:, :, :], grank[:, :, :], 2.0, None, ALU.is_lt))
                ch(dve.tensor_scalar(goff[:, :, :], grank[:, :, :], -1.0, BIG, ALU.add, ALU.mult))
                step(dve.tensor_tensor(pairs, pairs, spread(grank[:, :, :], 2), ALU.mult))
                step(dve.tensor_tensor(pairs, pairs, spread(goff[:, :, :], 2), ALU.add))
                ranks(bsc[:, :, :], E, egt[:, :, :, :], eeq[:, :, :, :], erank[:, :, :])
                for s in range(2):
                    ch(dve.tensor_scalar(sel[s][:, :, :], erank[:, :, :], float(s), None, ALU.is_equal))
                ch.wait()
                step(dve.tensor_tensor(both[:, :, :], sel[0][:, :, :], sel[1][:, :, :], ALU.add))
                dve.tensor_reduce(cnt[:, :], both[:, :, :].rearrange("p t e -> p e t"), AX.X, ALU.add).then_inc(cnt_ready, 1)
                for s in range(2):
                    step(dve.tensor_tensor(wsel[:, :, :], score[:, :, :], sel[s][:, :, :], ALU.mult))
                    step(dve.tensor_reduce(weight[s][:, :], wsel[:, :, :], AX.X, ALU.add))
                dve.wait_ge(tot_mm, 1)
                step(dve.tensor_copy(tot[:, :], X[1][:, 0, 0:E]))
                step(dve.tensor_tensor(part[:, :, :], tot[:, :].unsqueeze(1).to_broadcast([P, E, E]), upto[:, :, :], ALU.mult))
                step(dve.tensor_reduce(cum[:, :], part[:, :, :], AX.X, ALU.add))
                ch(dve.memset(past[:, :, 0:1], 1.0))
                step(dve.tensor_tensor(past[:, :, 1:E + 1], spread(pair[:, :, :].rearrange("p t s -> p (t s)"), E),
                                       cum[:, :].unsqueeze(1).to_broadcast([P, 2 * NT, E]), ALU.is_ge))
                step(dve.tensor_tensor(stretch[:, :, :], past[:, :, 0:E], past[:, :, 1:E + 1], ALU.subtract))
                for s in range(2):
                    st = stretch[:, :, :].rearrange("p (t s) g -> p t s g", s=2)[:, :, s, :]
                    ch(dve.tensor_tensor(one[:, :, s, :, :], spread(st, E), sel[s][:, :, :].unsqueeze(2).to_broadcast([P, NT, E, E]), ALU.mult))
                ch.wait()
                for s in range(2):
                    last = dve.tensor_tensor(onew[:, :, s, :, :].rearrange("p t g e -> p t (g e)"),
                                             one[:, :, s, :, :].rearrange("p t g e -> p t (g e)"),
                                             spread(weight[s][:, :], GE), ALU.mult)
                last.then_inc(onew_ready, 1)

                def evac(q):
                    dve.wait_ge(turned, q + 1)
                    dve.tensor_copy(oneT[q % 2][:, :, :], X[q % 2][:, :, :]).then_inc(oneT_ready, 1)

                def magnitudes():
                    dve.wait_ge(wsum_in, 32)
                    for k in range(2):
                        last = dve.tensor_reduce(wabs[:, k:k + 1], bw[k][:, :], AX.X, ALU.add, apply_absolute_value=True)
                    last.then_inc(wsum_ready, 1)

                def scales():
                    dve.wait_ge(wsum_mm, 1)
                    step(dve.tensor_scalar(wsc[:, :], wsum, 1.0 / (F1 * D), 1e-5, ALU.mult, ALU.max))
                    ch(dve.tensor_scalar(keep.wfac[:, :], wsc[:, :], 1.0 / 127.0, None, ALU.mult))
                    ch(dve.tensor_scalar(whalf[:, 0:2], wsc[:, :], 0.5, None, ALU.mult))
                    step(dve.tensor_scalar(whalf[:, 2:4], wsc[:, :], -0.5, None, ALU.mult))

                def rounded(k):
                    step(dve.tensor_scalar(bwq[k], bw[k][:, :], whalf[:, 2 + k:3 + k], None, ALU.is_lt))
                    step(dve.scalar_tensor_tensor(out=bwq[k], in0=bw[k][:, :], scalar=whalf[:, k:k + 1], in1=bwq[k],
                                                  op0=ALU.is_gt, op1=ALU.subtract))

                evac(0)
                for q in range(NT // 4):
                    if q + 1 < NT // 4:
                        evac(q + 1)
                    if q == 0:
                        magnitudes()
                    elif q < 3:
                        rounded(q - 1)
                    dve.wait_ge(th_ready, q + 1)
                    a, b = (HH[:, :, :, k * EH:(k + 1) * EH].rearrange("p a b f -> p (a b) f") for k in range(2))
                    step(dve.scalar_tensor_tensor(out=u[:, :, :], in0=th[:, :, :], scalar=1.0, in1=a, op0=ALU.add, op1=ALU.mult))
                    dve.scalar_tensor_tensor(out=hid[q % 2][:, :, :], in0=u[:, :, :], scalar=0.5, in1=b,
                                             op0=ALU.mult, op1=ALU.mult).then_inc(hid_ready, 1)
                    if q == 0:
                        scales()
                dve.wait_ge(sT_mm, 1)
                dve.tensor_copy(sT[:, :], ST[:, 0:GE]).then_inc(sT_ready, 1)
                dve.wait_ge(out_mm, 1)
                step(dve.tensor_tensor(keep.x[0:E, 0, :], out8[0:E, 0:D], keep.x[0:E, 0, :], ALU.add))


def phase_queries(nc, d, keep):
    with ExitStack() as ctx:
        sp = Space(nc, ctx, "pq")
        wq, bq, bq4, bo = sp.sb("wq", [P, C, D]), sp.sb("bq", [P, C]), sp.sb("bq4", [P, C]), sp.sb("bo", [P, D])
        nb = sp.sb("n", [P, G, D])
        nT = sp.sb("nT", [P, C, GT])
        A, Q = sp.ps("A", [P, C, GT]), sp.ps("Q", [P, C, GT])
        passed = keep.passed
        in_, bias_ready, q_ready, q_evac, x_biased, dve_self = (sp.sem(n) for n in (
            "in", "bias_ready", "q_ready", "q_evac", "x_biased", "dve_self"))
        ln = LayerNorm(sp, keep, 1, passed)

        def xt(i, j):
            return keep.x.rearrange("p t f -> p (t f)")[:, bass.ds(i * (G * D) + j * D, D)]

        with nc.Block() as block:
            @block.sync
            def _(sync):
                sync.dma_start(wq[:, :, :], d["l1w"][:, L1_W.index("wq"), :, :]).then_inc(in_, 16)
                sync.dma_start(bq[:, :], d["l1bq"]).then_inc(in_, 16)
                sync.dma_start(bo[:, :], d["l1bo"].partition_broadcast(P)).then_inc(in_, 16)

            @block.gpsimd
            def _(pool):
                pool.wait_ge(in_, 48)
                with pool.Fori(0, NG) as i:
                    ln.pool(pool, i, 0)
                    hold(pool, ln.norm_ready, ln.at(i, 0), passed)
                    g = keep.x[:, bass.ds(i * G, G), :]
                    pool.tensor_tensor(g, g, bo[:, :].unsqueeze(1).to_broadcast([P, G, D]), ALU.add).then_inc(x_biased, 1)

            @block.scalar
            def _(act):
                act.wait_ge(bias_ready, 1)
                with act.Fori(0, NG) as i:
                    act.wait_ge(ln.turned, ln.at(i, 0))
                    act.activation(nT[:, 0, :], A[:, 0, :], ACT.Copy).then_inc(ln.nT_ready, 1)
                    hold(act, q_ready, i + 1, passed)
                    for c in range(C):
                        last = act.activation(keep.qT[:, c:c + 1, bass.ds(i * GT, GT)], Q[:, c:c + 1, :], ACT.Identity,
                                              bias=bq4[:, c:c + 1], scale=HD ** -0.5)
                    last.then_inc(q_evac, 1)

            @block.tensor
            def _(pe):
                pe.wait_ge(in_, 48)
                with pe.Fori(0, NG) as i:
                    pe.wait_ge(ln.norm_ready, ln.at(i, 0))
                    for c in range(C):
                        for j in range(G):
                            mm = pe.transpose(A[:, c, j * P:(j + 1) * P], nb[:, j, c * P:(c + 1) * P], keep.ident[:, :])
                    mm.then_inc(ln.turned, 1)
                    pe.wait_ge(ln.nT_ready, 2 * ln.at(i, 0))
                    pe.wait_ge(q_evac, i + 1)
                    for m in range(C):
                        for c in range(C):
                            mm = pe.matmul(Q[:, m, :], wq[:, c, m * P:(m + 1) * P], nT[:, c, :], start=(c == 0), stop=(c == C - 1))
                    mm.then_inc(q_ready, 1)

            @block.vector
            def _(dve):
                dve.sem_inc(q_evac, 1)
                dve.wait_ge(in_, 48)
                dve.tensor_scalar(bq4[:, :], bq[:, :], HD ** -0.5, None, ALU.mult).then_inc(bias_ready, 1)
                PER = 4
                with dve.Fori(0, NG) as i:
                    ch = Chain(dve, dve_self, i * PER)
                    ln.dve(dve, ch, i, 0, lambda j: xt(i, j), lambda j: nb[:, j, :])
                    dve.wait_ge(ln.turned, ln.at(i, 0))
                    dve.tensor_copy(nT[:, 1, :], A[:, 1, :]).then_inc(ln.nT_ready, 1)
                    assert ch.n == PER


def phase_context_attention(nc, d, keep):
    with ExitStack() as ctx:
        sp = Space(nc, ctx, "p3")
        U = H // 2
        UC = U // C
        KA = (KEYS + 15) // 16 * 16
        KM = max(n for _, n in KCH)
        STACKED = UC * 4 * 16
        NPR = 3
        W = {n: sp.sb(f"w_{n}", [P, C, D]) for n in ("wk", "wv", "wo")}
        bk, bv = sp.sb("bk", [P, C]), sp.sb("bv", [P, D])
        maskd = sp.sb("maskd", [P, 2 * HD])
        fold = sp.sb("fold", [P, S])
        zeros = sp.sb("zeros", [P, KM])
        rows = sp.sb("rows", [P, KT, D])
        rowsT = sp.sb("rowsT", [P, C, KP])
        parts = [[sp.sb(f"k{r}_{c}", [P, KA], BF16) for r in range(3)] for c in range(C)]
        rest = [sp.sb(f"rest{n}", [P, KM]) for n in range(2)]
        stack = [sp.sb(f"stack{u}", [P, KA], BF16) for u in range(U)]
        V = [sp.sb(f"V{s}", [P, KT, D]) for s in range(2)]
        qpart = [sp.sb(f"q{r}", [P, C, S], BF16) for r in range(3)]
        qrest = sp.sb("qrest", [P, C, S])
        qs = [sp.sb(f"qs{s}", [P, 2, C, UC, 2, S], BF16) for s in range(2)]
        prob = [sp.sb(f"prob{n}", [P, KP]) for n in range(NPR)]
        mx = [sp.sb(f"mx{n}", [P, len(KCH)]) for n in range(NPR)]
        nmx = [sp.sb(f"nmx{n}", [P, 1]) for n in range(NPR)]
        probT = [sp.sb(f"probT{j}", [P, KP]) for j in range(UC)]
        sums = [sp.sb(f"sums{s}", [P, U]) for s in range(2)]
        rsum = sp.sb("rsum", [P, U])
        spreadr = sp.sb("spreadr", [P, U, 2 * HD])
        o0, o1 = sp.sb("o0", [P, C, S]), sp.sb("o1", [P, C, S])
        oT = sp.sb("oT", [P, C, P])
        Sc = [sp.ps(f"Sc{n}", [P, 512]) for n in range(2)]
        M = [sp.ps(f"M{n}", [P, 512]) for n in range(2)]
        T = [sp.ps(f"T{n}", [P, 512]) for n in range(2)]
        O = sp.ps("O", [P, C, P])
        RY = sp.ps("RY", [P, 512])
        R, Y = RY[:, 0:C * S].rearrange("p (c q) -> p c q", c=C), RY[:, C * S:C * S + D]
        landed, turned, k1_ready, split, pool_self = (sp.sem(n) for n in (
            "rows_landed", "rows_turned", "k1_ready", "split", "pool_self"))
        stacked = [sp.sem(f"stacked{c}") for c in range(C)]
        passed = keep.passed
        (in_, cleared, m_filled, m_used, bd_ready, bd_free, s_filled, s_used, max_ready, exp_ready, t_filled, t_used,
         o_ready, o_used, spread_ready, r_ready, oT_ready, y_ready, y_used, dve_self) = (sp.sem(n) for n in (
             "in", "cleared", "m_filled", "m_used", "bd_ready", "bd_free", "s_filled", "s_used", "max_ready",
             "exp_ready", "t_filled", "t_used", "o_ready", "o_used", "spread_ready", "r_ready", "oT_ready", "y_ready",
             "y_used", "dve_self"))
        NI = NT
        NQ = len(KCH)
        NTG = (KT + 3) // 4
        assert NTG == NQ
        VF = (KT + 1) // 2
        def turn(g):
            return [("turn", g, c) for c in range(C)]

        keys = [[("key", n, m) for n in range(NQ)] for m in range(C)]
        values = [("value", v, 0) for v in range(VF)]
        SCHEDULE = [turn(0), [turn(1)[0], keys[0][0]], [turn(1)[1], values[0]], [turn(2)[0], keys[0][1], turn(2)[1]],
                    [turn(3)[0], keys[0][2], turn(3)[1]], [values[1], keys[0][3]], [values[2], keys[1][0]],
                    [keys[1][1], values[3]], [keys[1][2], keys[1][3], values[4]], values[5:]]
        assert len(SCHEDULE) == U + 2 and NTG == 4 and VF == 7
        FILLS = sum(SCHEDULE, [])
        NFILL = len(FILLS)
        assert NFILL == NTG * C + NQ * C + VF and NFILL % 2 == 1
        SLOTS = [len(x) for x in SCHEDULE]
        LAST_TURN = FILLS.index(turn(NTG - 1)[-1])

        def slot(k):
            return range(sum(SLOTS[:k]), sum(SLOTS[:k + 1]))


        def load(sync, batch):
            src = d["ctx"][bass.ds(batch * KEYS, KF * P), :]
            sync.dma_start(rows[:, 0:KF, :], src.rearrange("(p t) f -> p t f", p=P)).then_inc(landed, 16)
            sync.dma_start(rows[0:KR, KF, :], d["ctx"][bass.ds(batch * KEYS + KF * P, KR), :]).then_inc(landed, 16)

        def stack_keys(sync, batch, c):
            hold(sync, split, NQ * (C * batch + c + 1) + 2, passed)
            for j in range(UC):
                for k, r in enumerate((0, 1, 2, 0)):
                    sync.dma_start(stack[UC * c + j][32 * k:32 * k + 32, 0:KEYS], parts[c][r][32 * j:32 * j + 32, 0:KEYS]).then_inc(stacked[c], 16)

        def turned_rows(pe, batch, f, g):
            needed = FILLS.index(turn(g)[-1])
            assert needed < f
            if needed > f - 2:
                pe.wait_ge(m_used, batch * NFILL + needed + 3)

        def fill(pe, f, s, batch):
            kind, a, b = FILLS[f]
            bank = M[(s + f) % 2]
            F = batch * NFILL + f
            if kind == "turn":
                if f == 0:
                    pe.wait_ge(landed, 32 * (batch + 1))
                pe.wait_ge(m_used, F + 1)
                for t in range(4 * a, min(4 * a + 4, KT)):
                    mm = pe.transpose(bank[:, (t - 4 * a) * P:(t - 4 * a + 1) * P], rows[:, t, b * P:(b + 1) * P], keep.ident[:, :])
                mm.then_inc(m_filled, 1)
                if f == LAST_TURN:
                    pe.wait_ge(m_filled, F + 1)
                    pe.sem_inc(turned, 1)
                return
            if kind == "key":
                pe.wait_ge(m_used, F + 1)
                k0, kn = KCH[a]
                turned_rows(pe, batch, f, (k0 + kn - 1) // 512)
                for c in range(C):
                    mm = pe.matmul(bank[:, 0:kn], W["wk"][:, c, b * P:(b + 1) * P], rowsT[:, c, k0:k0 + kn],
                                   start=(c == 0), stop=(c == C - 1))
            else:
                pe.wait_ge(m_used, F + 1)
                turned_rows(pe, batch, f, min(2 * a + 1, KT - 1) // 4)
                for t in range(2 * a, min(2 * a + 2, KT)):
                    for c in range(C):
                        mm = pe.matmul(bank[:, (t - 2 * a) * D:(t - 2 * a + 1) * D], rowsT[:, c, t * P:(t + 1) * P], W["wv"][:, c, :],
                                       start=(c == 0), stop=(c == C - 1))
            mm.then_inc(m_filled, 1)

        def drain(dve, f, s, batch):
            kind, a, b = FILLS[f]
            bank = M[(s + f) % 2]
            dve.wait_ge(m_filled, batch * NFILL + f + 1)
            if kind == "turn":
                n = (min(4 * a + 4, KT) - 4 * a) * P
                ins = dve.tensor_copy(rowsT[:, b, 4 * a * P:4 * a * P + n], bank[:, 0:n])
            elif kind == "key":
                k0, kn = KCH[a]
                x = NQ * (C * batch + b) + a
                hold(dve, split, x + 1, passed)
                hold(dve, k1_ready, x + 1, passed)
                ins = dve.scalar_tensor_tensor(out=rest[a % 2][:, 0:kn], in0=bank[:, 0:kn], scalar=bk[:, b:b + 1],
                                               in1=parts[b][0][:, k0:k0 + kn], op0=ALU.add, op1=ALU.subtract)
            else:
                n = min(2 * a + 2, KT) - 2 * a
                ins = dve.tensor_tensor(V[s][:, 2 * a:2 * a + n, :], bank[:, 0:n * D].rearrange("p (t f) -> p t f", t=n),
                                        bv[:, :].unsqueeze(1).to_broadcast([P, n, D]), ALU.add)
            ins.then_inc(m_used, 1)

        def first_part(act, f, s, batch, earlier=True):
            kind, a, b = FILLS[f]
            if kind != "key":
                return
            k0, kn = KCH[a]
            if a == 0 and earlier:
                act.wait_ge(stacked[b], STACKED * batch)
            act.wait_ge(m_filled, batch * NFILL + f + 1)
            act.activation(parts[b][0][:, k0:k0 + kn], M[(s + f) % 2][:, 0:kn], ACT.Identity, bias=bk[:, b:b + 1]).then_inc(k1_ready, 1)

        def other_parts(pool, ch, f, batch):
            kind, a, b = FILLS[f]
            if kind != "key":
                return
            k0, kn = KCH[a]
            hold(pool, m_used, batch * NFILL + f + 3, passed)
            ch(pool.tensor_copy(parts[b][1][:, k0:k0 + kn], rest[a % 2][:, 0:kn]))
            hold(pool, pool_self, ch.base + ch.n, passed)
            pool.tensor_tensor(parts[b][2][:, k0:k0 + kn], rest[a % 2][:, 0:kn], parts[b][1][:, k0:k0 + kn], ALU.subtract)\
                .then_inc(split, 1)

        def pairs_of_batches(eng, body):
            with eng.Fori(0, NI - 1) as i:
                body(i, False)
            body(NI - 1, True)

        with nc.Block() as block:
            @block.sync
            def _(sync):
                for n in W:
                    sync.dma_start(W[n][:, :, :], d["l1w"][:, L1_W.index(n), :, :]).then_inc(in_, 16)
                sync.dma_start(bk[:, :], d["l1bk"]).then_inc(in_, 16)
                sync.dma_start(bv[:, :], d["l1bv"].partition_broadcast(P)).then_inc(in_, 16)
                sync.dma_start(maskd[:, :], d["maskd"]).then_inc(in_, 16)
                sync.dma_start(fold[:, :], d["fold"]).then_inc(in_, 16)
                sync.wait_ge(cleared, 1)
                load(sync, 0)
                sync.wait_ge(turned, 1)
                load(sync, 1)
                for c in range(C):
                    stack_keys(sync, 0, c)

                def body(i, last):
                    for s in range(2):
                        if not last:
                            hold(sync, turned, 2 * i + s + 2, passed)
                            load(sync, 2 * i + s + 2)
                        if not (last and s == 1):
                            for c in range(C):
                                hold(sync, s_filled, NQ * (16 * i + 8 * s + UC * (c + 1)), passed)
                                stack_keys(sync, 2 * i + s + 1, c)

                pairs_of_batches(sync, body)

            @block.gpsimd
            def _(pool):
                pool.memset(rows[:, KF, :], 0.0)
                pool.memset(zeros[:, :], 0.0)
                for s in range(2):
                    pool.memset(qs[s][:, 1, :, :, :, :].rearrange("p c j a q -> p (c j a q)"), 0.0)
                for n in range(NPR):
                    last = pool.memset(prob[n][:, KEYS:KP], 0.0)
                last.then_inc(cleared, 1)
                pool.sem_inc(bd_free, 2)
                pool.wait_ge(cleared, 1)
                pool.wait_ge(in_, 112)

                def queries(ch, i, s):
                    hold(pool, bd_free, 2 * i + s + 1, passed)

                    def step(ins):
                        ch(ins)
                        hold(pool, pool_self, ch.base + ch.n, passed)

                    q = keep.qT[:, :, bass.ds(i * P + s * S, S)]
                    step(pool.tensor_copy(qpart[0][:, :, :], q))
                    step(pool.tensor_tensor(qrest[:, :, :], q, qpart[0][:, :, :], ALU.subtract))
                    step(pool.tensor_copy(qpart[1][:, :, :], qrest[:, :, :]))
                    step(pool.tensor_tensor(qpart[2][:, :, :], qrest[:, :, :], qpart[1][:, :, :], ALU.subtract))
                    for j in range(UC):
                        r = slice(32 * j, 32 * j + 32)
                        for k, slots in enumerate(((0, 0, 0, 1), (2, 1))):
                            for to, part in enumerate(slots):
                                ins = pool.tensor_tensor(qs[s][32 * to:32 * to + 32, k, :, j, :, :],
                                                         qpart[part][r, :, :].unsqueeze(2).to_broadcast([32, C, 2, S]),
                                                         keep.mask[r, 0:2].unsqueeze(1).unsqueeze(3).to_broadcast([32, C, 2, S]), ALU.mult)
                    step(ins)
                    pool.sem_inc(bd_ready, 1)

                def parts_of(ch, batch):
                    for f in range(NFILL):
                        other_parts(pool, ch, f, batch)

                start = Chain(pool, pool_self)
                queries(start, 0, 0)
                parts_of(start, 0)
                PER = 2 * (5 + C * NQ)

                def body(i, last):
                    ch = Chain(pool, pool_self, i * PER + start.n)
                    queries(ch, i, 1)
                    parts_of(ch, 2 * i + 1)
                    if not last:
                        queries(ch, i + 1, 0)
                        parts_of(ch, 2 * i + 2)
                        assert ch.n == PER, ch.n

                pairs_of_batches(pool, body)

            @block.tensor
            def _(pe):
                pe.wait_ge(in_, 112)
                pe.wait_ge(cleared, 1)
                for f in range(NFILL):
                    fill(pe, f, 0, 0)

                def score(i, s, u, n):
                    g = 16 * i + 8 * s + u
                    c, j = u // UC, u % UC
                    k0, kn = KCH[n]
                    if u == 0 and n == 0:
                        pe.wait_ge(bd_ready, 2 * i + s + 1)
                        pe.wait_ge(m_used, (2 * i + s + 1) * NFILL + 2)
                    if j == 0 and n == 0:
                        pe.wait_ge(stacked[c], STACKED * (2 * i + s + 1))
                    pe.wait_ge(s_used, NQ * g + n + 1)
                    for k in range(2):
                        mm = pe.matmul(Sc[n % 2][:, 0:kn], qs[s][:, k, c, j, :, :].rearrange("p a q -> p (a q)"),
                                       stack[u][:, k0:k0 + kn], start=(k == 0), stop=(k == 1))
                    mm.then_inc(s_filled, 1)
                    if u == U - 1 and n == NQ - 1:
                        pe.wait_ge(s_filled, NQ * (g + 1))
                        pe.sem_inc(bd_free, 1)

                def turn_probs(i, s, u, n):
                    g = 16 * i + 8 * s + u
                    if n == 0:
                        pe.wait_ge(exp_ready, g + 1)
                    pe.wait_ge(t_used, NQ * g + n + 1)
                    for t in range(4 * n, min(4 * n + 4, KT)):
                        mm = pe.transpose(T[n % 2][:, (t - 4 * n) * P:(t - 4 * n + 1) * P], prob[u % NPR][:, t * P:(t + 1) * P], keep.ident[:, :])
                    mm.then_inc(t_filled, 1)

                def weigh(i, s, c):
                    g = 16 * i + 8 * s + UC * (c + 1)
                    if c == 0:
                        pe.wait_ge(o_used, 2 * i + s + 1)
                    hold(pe, t_used, NQ * g + 2, passed)
                    for t in range(KT):
                        for j in range(UC):
                            mm = pe.matmul(O[32 * j:32 * j + 32, c, :], V[s][:, t, c * P + 32 * j:c * P + 32 * j + 32],
                                           probT[j][:, t * P:(t + 1) * P], start=(t == 0), stop=(t == KT - 1))
                    mm.then_inc(o_ready, 1)

                def body(i, last):
                    for s in range(2):
                        def prepare(k, m):
                            for f in list(slot(k))[m]:
                                if not (last and s == 1):
                                    fill(pe, f, 1 - s, 2 * i + s + 1)

                        for u in range(U):
                            score(i, s, u, 0)
                            score(i, s, u, 1)
                            prepare(u, slice(0, 1))
                            if u == UC + 1:
                                weigh(i, s, 0)
                            for n in range(2, NQ):
                                if u:
                                    turn_probs(i, s, u - 1, n - 2)
                                score(i, s, u, n)
                            prepare(u, slice(1, 2))
                            if u:
                                for n in range(NQ - 2, NQ):
                                    turn_probs(i, s, u - 1, n)
                            prepare(u, slice(2, None))
                        prepare(U, slice(0, 1))
                        for n in range(NQ - 2):
                            turn_probs(i, s, U - 1, n)
                        prepare(U, slice(1, None))
                        for n in range(NQ - 2, NQ):
                            turn_probs(i, s, U - 1, n)
                        prepare(U + 1, slice(0, 1))
                        pe.wait_ge(spread_ready, 2 * i + s + 1)
                        for c in range(C):
                            mm = pe.matmul(R[:, c, :], spreadr[:, UC * c:UC * c + UC, :].rearrange("p a e -> p (a e)"), fold[:, :],
                                           start=True, stop=True)
                        mm.then_inc(r_ready, 1)
                        weigh(i, s, 1)
                        prepare(U + 1, slice(1, None))
                    pe.wait_ge(oT_ready, 2 * i + 2)
                    pe.wait_ge(y_used, i + 1)
                    for c in range(C):
                        mm = pe.matmul(Y, oT[:, c, :], W["wo"][:, c, :], start=(c == 0), stop=(c == C - 1))
                    mm.then_inc(y_ready, 1)

                pairs_of_batches(pe, body)

            @block.scalar
            def _(act):
                act.sem_inc(t_used, 2)
                act.wait_ge(cleared, 1)
                act.wait_ge(in_, 112)
                for f in range(NFILL):
                    first_part(act, f, 0, 0, earlier=False)

                def exps(i, s, u):
                    g = 16 * i + 8 * s + u
                    act.wait_ge(max_ready, g + 1)
                    act.activation(prob[u % NPR][:, 0:KEYS], prob[u % NPR][:, 0:KEYS], ACT.Exp, bias=nmx[u % NPR][:, 0:1],
                                   accum_out=sums[s][:, u:u + 1]).then_inc(exp_ready, 1)

                def turned_out(i, s, u, which=range(NQ)):
                    g = 16 * i + 8 * s + u
                    for n in which:
                        w = (min(4 * n + 4, KT) - 4 * n) * P
                        act.wait_ge(t_filled, NQ * g + n + 1)
                        act.activation(probT[u % UC][:, 4 * n * P:4 * n * P + w], T[n % 2][:, 0:w], ACT.Copy).then_inc(t_used, 1)

                def body(i, last):
                    for s in range(2):
                        def prepared(k, m):
                            for f in list(slot(k))[m]:
                                if not (last and s == 1):
                                    first_part(act, f, 1 - s, 2 * i + s + 1)

                        for u in range(U):
                            prepared(u, slice(0, 1))
                            if u:
                                turned_out(i, s, u - 1, range(NQ - 2))
                            prepared(u, slice(1, 2))
                            exps(i, s, u)
                            if u:
                                turned_out(i, s, u - 1, range(NQ - 2, NQ))
                            prepared(u, slice(2, None))
                        prepared(U, slice(0, 1))
                        turned_out(i, s, U - 1, range(NQ - 2))
                        prepared(U, slice(1, None))
                        turned_out(i, s, U - 1, range(NQ - 2, NQ))
                        prepared(U + 1, slice(None))

                pairs_of_batches(act, body)

            @block.vector
            def _(dve):
                dve.sem_inc(m_used, 2)
                dve.sem_inc(split, 2)
                dve.sem_inc(s_used, 2)
                dve.sem_inc(o_used, 1)
                dve.sem_inc(y_used, 1)
                dve.wait_ge(in_, 112)
                dve.wait_ge(cleared, 1)
                for f in range(NFILL):
                    drain(dve, f, 0, 0)
                PER = 4

                def body(i, last):
                    ch = Chain(dve, dve_self, i * PER)
                    for s in range(2):
                        def prepared(k, m=slice(None)):
                            for f in list(slot(k))[m]:
                                if not (last and s == 1):
                                    drain(dve, f, 1 - s, 2 * i + s + 1)

                        for u in range(U):
                            g = 16 * i + 8 * s + u
                            for n, (k0, kn) in enumerate(KCH):
                                hold(dve, s_filled, NQ * g + n + 1, passed)
                                ins = dve.tensor_tensor_reduce(prob[u % NPR][:, k0:k0 + kn], Sc[n % 2][:, 0:kn], zeros[:, 0:kn], 1.0, -3.0e38,
                                                               ALU.add, ALU.max, mx[u % NPR][:, n:n + 1])
                                ins.then_inc(s_used, 1)
                            dve.wait_ge(s_used, NQ * (g + 1) + 2)
                            dve.tensor_reduce(nmx[u % NPR][:, :], mx[u % NPR][:, :], AX.X, ALU.max, negate=True).then_inc(max_ready, 1)
                            prepared(u)
                        prepared(U)
                        dve.wait_ge(exp_ready, 16 * i + 8 * (s + 1))
                        ch(dve.reciprocal(rsum[:, :], sums[s][:, :]))
                        ch.wait()
                        dve.tensor_tensor(spreadr[:, :, :], rsum[:, :].unsqueeze(2).to_broadcast([P, U, 2 * HD]),
                                          maskd[:, :].unsqueeze(1).to_broadcast([P, U, 2 * HD]), ALU.mult).then_inc(spread_ready, 1)
                        prepared(U + 1, slice(0, 1))
                        dve.wait_ge(o_ready, 2 * (2 * i + s) + 2)
                        ch(dve.tensor_scalar(o0[:, :, :], O[:, :, 0:S], keep.mask[:, 0:1], None, ALU.mult))
                        ch.wait()
                        ins = dve.scalar_tensor_tensor(out=o1[:, :, :], in0=O[:, :, S:P], scalar=keep.mask[:, 1:2], in1=o0[:, :, :],
                                                       op0=ALU.mult, op1=ALU.add)
                        ins.then_inc(o_used, 1)
                        dve.wait_ge(o_used, 2 * i + s + 2)
                        dve.wait_ge(r_ready, 2 * i + s + 1)
                        dve.tensor_tensor(oT[:, :, s * S:(s + 1) * S], R, o1[:, :, :], ALU.mult).then_inc(oT_ready, 1)
                        prepared(U + 1, slice(1, None))
                    hold(dve, y_ready, i + 1, passed)
                    xi = keep.x.rearrange("p t f -> p (t f)")
                    xi = xi[:, i * D:(i + 1) * D] if last else xi[:, bass.ds(i * D, D)]
                    dve.tensor_tensor(xi, Y, xi, ALU.add).then_inc(y_used, 1)
                    assert ch.n == PER, ch.n

                pairs_of_batches(dve, body)


def phase_layer1(nc, d, keep):
    with ExitStack() as ctx:
        sp = Space(nc, ctx, "p4")
        NB = GT // S
        K = 4
        pw = sp.sb("pw", [P, C, D])
        hgw = sp.sb("hgw", [P, 4, 2, P])
        gow = sp.sb("gow", [P, 4, S])
        fgw, fvw = sp.sb("fgw", [P, C, FC * P]), sp.sb("fvw", [P, C, FC * P])
        fow = sp.sb("fow", [P, FC, D])
        pwb = sp.sb("pwb", [P, D])
        dw, dwb = sp.sb("dw", [P, C, K]), sp.sb("dwb", [P, C])
        gam = sp.sb("gam", [P, 3, C])
        w1q, w2q, wfac = keep.w1q, keep.w2q, keep.wfac
        first = sp.sb("first", [P, G, D])
        y = sp.sb("y", [P, G, D])
        rb = sp.sb("rb", [P, G, D])
        ss, rs = sp.sb("ss", [P, G]), sp.sb("rs", [P, G])
        floor = sp.sb("floor", [P, G])
        uT = sp.sb("uT", [P, C, NB, S + K - 1])
        cv = sp.sb("cv", [P, C, GT])
        nT = sp.sb("nT", [P, C, GT])
        tg, thid = ([sp.sb(f"{n}{k}", [P, 2, GT]) for k in range(2)] for n in ("tg", "thid"))
        z, q, a, v = ([sp.sb(f"{n}{k}", [P, 2, GT]) for k in range(2)] for n in ("z", "q", "a", "v"))
        h = sp.sb("h", [P, 4, GT])
        tf, fu = ([sp.sb(f"{n}{k}", [P, GT]) for k in range(2)] for n in ("tf", "fu"))
        ff = sp.sb("ff", [P, FC, GT])
        am, s1, gs = (sp.sb(n, [P, G]) for n in ("am", "s1", "gs"))
        xq = sp.sb("xq", [P, G, D], BF16)
        xqT = sp.sb("xqT", [P, C, GT], BF16)
        hb = [sp.sb(f"hb{k}", [P, F1]) for k in range(2)]
        hr = sp.sb("hr", [P, F1])
        am2, s2, es = (sp.sb(n, [P, G]) for n in ("am2", "s2", "es"))
        hq = [sp.sb(f"hq{k}", [P, F1], BF16) for k in range(2)]
        hqT = [sp.sb(f"hqT{k}", [P, F1C, P], BF16) for k in range(2)]
        identb = sp.sb("identb", [P, P], BF16)
        A, Q = sp.ps("A", [P, 4, 512]), sp.ps("Q", [P, 4, 512])
        Y = A[:, 2:4, :]
        passed = keep.passed
        (small_in, in_, cleared, prep, sq_ready, floor_ready, rs_ready, rb_ready, turned, nT_ready, cv_ready, y_biased,
         x_joined, y_ready, y_used, hg_ready, tanh_ready, z_ready, h_ready, ff_filled, tf_ready, ff_ready, xq_ready, xq_turned,
         xqT_ready, up_ready, gelu_ready, hq_ready, hq_turned, hqT_ready, dve_self, pool_self) = (sp.sem(n) for n in (
             "small_in", "in", "cleared", "prep", "sq_ready", "floor_ready", "rs_ready", "rb_ready", "turned",
             "nT_ready", "cv_ready", "y_biased", "x_joined", "y_ready", "y_used", "hg_ready", "tanh_ready", "z_ready", "h_ready",
             "ff_filled", "tf_ready", "ff_ready", "xq_ready", "xq_turned", "xqT_ready", "up_ready", "gelu_ready", "hq_ready",
             "hq_turned", "hqT_ready", "dve_self", "pool_self"))
        ln = LayerNorm(sp, keep, 2, passed)
        loads = [(pw, d["l1w"][:, L1_W.index("pw"), :, :]), (hgw, d["hgw"]), (gow, d["gow"]), (fgw, d["fgw"]), (fvw, d["fvw"]),
                 (fow, d["fow"]), (pwb, d["pwb"].partition_broadcast(P))]
        n_in = 16 * len(loads)
        YU = 7

        def full(t):
            return t[tuple(slice(None) for _ in t.shape)]

        def xt(i, j):
            return keep.x.rearrange("p t f -> p (t f)")[:, bass.ds(i * (G * D) + j * D, D)]

        def xg(i):
            return keep.x[:, bass.ds(i * G, G), :]

        def groups(eng, body):
            with eng.Fori(0, NG - 1) as i:
                body(i, False)
            body(NG - 1, True)

        START = 1

        def own(last):
            return 1 if last else 2

        with nc.Block() as block:
            @block.sync
            def _(sync):
                for t, src in ((dw, d["dw"]), (dwb, d["dwb"]), (gam, d["gam"])):
                    sync.dma_start(full(t), src).then_inc(small_in, 16)
                for t, src in loads:
                    sync.dma_start(full(t), src).then_inc(in_, 16)

            @block.gpsimd
            def _(pool):
                pool.memset(uT[:, :, :, 0:K - 1], 0.0)
                pool.tensor_copy(identb[:, :], keep.ident[:, :]).then_inc(cleared, 1)
                def rms(ch, i, k):
                    hold(pool, sq_ready, 3 * i + k + 1, passed)
                    ch(pool.tensor_scalar(floor[:, :], ss[:, :], 1e-24, None, ALU.max))
                    hold(pool, pool_self, ch.base + ch.n, passed)
                    pool.tensor_tensor(rs[:, :], floor[:, :], keep.neg_half[:, 0:G], ALU.pow).then_inc(rs_ready, 1)

                def start(ch, i):
                    rms(ch, i, 0)
                    hold(pool, rb_ready, 3 * i + 1, passed)
                    pool.tensor_tensor(first[:, :, :], first[:, :, :], pwb[:, :].unsqueeze(1).to_broadcast([P, G, D]), ALU.add)\
                        .then_inc(y_biased, 1)

                ln.pool(pool, 0, 0)
                begin = Chain(pool, pool_self)
                pool.wait_ge(in_, n_in)
                start(begin, 0)

                def body(i, last):
                    ch = Chain(pool, pool_self, i * 3 + begin.n)
                    rms(ch, i, 1)
                    for r in range(2):
                        hold(pool, tanh_ready, 2 * i + r + 1, passed)
                        pool.tensor_scalar(z[r][:, :, :], tg[r][:, :, :], 0.5, 0.5, ALU.mult, ALU.add).then_inc(z_ready, 1)
                    rms(ch, i, 2)
                    hold(pool, rb_ready, 3 * i + 3, passed)
                    pool.tensor_tensor(y[:, :, :], y[:, :, :], xg(i), ALU.add).then_inc(x_joined, 1)
                    if not last:
                        ln.pool(pool, i, START)
                        start(ch, i + 1)
                        assert ch.n == 3
                    ln.pool(pool, i, own(last))

                groups(pool, body)

            @block.scalar
            def _(act):
                act.wait_ge(prep, 1)

                def start(i):
                    act.wait_ge(turned, 3 * i + 1)
                    act.activation(uT[:, 0, :, K - 1:], A[:, 0, :].rearrange("p (b l) -> p b l", l=S), ACT.Copy).then_inc(nT_ready, 1)

                start(0)

                def body(i, last):
                    act.wait_ge(turned, 3 * i + 2)
                    act.activation(nT[:, 0, :], A[:, 0, :], ACT.Copy, scale=gam[:, 1, 0:1]).then_inc(nT_ready, 1)
                    for r in range(2):
                        src = (Q, A)[r]
                        act.wait_ge(hg_ready, 2 * i + r + 1)
                        act.activation(tg[r][:, :, :], src[:, 2:4, :], ACT.Tanh, scale=0.5)
                        act.activation(thid[r][:, :, :], src[:, 0:2, :], ACT.Tanh, scale=0.5).then_inc(tanh_ready, 1)
                    act.wait_ge(turned, 3 * i + 3)
                    act.activation(nT[:, 0, :], A[:, 0, :], ACT.Copy, scale=gam[:, 2, 0:1]).then_inc(nT_ready, 1)
                    for f in range(FC):
                        act.wait_ge(ff_filled, FC * i + f + 1)
                        act.activation(tf[f % 2][:, :], Q[:, 2 * (f % 2), :], ACT.Tanh, scale=0.5).then_inc(tf_ready, 1)
                    if not last:
                        start(i + 1)

                    def turned_hidden(j):
                        act.wait_ge(hq_turned, G * i + j + 1)
                        act.activation(hqT[j % 2][:, :, :].rearrange("p c t -> p (c t)"), A[:, 1, :].bitcast(BF16), ACT.Copy).then_inc(hqT_ready, 1)

                    for j in range(G):
                        act.wait_ge(up_ready, G * i + j + 1)
                        act.activation(hb[j % 2][:, :], Q[:, 2 * (j % 2):2 * (j % 2) + 2, :], ACT.Gelu, scale=gs[:, j:j + 1])\
                           .then_inc(gelu_ready, 1)
                        if j:
                            turned_hidden(j - 1)
                    turned_hidden(G - 1)

                groups(act, body)

            @block.tensor
            def _(pe):

                def turn(i, k):
                    pe.wait_ge(rb_ready, 3 * i + k + 1)
                    for c in range(C):
                        for j in range(G):
                            mm = pe.transpose(A[:, c, j * P:(j + 1) * P], rb[:, j, c * P:(c + 1) * P], keep.ident[:, :])
                    mm.then_inc(turned, 1)

                turn(0, 0)
                pe.wait_ge(in_, n_in)

                def body(i, last):
                    pe.wait_ge(y_used, YU * i + 1)
                    pe.wait_ge(cv_ready, i + 1)
                    for j in range(G):
                        for c in range(C):
                            mm = pe.matmul(Y[:, j // 2, (j % 2) * D:(j % 2 + 1) * D], cv[:, c, j * P:(j + 1) * P], pw[:, c, :],
                                           start=(c == 0), stop=(c == C - 1))
                    mm.then_inc(y_ready, 1)
                    turn(i, 1)
                    pe.wait_ge(nT_ready, 6 * i + 4)
                    for r in range(2):
                        dst = (Q, A)[r]
                        for kind in range(2):
                            for hh in range(2):
                                head = 2 * r + hh
                                mm = pe.matmul(dst[:, 2 * kind + hh, :], hgw[:, head, kind, :], nT[:, head // 2, :], start=True, stop=True)
                        mm.then_inc(hg_ready, 1)
                    pe.wait_ge(h_ready, 2 * i + 2)
                    for j in range(G):
                        for head in range(4):
                            mm = pe.matmul(Y[:, j // 2, (j % 2) * D + head * S:(j % 2) * D + (head + 1) * S],
                                           h[:, head, j * P:(j + 1) * P], gow[:, head, :], start=True, stop=True)
                    mm.then_inc(y_ready, 1)
                    turn(i, 2)
                    pe.wait_ge(nT_ready, 6 * i + 6)
                    for f in range(FC):
                        if f >= 2:
                            pe.wait_ge(ff_ready, FC * i + f - 1)
                        for k, w in enumerate((fgw, fvw)):
                            for c in range(C):
                                mm = pe.matmul(Q[:, 2 * (f % 2) + k, :], w[:, c, f * P:(f + 1) * P], nT[:, c, :],
                                               start=(c == 0), stop=(c == C - 1))
                        mm.then_inc(ff_filled, 1)
                    if not last:
                        turn(i + 1, 0)
                    pe.wait_ge(ff_ready, FC * i + FC)
                    for j in range(G):
                        for f in range(FC):
                            mm = pe.matmul(Y[:, j // 2, (j % 2) * D:(j % 2 + 1) * D], ff[:, f, j * P:(j + 1) * P], fow[:, f, :],
                                           start=(f == 0), stop=(f == FC - 1))
                    mm.then_inc(y_ready, 1)
                    pe.wait_ge(xq_ready, i + 1)
                    if not last:
                        pe.wait_ge(nT_ready, 6 * i + 8)
                    for c in range(C):
                        for j in range(G):
                            mm = pe.transpose(A[:, 0, :].bitcast(BF16)[:, (c * G + j) * P:(c * G + j + 1) * P],
                                              xq[:, j, c * P:(c + 1) * P], identb[:, :])
                    mm.then_inc(xq_turned, 1)
                    pe.wait_ge(xqT_ready, i + 1)

                    def up(j):
                        if j >= 2:
                            pe.wait_ge(gelu_ready, G * i + j - 1)
                        for o in range(2):
                            for c in range(C):
                                mm = pe.matmul(Q[:, 2 * (j % 2) + o, :], xqT[:, c, j * P:(j + 1) * P], w1q[:, c, o * 512:(o + 1) * 512],
                                               start=(c == 0), stop=(c == C - 1))
                        mm.then_inc(up_ready, 1)

                    up(0)
                    up(1)
                    for j in range(G):
                        pe.wait_ge(hq_ready, G * i + j + 1)
                        for c in range(F1C):
                            mm = pe.transpose(A[:, 1, :].bitcast(BF16)[:, c * P:(c + 1) * P], hq[j % 2][:, c * P:(c + 1) * P], identb[:, :])
                        mm.then_inc(hq_turned, 1)
                        if j + 2 < G:
                            up(j + 2)
                        pe.wait_ge(hqT_ready, G * i + j + 1)
                        if j >= 2:
                            pe.wait_ge(y_used, YU * i + 3 + j)
                        for c in range(F1C):
                            mm = pe.matmul(Y[:, j % 2, 0:D], hqT[j % 2][:, c, :], w2q[:, c, :],
                                           start=(c == 0), stop=(c == F1C - 1))
                        mm.then_inc(y_ready, 1)

                groups(pe, body)

            @block.vector
            def _(dve):
                dve.sem_inc(y_used, 1)
                dve.wait_ge(small_in, 48)
                dve.wait_ge(cleared, 1)
                pc = Chain(dve, dve_self)

                def step(ins):
                    pc(ins)
                    pc.wait()

                step(dve.tensor_scalar(gam[:, :, :], gam[:, :, :], 1.0, None, ALU.add))
                pc(dve.tensor_tensor(dw[:, :, :], dw[:, :, :], gam[:, 0, :].unsqueeze(2).to_broadcast([P, C, K]), ALU.mult))
                dve.engine_nop().then_inc(prep, 1)

                def rms(i, k, rows):
                    for j in range(G):
                        last = dve.tensor_tensor_reduce(rb[:, j, :], rows[:, j, :], rows[:, j, :], 1.0, 0.0, ALU.mult, ALU.add, ss[:, j:j + 1])
                    last.then_inc(sq_ready, 1)
                    dve.wait_ge(rs_ready, 3 * i + k + 1)
                    for j in range(G):
                        last = dve.tensor_scalar(rb[:, j, :], rows[:, j, :], rs[:, j:j + 1], float(D) ** 0.5, ALU.mult, ALU.mult)
                    last.then_inc(rb_ready, 1)

                def convolve(ch, i):
                    dve.wait_ge(turned, 3 * i + 1)
                    dve.tensor_copy(uT[:, 1, :, K - 1:], A[:, 1, :].rearrange("p (b l) -> p b l", l=S)).then_inc(nT_ready, 1)
                    dve.wait_ge(nT_ready, 6 * i + 2)
                    cvv = cv[:, :, :].rearrange("p c (b l) -> p c b l", l=S)
                    for c in range(C):
                        ch(dve.tensor_scalar(cvv[:, c, :, :], uT[:, c, :, 0:S], dw[:, c, 0:1], dwb[:, c:c + 1], ALU.mult, ALU.add))
                    for k in range(1, K):
                        ch.wait()
                        for c in range(C):
                            ins = dve.scalar_tensor_tensor(out=cvv[:, c, :, :], in0=uT[:, c, :, k:k + S], scalar=dw[:, c, k:k + 1],
                                                           in1=cvv[:, c, :, :], op0=ALU.mult, op1=ALU.add)
                            if k < K - 1:
                                ch(ins)
                    ins.then_inc(cv_ready, 1)

                ln.dve(dve, pc, 0, 0, lambda j: xt(0, j), lambda j: first[:, j, :])
                dve.wait_ge(ln.norm_ready, 1)
                rms(0, 0, first)
                convolve(pc, 0)
                BASE = pc.n
                PER = 66

                def body(i, last):
                    ch = Chain(dve, dve_self, i * PER + BASE)

                    def go(ins):
                        ch(ins)
                        ch.wait()

                    def rows_in():
                        return Y.rearrange("p a (b f) -> p (a b) f", b=2)

                    dve.wait_ge(y_biased, i + 1)
                    dve.wait_ge(y_ready, YU * i + 1)
                    go(dve.tensor_tensor(y[:, :, :], rows_in(), first[:, :, :], ALU.add))
                    dve.sem_inc(y_used, 1)
                    rms(i, 1, y)
                    dve.wait_ge(turned, 3 * i + 2)
                    dve.tensor_scalar(nT[:, 1, :], A[:, 1, :], gam[:, 1, 1:2], None, ALU.mult).then_inc(nT_ready, 1)
                    for r in range(2):
                        src = (Q, A)[r]
                        dve.wait_ge(tanh_ready, 2 * i + r + 1)
                        go(dve.tensor_scalar(a[r][:, :, :], tg[r][:, :, :], -0.5, 0.5, ALU.mult, ALU.add))
                        ch(dve.memset(a[r][:, :, :].rearrange("p a (b l) -> p (a b) l", l=S)[:, :, 0:1], 0.0))
                        ch(dve.tensor_scalar(q[r][:, :, :], thid[r][:, :, :], 0.0, 0.5, ALU.min, ALU.mult))
                        dve.wait_ge(z_ready, 2 * i + r + 1)
                        ch.wait()
                        go(dve.scalar_tensor_tensor(out=v[r][:, :, :], in0=src[:, 0:2, :], scalar=0.0, in1=q[r][:, :, :], op0=ALU.max, op1=ALU.add))
                        go(dve.scalar_tensor_tensor(out=v[r][:, :, :], in0=v[r][:, :, :], scalar=0.5, in1=z[r][:, :, :], op0=ALU.add, op1=ALU.mult))
                        dve.tensor_tensor_scan(h[:, 2 * r:2 * r + 2, :].rearrange("p a t -> p (a t)"), a[r][:, :, :].rearrange("p a t -> p (a t)"),
                                               v[r][:, :, :].rearrange("p a t -> p (a t)"), 0.0, ALU.mult, ALU.add).then_inc(h_ready, 1)
                    dve.wait_ge(y_ready, YU * i + 2)
                    go(dve.tensor_tensor(y[:, :, :], rows_in(), y[:, :, :], ALU.add))
                    dve.sem_inc(y_used, 1)
                    rms(i, 2, y)
                    dve.wait_ge(turned, 3 * i + 3)
                    dve.tensor_scalar(nT[:, 1, :], A[:, 1, :], gam[:, 2, 1:2], None, ALU.mult).then_inc(nT_ready, 1)
                    for f in range(FC):
                        dve.wait_ge(tf_ready, FC * i + f + 1)
                        go(dve.scalar_tensor_tensor(out=fu[f % 2][:, :], in0=tf[f % 2][:, :], scalar=1.0, in1=Q[:, 2 * (f % 2), :],
                                                    op0=ALU.add, op1=ALU.mult))
                        dve.scalar_tensor_tensor(out=ff[:, f, :], in0=fu[f % 2][:, :], scalar=0.5, in1=Q[:, 2 * (f % 2) + 1, :],
                                                 op0=ALU.mult, op1=ALU.mult).then_inc(ff_ready, 1)
                        if f == 1 and not last:
                            ln.dve(dve, ch, i, START, lambda j: xt(i + 1, j), lambda j: first[:, j, :])
                        if f == 3 and not last:
                            hold(dve, ln.norm_ready, ln.at(i, START), passed)
                            rms(i + 1, 0, first)
                    if not last:
                        convolve(ch, i + 1)
                    dve.wait_ge(x_joined, i + 1)
                    dve.wait_ge(y_ready, YU * i + 3)
                    ch(dve.tensor_tensor(xg(i), rows_in(), y[:, :, :], ALU.add))
                    hold(dve, dve_self, i * PER + BASE + ch.n, passed)
                    dve.sem_inc(y_used, 1)
                    ln.dve(dve, ch, i, own(last), lambda j: xt(i, j), lambda j: y[:, j, :])
                    dve.wait_ge(ln.norm_ready, ln.at(i, own(last)))
                    go(dve.tensor_reduce(am[:, :], y[:, :, :], AX.X, ALU.max, apply_absolute_value=True))
                    go(dve.tensor_scalar(am[:, :], am[:, :], 1e-5, None, ALU.max))
                    ch(dve.tensor_scalar(gs[:, :], am[:, :], wfac[:, 0:1], None, ALU.mult))
                    go(dve.reciprocal(s1[:, :], am[:, :]))
                    go(dve.tensor_scalar(s1[:, :], s1[:, :], 127.0, None, ALU.mult))
                    for j in range(G):
                        ch(dve.tensor_scalar(rb[:, j, :], y[:, j, :], s1[:, j:j + 1], MAGIC, ALU.mult, ALU.add))
                    ch.wait()
                    dve.tensor_scalar(xq[:, :, :], rb[:, :, :], MAGIC, 127.0, ALU.subtract, ALU.min).then_inc(xq_ready, 1)
                    dve.wait_ge(xq_turned, i + 1)
                    dve.tensor_copy(xqT[:, :, :].rearrange("p c t -> p (c t)"), A[:, 0, :].bitcast(BF16)).then_inc(xqT_ready, 1)

                    def down(j):
                        hold(dve, y_ready, YU * i + 4 + j, passed)
                        dve.scalar_tensor_tensor(out=xt(i, j), in0=Y[:, j % 2, 0:D], scalar=es[:, j:j + 1], in1=xt(i, j),
                                                 op0=ALU.mult, op1=ALU.add).then_inc(y_used, 1)

                    for j in range(G):
                        dve.wait_ge(gelu_ready, G * i + j + 1)
                        m = am2[:, j:j + 1]
                        go(dve.tensor_reduce(m, hb[j % 2][:, :], AX.X, ALU.max, apply_absolute_value=True))
                        go(dve.tensor_scalar(m, m, 1e-5, None, ALU.max))
                        ch(dve.tensor_scalar(es[:, j:j + 1], m, wfac[:, 1:2], None, ALU.mult))
                        go(dve.reciprocal(s2[:, j:j + 1], m))
                        go(dve.tensor_scalar(s2[:, j:j + 1], s2[:, j:j + 1], 127.0, None, ALU.mult))
                        go(dve.tensor_scalar(hr[:, :], hb[j % 2][:, :], s2[:, j:j + 1], MAGIC, ALU.mult, ALU.add))
                        dve.tensor_scalar(hq[j % 2][:, :], hr[:, :], MAGIC, 127.0, ALU.subtract, ALU.min).then_inc(hq_ready, 1)
                        if j:
                            down(j - 1)
                    down(G - 1)
                    hold(dve, y_used, YU * i + 1 + YU, passed)
                    assert last or ch.n == PER, ch.n

                groups(dve, body)


class Keep:

    def __init__(self, nc, ctx):
        def sb(name, shape):
            return ctx.enter_context(nc.sbuf_tensor(f"keep_{name}", shape, F32))

        self.x = sb("x", [P, NT, D])
        self.ident = sb("ident", [P, P])
        self.mask = sb("mask", [P, 4])
        self.ones = sb("ones", [P, P])
        self.neg_half = sb("neg_half", [P, NT])
        self.w1q = ctx.enter_context(nc.sbuf_tensor("keep_w1q", [P, C, F1], BF16))
        self.w2q = ctx.enter_context(nc.sbuf_tensor("keep_w2q", [P, F1C, D], BF16))
        self.wfac = sb("wfac", [P, 2])
        self.passed = ctx.enter_context(nc.semaphore("passed"))


def layer0_inputs(nc, d, keep, ctx):
    def sb(name, shape):
        return ctx.enter_context(nc.sbuf_tensor(f"l0_{name}", shape, F32))

    W = {n: sb(f"w_{n}", [P, C, D]) for n in L0_W if n != "xa_w2"}
    wg, bq, bk = sb("wg", [P, C, E]), sb("bq", [P, C]), sb("bk", [P, C])
    bv, bo = sb("bv", [P, D]), sb("bo", [P, D])
    dist, slopes = sb("dist", [P, S]), sb("slopes", [P, 8])
    head_pairs = d["slopes"].rearrange("(j a) -> a j", a=2)
    keep.l0 = W, wg, bq, bk, bv, bo, dist, slopes
    keep.l0_in = ctx.enter_context(nc.semaphore("l0_in"))
    keep.c2_in = ctx.enter_context(nc.semaphore("c2_in"))
    keep.l0_loads = [(W[n][:, :, :], d["l0w"][:, L0_W.index(n), :, :]) for n in W] + [
        (wg[:, :, :], d["l0wg"]), (bq[:, :], d["l0bq"]), (bk[:, :], d["l0bk"]),
        (bv[:, :], d["l0bv"].partition_broadcast(P)), (bo[:, :], d["l0bo"].partition_broadcast(P)),
        (dist[:, :], d["dist"]),
        (slopes[0:S, :], head_pairs[0].partition_broadcast(S)), (slopes[S:P, :], head_pairs[1].partition_broadcast(S))]


def program(nc, d, out):
    with ExitStack() as ctx:
        keep = Keep(nc, ctx)
        with ExitStack() as routed:
            keep.first = routed.enter_context(nc.sbuf_tensor("keep_first", [E, NG, D], F32))
            keep.logits = routed.enter_context(nc.sbuf_tensor("keep_logits", [P, NT, E], F32))
            with ExitStack() as early:
                keep.c2bc = early.enter_context(nc.sbuf_tensor("keep_c2bc", [P, NT, D], F32))
                layer0_inputs(nc, d, keep, early)
                phase_context_sums(nc, d, keep)
                phase_layer0(nc, d, keep)
            phase_experts(nc, d, keep)
        with ExitStack() as late:
            keep.qT = late.enter_context(nc.sbuf_tensor("keep_qT", [P, C, B * S], F32))
            phase_queries(nc, d, keep)
            phase_context_attention(nc, d, keep)
        phase_layer1(nc, d, keep)
        phase_store(nc, keep, out)


def phase_store(nc, keep, out):
    with nc.semaphore("out_stored") as stored, nc.Block() as block:
        @block.sync
        def _(sync):
            sync.dma_start(out.rearrange("(t p) f -> p t f", p=P), keep.x[:, :, :]).then_inc(stored, 16)
            sync.wait_ge(stored, 16)


def kernel(**inputs):
    import numpy as np
    import concourse.bacc as bacc
    from concourse.bass_utils import run_bass_kernel_spmd

    a = {k: np.ascontiguousarray(v) for k, v in inputs.items()}
    f = np.float32

    def lhs(w):
        return np.ascontiguousarray(w.reshape(-1, P, w.shape[1]).transpose(1, 0, 2))

    def col(v):
        return np.ascontiguousarray(v.reshape(-1, P).T)

    xw = a["L0_xattn_W"]
    l0 = {"xa_w1": xw[:, :D].T, "xa_w2": xw[:, D:].T, "wq": a["L0_attn_Wq"].T, "wk": a["L0_attn_Wk"].T,
          "wv": a["L0_attn_Wv"].T, "wo": a["L0_attn_Wo"].T, "sw1": a["L0_ffn_sw1"].T, "sw3": a["L0_ffn_sw3"].T,
          "sw2": a["L0_ffn_sw2"].T}
    l1 = {"wq": a["L1_xattn_Wq"].T, "wk": a["L1_xattn_Wk"].T, "wv": a["L1_xattn_Wv"].T, "wo": a["L1_xattn_Wo"].T,
          "pw": a["L1_attn_pw_w"].T}
    r = np.arange(P)
    own = np.stack([(r // HD) % 2 == 0, (r // HD) % 2 == 1], 1).astype(f)
    ins = {
        "x": a["x"].reshape(B * S, D),
        "ctx": a["ctx_1024"].reshape(B * KEYS, D),
        "ident": np.eye(P, dtype=f),
        "mask": np.concatenate([own, own * f(0.25)], 1),
        "l0w": np.ascontiguousarray(np.stack([lhs(l0[n]) for n in L0_W], 1)),
        "xa_b": a["L0_xattn_b"],
        "l0wg": lhs(a["L0_ffn_w_gate"].T),
        "l0bq": col(a["L0_attn_bq"]), "l0bk": col(a["L0_attn_bk"]), "l0bv": a["L0_attn_bv"], "l0bo": a["L0_attn_bo"],
        "dist": (np.arange(S)[None, :] - (r % S)[:, None]).astype(f),
        "slopes": a["L0_attn_slopes"],
        "l1w": np.ascontiguousarray(np.stack([lhs(l1[n]) for n in L1_W], 1)),
    }
    e = np.arange(E)
    ins.update({
        "l0w13": np.ascontiguousarray(np.concatenate([a["L0_ffn_w1"], a["L0_ffn_w3"]], 2).reshape(E, C, P, D).transpose(2, 1, 0, 3)),
        "l0w2": np.ascontiguousarray(a["L0_ffn_w2"].transpose(1, 0, 2)),
        "l0eb": a["L0_ffn_expert_bias"],
        "pair": (2 * (np.arange(NT)[None, :, None] * P + r[:, None, None]) + np.arange(2)[None, None, :]).astype(f),
        "below": (e[None, :] < e[:, None]).astype(f),
        "upto": (e[None, :] <= e[:, None]).astype(f),
    })
    ins.update({
        "l1bq": col(a["L1_xattn_bq"]), "l1bk": col(a["L1_xattn_bk"]), "l1bv": a["L1_xattn_bv"], "l1bo": a["L1_xattn_bo"],
        "maskd": (r[:, None] // S == np.arange(2 * HD)[None, :] // HD).astype(f),
        "fold": (r[:, None] % S == np.arange(S)[None, :]).astype(f),
    })
    def padded(w, rows, cols):
        out = np.zeros((rows, cols), f)
        out[:w.shape[0], :w.shape[1]] = w
        return out

    hgw = np.zeros((P, 4, 2, P), f)
    gow = np.zeros((P, 4, S), f)
    for h in range(4):
        lo = (h % 2) * S
        hgw[lo:lo + S, h, 0, :DI] = a["L1_attn_w_hg"][h][:, :DI]
        hgw[lo:lo + S, h, 1, :DI] = a["L1_attn_w_hg"][h][:, DI:]
        gow[:DI, h, :] = a["L1_attn_w_out"][h]
    ins.update({
        "hgw": hgw, "gow": gow,
        "fgw": lhs(padded(a["L1_attn_w_gate"], D, FC * P)), "fvw": lhs(padded(a["L1_attn_w_value"], D, FC * P)),
        "fow": lhs(padded(a["L1_attn_w_ff_out"], FC * P, D)), "pwb": a["L1_attn_pw_b"],
        "dw": lhs(a["L1_attn_dw_w"][:, 0, :]), "dwb": col(a["L1_attn_dw_b"]),
        "gam": np.ascontiguousarray(np.stack([col(a[f"L1_attn_{n}_gamma"]) for n in ("conv", "gru", "ff")], 1)),
        "w1": lhs(a["L1_ffn_w1"].T), "w2": lhs(a["L1_ffn_w2"].T),
    })
    nc = bacc.Bacc("TRN2", target_bir_lowering=False, num_devices=1)
    d = {k: nc.dram_tensor(f"in_{k}_dram", v.shape, mybir.dt.from_np(v.dtype), kind="ExternalInput").ap()
         for k, v in ins.items()}
    d["c2_scratch"] = nc.dram_tensor("c2_scratch", [B, D], F32).ap()
    out = nc.dram_tensor("out_0_dram", (B * S, D), F32, kind="ExternalOutput").ap()
    program(nc, d, out)
    res = run_bass_kernel_spmd(nc, [{f"in_{k}_dram": v for k, v in ins.items()}], core_ids=[0])
    return res.results[0]["out_0_dram"].reshape(B, S, D)
```
